# Optimizing a Trainium2 kernel written in Bass

```python
import numpy as np
import jax
import jax.numpy as jnp

def _softmax(x, axis=-1):
    return jax.nn.softmax(x, axis=axis)

def _gelu(x):
    return jax.nn.gelu(x, approximate=True)

def _silu(x):
    return jax.nn.silu(x)

def _sigmoid(x):
    return jax.nn.sigmoid(x)

def _layernorm(x, axis=-1, eps=1e-05):
    m = jnp.mean(x, axis=axis, keepdims=True)
    v = jnp.var(x, axis=axis, keepdims=True)
    return (x - m) / jnp.sqrt(v + eps)

def _scatter_add(tgt, idx, src, axis=0):
    return tgt.at[idx].add(src)

def _segment_sum(src, seg, n):
    return jax.ops.segment_sum(src, seg, n)
kernel_name = 'mk_lm_tower_d2_tok_ids768_r4_9cca65'

def setup_inputs(seed: int=0):
    np.random.seed(seed)
    _w = jnp.asarray

    def _rec_inputs():
        import jax
        import jax.numpy as jnp
        _rk = jax.random.key(seed)
        x = jax.random.randint(jax.random.fold_in(_rk, 1), (4, 1024), 0, 50226, jnp.int32)
        return x
    x = _rec_inputs()

    def _L0_tok_setup():
        import jax, jax.numpy as jnp
        import numpy as np
        VOCAB = 50257
        EMBED = 192
        B, C = (4, 512)
        key = jax.random.key(seed)
        k1, k2 = jax.random.split(key)
        x = jax.random.randint(k1, (B, C), 0, VOCAB)
        embed_matrix = jax.random.normal(k2, (VOCAB, EMBED), dtype=jnp.float32)
        return {'x': x, 'embed_matrix': embed_matrix}
    _L0_tok_all = _L0_tok_setup()
    _L0_tok_in = {k: v for k, v in _L0_tok_all.items() if k in ('embed_matrix',)}
    del _L0_tok_all

    def _L0_attn_setup():
        import jax, jax.numpy as jnp
        import numpy as np
        D_MODEL, D_STATE, D_CONV = (192, 8, 3)
        D_INNER = D_MODEL
        BATCH, SEQ = (4, 2048)

        def _forward(x, W_in, conv_w, conv_b, B, C, D, W_out):
            xz = x @ W_in
            xc, z = jnp.split(xz, 2, axis=-1)
            xc = jnp.transpose(xc, (0, 2, 1))
            xc = jax.lax.conv_general_dilated(xc, conv_w, window_strides=(1,), padding=[(D_CONV - 1, 0)], dimension_numbers=('NCH', 'OIH', 'NCH'), feature_group_count=D_INNER)
            xc = xc + conv_b[None, :, None]
            xc = jnp.transpose(xc, (0, 2, 1))
            xc = jax.nn.silu(xc)
            z = jax.nn.silu(z)
            BC = jnp.sum(B * C, axis=-1)
            y = jnp.cumsum(xc, axis=1) * BC + xc * D
            out = y * z @ W_out
            return out
        key = jax.random.key(seed)
        ks = jax.random.split(key, 7)
        x = jax.random.normal(ks[0], (BATCH, SEQ, D_MODEL), dtype=jnp.float32)
        W_in = jax.random.normal(ks[1], (D_MODEL, 2 * D_INNER), dtype=jnp.float32) * 0.02
        conv_w = jax.random.normal(ks[2], (D_INNER, 1, D_CONV), dtype=jnp.float32) * 0.1
        conv_b = jnp.zeros((D_INNER,), dtype=jnp.float32)
        B = jax.random.normal(ks[3], (D_INNER, D_STATE), dtype=jnp.float32)
        C = jax.random.normal(ks[4], (D_INNER, D_STATE), dtype=jnp.float32)
        D = jnp.ones((D_INNER,), dtype=jnp.float32)
        W_out = jax.random.normal(ks[5], (D_INNER, D_MODEL), dtype=jnp.float32) * 0.02
        return {'x': x, 'W_in': W_in, 'conv_w': conv_w, 'conv_b': conv_b, 'B': B, 'C': C, 'D': D, 'W_out': W_out}
    _L0_attn_all = _L0_attn_setup()
    _L0_attn_in = {k: v for k, v in _L0_attn_all.items() if k in ('W_in', 'conv_w', 'conv_b', 'B', 'C', 'D', 'W_out')}
    del _L0_attn_all

    def _L0_ffn_setup():
        import jax, jax.numpy as jnp
        import numpy as np
        B, L, D, H, F = (4, 512, 192, 12, 768)
        ROUTE_FRAC = 0.15
        LN_EPS = 1e-05

        def _ln(x, g, b):
            m = jnp.mean(x, axis=-1, keepdims=True)
            v = jnp.mean((x - m) ** 2, axis=-1, keepdims=True)
            return (x - m) * jax.lax.rsqrt(v + LN_EPS) * g + b
        key = jax.random.key(seed)
        ks = jax.random.split(key, 20)
        s = 0.02
        return {'hidden_states': jax.random.normal(ks[0], (B, L, D), dtype=jnp.float32), 'g1': jnp.ones((D,), jnp.float32), 'b1': jnp.zeros((D,), jnp.float32), 'g2': jnp.ones((D,), jnp.float32), 'b2': jnp.zeros((D,), jnp.float32), 'Wr': jax.random.normal(ks[1], (D,), jnp.float32) * s, 'br': jnp.zeros((), jnp.float32), 'Wq': jax.random.normal(ks[2], (D, D), jnp.float32) * s, 'bq': jnp.zeros((D,), jnp.float32), 'Wk': jax.random.normal(ks[3], (D, D), jnp.float32) * s, 'bk': jnp.zeros((D,), jnp.float32), 'Wv': jax.random.normal(ks[4], (D, D), jnp.float32) * s, 'bv': jnp.zeros((D,), jnp.float32), 'Wo': jax.random.normal(ks[5], (D, D), jnp.float32) * s, 'bo': jnp.zeros((D,), jnp.float32), 'Wm': jax.random.normal(ks[6], (D, D), jnp.float32) * s, 'bm': jnp.zeros((D,), jnp.float32), 'W1': jax.random.normal(ks[7], (D, F), jnp.float32) * s, 'bf1': jnp.zeros((F,), jnp.float32), 'W2': jax.random.normal(ks[8], (F, D), jnp.float32) * s, 'bf2': jnp.zeros((D,), jnp.float32)}
    _L0_ffn_all = _L0_ffn_setup()
    _L0_ffn_in = {k: v for k, v in _L0_ffn_all.items() if k in ('g1', 'b1', 'g2', 'b2', 'Wr', 'br', 'Wq', 'bq', 'Wk', 'bk', 'Wv', 'bv', 'Wo', 'bo', 'Wm', 'bm', 'W1', 'bf1', 'W2', 'bf2')}
    del _L0_ffn_all

    def _L1_attn_setup():
        import jax, jax.numpy as jnp
        import numpy as np
        N_STATE = 192
        N_HEAD = 12
        D_HEAD = N_STATE // N_HEAD
        M_SLOTS = 100

        def _split_heads(t):
            B, T, _ = t.shape
            return t.reshape(B, T, N_HEAD, D_HEAD).transpose(0, 2, 1, 3)

        def _merge_heads(t):
            B, H, T, D = t.shape
            return t.transpose(0, 2, 1, 3).reshape(B, T, H * D)

        def _attn(q, k, v):
            w = jax.nn.softmax(jnp.einsum('bhqd,bhkd->bhqk', q, k), axis=-1)
            return jnp.einsum('bhqk,bhkd->bhqd', w, v)
        key = jax.random.key(seed)
        ks = jax.random.split(key, 10)
        B, S = (2, 512)
        sc = 0.02
        return {'x': jax.random.normal(ks[0], (B, S, N_STATE), dtype=jnp.float32), 'w_attn': jax.random.normal(ks[1], (N_STATE, 3 * N_STATE), dtype=jnp.float32) * sc, 'b_attn': jnp.zeros((3 * N_STATE,), dtype=jnp.float32), 'w_proj': jax.random.normal(ks[2], (N_STATE, N_STATE), dtype=jnp.float32) * sc, 'b_proj': jnp.zeros((N_STATE,), dtype=jnp.float32), 'w_mem': jax.random.normal(ks[3], (N_STATE, 2 * N_STATE), dtype=jnp.float32) * sc, 'b_mem': jnp.zeros((2 * N_STATE,), dtype=jnp.float32), 'w_alpha': jax.random.normal(ks[4], (2 * N_STATE, N_STATE), dtype=jnp.float32) * sc, 'b_alpha': jnp.zeros((N_STATE,), dtype=jnp.float32), 'memory_features': jax.random.normal(ks[5], (1, M_SLOTS, N_STATE), dtype=jnp.float32) * sc}
    _L1_attn_all = _L1_attn_setup()
    _L1_attn_in = {k: v for k, v in _L1_attn_all.items() if k in ('w_attn', 'b_attn', 'w_proj', 'b_proj', 'w_mem', 'b_mem', 'w_alpha', 'b_alpha', 'memory_features')}
    del _L1_attn_all

    def _L1_ffn_setup():
        import jax, jax.numpy as jnp
        import numpy as np
        EMBED_DIM = 192
        FF_MULT = 4
        HIDDEN = EMBED_DIM * FF_MULT
        BATCH, SEQ = (32, 256)
        EPS = 1e-06

        def rmsnorm(x, g):
            return x * jax.lax.rsqrt(jnp.mean(x * x, axis=-1, keepdims=True) + EPS) * g

        def act_quant(x):
            scale = 127.0 / jnp.clip(jnp.max(jnp.abs(x), axis=-1, keepdims=True), 1e-05, None)
            return jnp.clip(jnp.round(x * scale), -128.0, 127.0) / scale

        def weight_quant(w):
            scale = 1.0 / jnp.clip(jnp.mean(jnp.abs(w)), 1e-05, None)
            return jnp.clip(jnp.round(w * scale), -1.0, 1.0) / scale

        def bitlinear(x, w, g):
            xn = rmsnorm(x, g)
            xq = xn + jax.lax.stop_gradient(act_quant(xn) - xn)
            wq = w + jax.lax.stop_gradient(weight_quant(w) - w)
            return jnp.einsum('bsd,fd->bsf', xq, wq)
        key = jax.random.key(seed)
        k1, k2, k3 = jax.random.split(key, 3)
        x = jax.random.normal(k1, (BATCH, SEQ, EMBED_DIM), dtype=jnp.float32)
        w1 = jax.random.normal(k2, (HIDDEN, EMBED_DIM), dtype=jnp.float32) * 0.02
        w2 = jax.random.normal(k3, (EMBED_DIM, HIDDEN), dtype=jnp.float32) * 0.02
        g1 = jnp.ones((EMBED_DIM,), dtype=jnp.float32)
        g2 = jnp.ones((HIDDEN,), dtype=jnp.float32)
        return {'x': x, 'w1': w1, 'g1': g1, 'w2': w2, 'g2': g2}
    _L1_ffn_all = _L1_ffn_setup()
    _L1_ffn_in = {k: v for k, v in _L1_ffn_all.items() if k in ('w1', 'g1', 'w2', 'g2')}
    del _L1_ffn_all
    return {'x': x, 'L0_tok_embed_matrix': _L0_tok_in['embed_matrix'], 'L0_attn_W_in': _L0_attn_in['W_in'], 'L0_attn_conv_w': _L0_attn_in['conv_w'], 'L0_attn_conv_b': _L0_attn_in['conv_b'], 'L0_attn_B': _L0_attn_in['B'], 'L0_attn_C': _L0_attn_in['C'], 'L0_attn_D': _L0_attn_in['D'], 'L0_attn_W_out': _L0_attn_in['W_out'], 'L0_ffn_g1': _L0_ffn_in['g1'], 'L0_ffn_b1': _L0_ffn_in['b1'], 'L0_ffn_g2': _L0_ffn_in['g2'], 'L0_ffn_b2': _L0_ffn_in['b2'], 'L0_ffn_Wr': _L0_ffn_in['Wr'], 'L0_ffn_br': _L0_ffn_in['br'], 'L0_ffn_Wq': _L0_ffn_in['Wq'], 'L0_ffn_bq': _L0_ffn_in['bq'], 'L0_ffn_Wk': _L0_ffn_in['Wk'], 'L0_ffn_bk': _L0_ffn_in['bk'], 'L0_ffn_Wv': _L0_ffn_in['Wv'], 'L0_ffn_bv': _L0_ffn_in['bv'], 'L0_ffn_Wo': _L0_ffn_in['Wo'], 'L0_ffn_bo': _L0_ffn_in['bo'], 'L0_ffn_Wm': _L0_ffn_in['Wm'], 'L0_ffn_bm': _L0_ffn_in['bm'], 'L0_ffn_W1': _L0_ffn_in['W1'], 'L0_ffn_bf1': _L0_ffn_in['bf1'], 'L0_ffn_W2': _L0_ffn_in['W2'], 'L0_ffn_bf2': _L0_ffn_in['bf2'], 'L1_attn_w_attn': _L1_attn_in['w_attn'], 'L1_attn_b_attn': _L1_attn_in['b_attn'], 'L1_attn_w_proj': _L1_attn_in['w_proj'], 'L1_attn_b_proj': _L1_attn_in['b_proj'], 'L1_attn_w_mem': _L1_attn_in['w_mem'], 'L1_attn_b_mem': _L1_attn_in['b_mem'], 'L1_attn_w_alpha': _L1_attn_in['w_alpha'], 'L1_attn_b_alpha': _L1_attn_in['b_alpha'], 'L1_attn_memory_features': _L1_attn_in['memory_features'], 'L1_ffn_w1': _L1_ffn_in['w1'], 'L1_ffn_g1': _L1_ffn_in['g1'], 'L1_ffn_w2': _L1_ffn_in['w2'], 'L1_ffn_g2': _L1_ffn_in['g2']}

def reference(x, L0_tok_embed_matrix, L0_attn_W_in, L0_attn_conv_w, L0_attn_conv_b, L0_attn_B, L0_attn_C, L0_attn_D, L0_attn_W_out, L0_ffn_g1, L0_ffn_b1, L0_ffn_g2, L0_ffn_b2, L0_ffn_Wr, L0_ffn_br, L0_ffn_Wq, L0_ffn_bq, L0_ffn_Wk, L0_ffn_bk, L0_ffn_Wv, L0_ffn_bv, L0_ffn_Wo, L0_ffn_bo, L0_ffn_Wm, L0_ffn_bm, L0_ffn_W1, L0_ffn_bf1, L0_ffn_W2, L0_ffn_bf2, L1_attn_w_attn, L1_attn_b_attn, L1_attn_w_proj, L1_attn_b_proj, L1_attn_w_mem, L1_attn_b_mem, L1_attn_w_alpha, L1_attn_b_alpha, L1_attn_memory_features, L1_ffn_w1, L1_ffn_g1, L1_ffn_w2, L1_ffn_g2):
    import jax
    import jax.numpy as jnp

    def _L0_tok_ref(x, embed_matrix):
        import jax, jax.numpy as jnp
        import numpy as np
        VOCAB = 50257
        EMBED = 192
        B, C = (4, 512)
        return jnp.take(embed_matrix, x, axis=0)

    def _L0_attn_ref(x, W_in, conv_w, conv_b, B, C, D, W_out):
        import jax, jax.numpy as jnp
        import numpy as np
        D_MODEL, D_STATE, D_CONV = (192, 8, 3)
        D_INNER = D_MODEL
        BATCH, SEQ = (4, 2048)

        def _forward(x, W_in, conv_w, conv_b, B, C, D, W_out):
            xz = x @ W_in
            xc, z = jnp.split(xz, 2, axis=-1)
            xc = jnp.transpose(xc, (0, 2, 1))
            xc = jax.lax.conv_general_dilated(xc, conv_w, window_strides=(1,), padding=[(D_CONV - 1, 0)], dimension_numbers=('NCH', 'OIH', 'NCH'), feature_group_count=D_INNER)
            xc = xc + conv_b[None, :, None]
            xc = jnp.transpose(xc, (0, 2, 1))
            xc = jax.nn.silu(xc)
            z = jax.nn.silu(z)
            BC = jnp.sum(B * C, axis=-1)
            y = jnp.cumsum(xc, axis=1) * BC + xc * D
            out = y * z @ W_out
            return out
        return _forward(x, W_in, conv_w, conv_b, B, C, D, W_out)

    def _L0_ffn_ref(hidden_states, g1, b1, g2, b2, Wr, br, Wq, bq, Wk, bk, Wv, bv, Wo, bo, Wm, bm, W1, bf1, W2, bf2):
        import jax, jax.numpy as jnp
        import numpy as np
        B, L, D, H, F = (4, 512, 192, 12, 768)
        ROUTE_FRAC = 0.15
        LN_EPS = 1e-05

        def _ln(x, g, b):
            m = jnp.mean(x, axis=-1, keepdims=True)
            v = jnp.mean((x - m) ** 2, axis=-1, keepdims=True)
            return (x - m) * jax.lax.rsqrt(v + LN_EPS) * g + b
        b, l, d = hidden_states.shape
        dh = d // H
        normed = _ln(hidden_states, g1, b1)
        scores = jax.nn.sigmoid(jnp.einsum('bld,d->bl', normed, Wr) + br)
        k = max(1, int(round(ROUTE_FRAC * l)))
        _, idx = jax.lax.top_k(-scores, k)
        attn_mask = jnp.zeros((b, l), bool).at[jnp.arange(b)[:, None], idx].set(True)
        q = (normed @ Wq + bq).reshape(b, l, H, dh)
        kk = (normed @ Wk + bk).reshape(b, l, H, dh)
        v = (normed @ Wv + bv).reshape(b, l, H, dh)
        logits = jnp.einsum('blhd,bmhd->bhlm', q, kk) / jnp.sqrt(jnp.float32(dh))
        probs = jax.nn.softmax(logits, axis=-1)
        ctx = jnp.einsum('bhlm,bmhd->blhd', probs, v).reshape(b, l, d)
        attn_out = ctx @ Wo + bo
        w = scores / (jnp.sum(scores, axis=1, keepdims=True) + 1e-06)
        pooled = jnp.einsum('bl,bld->bd', w, normed)
        mix_out = (normed + scores[..., None] * pooled[:, None, :]) @ Wm + bm
        merged = jnp.where(attn_mask[..., None], attn_out, mix_out)
        h = hidden_states + merged
        n2 = _ln(h, g2, b2)
        ffn = jax.nn.gelu(n2 @ W1 + bf1, approximate=False) @ W2 + bf2
        return h + ffn

    def _L1_attn_ref(x, w_attn, b_attn, w_proj, b_proj, w_mem, b_mem, w_alpha, b_alpha, memory_features):
        import jax, jax.numpy as jnp
        import numpy as np
        N_STATE = 192
        N_HEAD = 12
        D_HEAD = N_STATE // N_HEAD
        M_SLOTS = 100

        def _split_heads(t):
            B, T, _ = t.shape
            return t.reshape(B, T, N_HEAD, D_HEAD).transpose(0, 2, 1, 3)

        def _merge_heads(t):
            B, H, T, D = t.shape
            return t.transpose(0, 2, 1, 3).reshape(B, T, H * D)

        def _attn(q, k, v):
            w = jax.nn.softmax(jnp.einsum('bhqd,bhkd->bhqk', q, k), axis=-1)
            return jnp.einsum('bhqk,bhkd->bhqd', w, v)
        B, S, _ = x.shape
        qkv = x @ w_attn + b_attn
        q, k, v = jnp.split(qkv, 3, axis=-1)
        q = _split_heads(q)
        k = _split_heads(k)
        v = _split_heads(v)
        a = _merge_heads(_attn(q, k, v))
        mem = jnp.broadcast_to(memory_features, (B, M_SLOTS, N_STATE))
        mkv = mem @ w_mem + b_mem
        mk, mv = jnp.split(mkv, 2, axis=-1)
        mk = _split_heads(mk)
        mv = _split_heads(mv)
        a1 = _merge_heads(_attn(q, mk, mv))
        alpha = jax.nn.sigmoid(jnp.concatenate([a, a1], axis=-1) @ w_alpha + b_alpha)
        fused = alpha * a + (1.0 - alpha) * a1
        return fused @ w_proj + b_proj

    def _L1_ffn_ref(x, w1, g1, w2, g2):
        import jax, jax.numpy as jnp
        import numpy as np
        EMBED_DIM = 192
        FF_MULT = 4
        HIDDEN = EMBED_DIM * FF_MULT
        BATCH, SEQ = (32, 256)
        EPS = 1e-06

        def rmsnorm(x, g):
            return x * jax.lax.rsqrt(jnp.mean(x * x, axis=-1, keepdims=True) + EPS) * g

        def act_quant(x):
            scale = 127.0 / jnp.clip(jnp.max(jnp.abs(x), axis=-1, keepdims=True), 1e-05, None)
            return jnp.clip(jnp.round(x * scale), -128.0, 127.0) / scale

        def weight_quant(w):
            scale = 1.0 / jnp.clip(jnp.mean(jnp.abs(w)), 1e-05, None)
            return jnp.clip(jnp.round(w * scale), -1.0, 1.0) / scale

        def bitlinear(x, w, g):
            xn = rmsnorm(x, g)
            xq = xn + jax.lax.stop_gradient(act_quant(xn) - xn)
            wq = w + jax.lax.stop_gradient(weight_quant(w) - w)
            return jnp.einsum('bsd,fd->bsf', xq, wq)
        h = jax.nn.gelu(bitlinear(x, w1, g1), approximate=False)
        return bitlinear(h, w2, g2)
    h = _L0_tok_ref(x, L0_tok_embed_matrix)
    h = h + _L0_attn_ref(_layernorm(h, axis=-1), L0_attn_W_in, L0_attn_conv_w, L0_attn_conv_b, L0_attn_B, L0_attn_C, L0_attn_D, L0_attn_W_out)
    h = h + _L0_ffn_ref(_layernorm(h, axis=-1), L0_ffn_g1, L0_ffn_b1, L0_ffn_g2, L0_ffn_b2, L0_ffn_Wr, L0_ffn_br, L0_ffn_Wq, L0_ffn_bq, L0_ffn_Wk, L0_ffn_bk, L0_ffn_Wv, L0_ffn_bv, L0_ffn_Wo, L0_ffn_bo, L0_ffn_Wm, L0_ffn_bm, L0_ffn_W1, L0_ffn_bf1, L0_ffn_W2, L0_ffn_bf2)
    h = h + _L1_attn_ref(_layernorm(h, axis=-1), L1_attn_w_attn, L1_attn_b_attn, L1_attn_w_proj, L1_attn_b_proj, L1_attn_w_mem, L1_attn_b_mem, L1_attn_w_alpha, L1_attn_b_alpha, L1_attn_memory_features)
    h = h + _L1_ffn_ref(_layernorm(h, axis=-1), L1_ffn_w1, L1_ffn_g1, L1_ffn_w2, L1_ffn_g2)
    return h

_drawn_inputs = setup_inputs


def setup_inputs(seed=0):
    import zlib

    import numpy as np

    out = dict(_drawn_inputs(seed))
    spreads = {'L0_attn_conv_b': (0.0, 0.1),
     'L0_attn_D': (1.0, 0.6),
     'L0_ffn_g1': (1.0, 0.6),
     'L0_ffn_b1': (0.0, 0.8),
     'L0_ffn_g2': (1.0, 0.6),
     'L0_ffn_b2': (0.0, 0.8),
     'L0_ffn_bq': (0.0, 0.8),
     'L0_ffn_bk': (0.0, 0.8),
     'L0_ffn_bv': (0.0, 0.8),
     'L0_ffn_bo': (0.0, 0.8),
     'L0_ffn_bm': (0.0, 0.386),
     'L0_ffn_bf1': (0.0, 0.8),
     'L0_ffn_bf2': (0.0, 0.332),
     'L1_attn_b_attn': (0.0, 0.8),
     'L1_attn_b_proj': (0.0, 0.35),
     'L1_attn_b_mem': (0.0, 0.8),
     'L1_attn_b_alpha': (0.0, 0.8),
     'L1_ffn_g1': (1.0, 0.6),
     'L1_ffn_g2': (1.0, 0.6)}
    factors = {'L0_attn_conv_w': 3.261,
     'L0_ffn_Wq': 8.0,
     'L0_ffn_Wk': 8.0,
     'L0_ffn_Wv': 8.0,
     'L0_ffn_Wo': 8.0,
     'L0_ffn_W1': 2.983,
     'L0_ffn_W2': 2.757,
     'L1_attn_w_attn': 8.0,
     'L1_attn_w_proj': 8.0,
     'L1_attn_w_mem': 8.0,
     'L1_attn_w_alpha': 8.0,
     'L1_attn_memory_features': 8.0}
    for name, (base, spread) in spreads.items():
        noise = np.random.default_rng([zlib.crc32(name.encode()), seed]).standard_normal(out[name].shape)
        drawn = base * np.exp(spread * noise) if base else spread * noise
        out[name] = jnp.asarray(drawn.astype(out[name].dtype))
    for name, factor in factors.items():
        out[name] = (out[name] * factor).astype(out[name].dtype)
    return out
```

```python
from contextlib import ExitStack

import concourse.bass as bass
from concourse import mybir

F32 = mybir.dt.float32
BF16 = mybir.dt.bfloat16
I32 = mybir.dt.int32
ALU = mybir.AluOpType
ACT = mybir.ActivationFunctionType
AX = mybir.AxisListType

P = 128
D = 192
CH = 96
NB = 4
L = 1024
T = L // P
HALF = 512
H = 12
DH = D // H
VW = DH + 1
F = 768
FC = F // P
MS = 100
MSP = 104
NSEL = max(1, int(round(0.15 * L)))
QC = NSEL // 2
QP = 80
MAGIC = 12582912.0
LN_EPS = 1e-5
RMS_EPS = 1e-6
Q_PARTS = (0, 0, 1, 0, 2, 1)
K_PARTS = (0, 1, 0, 2, 0, 1)
KP = 6 * DH
NH = 2
VEC_LINKS = 156


def build(nc, A, out):
    ctx = ExitStack()
    with ctx:
        def sb(name, shape, dt=F32):
            return ctx.enter_context(nc.sbuf_tensor(name, shape, dt))

        def pb(name, shape, dt=F32):
            return ctx.enter_context(nc.psum_tensor(name, shape, dt))

        def sem(name):
            return ctx.enter_context(nc.semaphore(name))

        ident = sb("ident", [P, P])
        identb = sb("identb", [P, P], BF16)
        earlier = sb("earlier", [P, P])
        ones = sb("ones", [P, P])
        neghalf = sb("neghalf", [P, T])
        slot_i = sb("slot_i", [P, 2, QP], I32)
        slot = sb("slot", [P, 2, QP])
        rowslot_i = sb("rowslot_i", [P, 2], I32)
        rowslot = sb("rowslot", [P, 2])
        tok_i = sb("tok_i", [P, NB * T], I32)
        win = sb("win", [CH, 2, 2 * D])
        wout = sb("wout", [CH, 2, D])
        convw = sb("convw", [CH, 2, 3])
        cols = sb("cols", [CH, 2, 8])
        bmat = sb("bmat", [CH, 2, 8])
        cmat = sb("cmat", [CH, 2, 8])
        wr = sb("wr", [CH + 1, 2, 1])
        wq = sb("wq", [CH + 1, 2, D])
        wk = sb("wk", [CH + 1, 2, D])
        wv = sb("wv", [CH + 1, 2, D])
        wo = sb("wo", [CH + 1, 2, D])
        wm = sb("wm", [CH + 1, 2, D])
        wf1 = sb("wf1", [CH + 1, 2, F])
        wf2 = sb("wf2", [P, FC, D])
        bf2 = sb("bf2", [1, D])
        wat = sb("wat", [CH + 1, 2, 3 * D])
        wal = sb("wal", [CH + 1, 4, D])
        wpr = sb("wpr", [CH + 1, 2, D])
        g1bc = sb("g1bc", [P, D])
        g2bc = sb("g2bc", [P, F])
        wb1 = sb("wb1", [CH, 2, F], BF16)
        wb2 = sb("wb2", [P, FC, D], BF16)
        wscale = sb("wscale", [P, 2])
        wsinv = sb("wsinv", [P, 2])
        ksm = sb("ksm", [KP + 4, H, MSP], BF16)
        vm = sb("vm", [MS, H, VW])

        G = sb("G", [P, T, D])
        X = sb("X", [P, T, D])
        U = sb("U", [P, T, D])
        HP = sb("HP", [P, T, D])
        HS = sb("HS", [P, T, D])
        st = sb("st", [P, T, 6])
        mv = sb("mv", [P, T, 2])
        rn = sb("rn", [P, T])
        rnn = sb("rnn", [P, T])
        tp = sb("tp", [P, T])
        V = sb("V", [P, T, H, VW])
        XT = sb("XT", [CH + 1, 2, L])
        big = sb("big", [P, T * F + 4])
        XC = big[0:CH, 0:2 * (L + 2)].rearrange("p (c n) -> p c n", c=2)
        XS = big[0:CH, 2052:2052 + 2 * L].rearrange("p (c n) -> p c n", c=2)
        CUM = big[0:CH, 4100:4100 + 2 * L].rearrange("p (c n) -> p c n", c=2)
        hid = big[:, 0:FC * L].rearrange("p (f n) -> p f n", f=FC)
        BT = big[0:CH, 0:2 * L].rearrange("p (c n) -> p c n", c=2)
        HG = big[:, 0:T * F].rearrange("p (t f) -> p t f", t=T)
        rawq = sb("rawq", [P, H * L // 2])
        QS = rawq[0:KP + 4, :].bitcast(BF16).rearrange("p (h n) -> p h n", h=H)
        Y1 = rawq[0:CH, 0:2 * L].rearrange("p (c n) -> p c n", c=2)
        Z = rawq[0:CH, 2 * L:4 * L].rearrange("p (c n) -> p c n", c=2)
        PSEL = rawq[:, 4 * L:4 * L + T * 2 * QP].rearrange("p (t n) -> p t n", t=T)
        KS = sb("KS", [KP + 4, H, L], BF16)
        QS0 = sb("QS0", [KP + 4, H, 2 * QP], BF16)
        spl0 = sb("spl0", [CH, 3, 2, 2 * QP], BF16)
        R1 = sb("R1", [CH, 2, HALF])
        E = sb("E", [P, 3, L])
        spl = E[0:CH, :, :].rearrange("p a n -> p (a n)").bitcast(BF16).rearrange("p (a c n) -> p a c n", a=3, c=2)
        E0 = E[:, :, :].rearrange("p a n -> p (a n)")[:, 0:2 * T * 2 * QP].rearrange("p (a n) -> p a n", a=2)
        srow = sb("srow", [P, L])
        PT = rawq[:, 0:2 * L].rearrange("p (q n) -> p q n", q=2)
        XQ = rawq[:, 0:768].bitcast(BF16).rearrange("p (t d) -> p t d", t=T)
        XQT = rawq[0:CH, 768:1792].bitcast(BF16).rearrange("p (c n) -> p c n", c=2)
        HQ = rawq[:, 2560:3328].bitcast(BF16)
        HQT = rawq[:, 1792:2560].bitcast(BF16).rearrange("p (t f) -> p t f", t=2)
        NTS = sb("NTS", [CH + 1, 2, 2 * QP])
        CX = sb("CX", [QP, 2, D])
        CXT = sb("CXT", [CH + 1, 2, 2 * QP])
        ATS = sb("ATS", [QP, 2, D])
        sc = sb("sc", [P, T])
        sc1 = sb("sc1", [P, T])
        cnt = sb("cnt", [P, 3, T])
        rank = sb("rank", [P, T])
        notsel = sb("notsel", [P, T])
        junk = sb("junk", [P, L])
        junk2 = sb("junk2", [P, P])
        pool3 = sb("pool3", [CH, 8])
        nmp = sb("nmp", [P, T, 2])
        nm = sb("nm", [P, T, 2])
        nms = sb("nms", [P, 2, T, 2, 2], BF16)
        rec = sb("rec", [P, 2 * T])
        e2 = rawq[:, 3328:3328 + 4 * D].rearrange("p (i t d) -> p i t d", i=2, t=2)
        amax = sb("amax", [P, T])
        qsc = sb("qsc", [P, T])
        qinv = sb("qinv", [P, T])
        gsc = sb("gsc", [P, T])
        ss = sb("ss", [P, T])
        wsum = sb("wsum", [P, 2])
        memt = sb("memt", [CH + 1, 2, MS])
        memn = sb("memn", [MS, D])
        splm = sb("splm", [CH, 3, 2, MSP], BF16)

        ST = [pb("ST0", [P, 2 * HALF]), pb("ST1", [P, 2 * HALF])]
        S = [pb("S0", [P, HALF]), pb("S1", [P, HALF])]
        PV = pb("PV", [P, HALF])
        MT = pb("MT", [P, 2 * HALF], BF16)
        MTf = MT[:, :].bitcast(F32)
        ring4 = [ST[0][:, 0:HALF], ST[0][:, HALF:2 * HALF], ST[1][:, 0:HALF], ST[1][:, HALF:2 * HALF]]
        O = [PV[:, :], MTf]

        scr_k = nc.dram_tensor("scr_k", (3, D, L), BF16, kind="Internal").ap()
        scr_q = nc.dram_tensor("scr_q", (3, D, L), BF16, kind="Internal").ap()
        scr_q0 = nc.dram_tensor("scr_q0", (3, D, 2 * QP), BF16, kind="Internal").ap()
        scr_m = nc.dram_tensor("scr_m", (3, D, MSP), BF16, kind="Internal").ap()

        names = """loaded consts tokens gathered stats rstd xnorm turned evac inproj inproj_out conv silu
            gated outproj h1 logit expz score srow_turned srow_copied picks rank_turned pt gathersel nts
            proj hi resid mid lo vproj vcopied units reduced rowmax mturned mcopied st0 ex0 pv0 ctx ctxn
            ctxt ctxtc att atts pooled pooledv mixin mixed merged hidden gelu ffn h2 stile exps pv normed
            alpha alphae fusedx fproj h3 quant qturned qcopied bhid bgelu hss hrms hquant hturned hcopied
            bout outs stored vlink plink xpose pp pa pd kw0 kw1 kr0 kr1 qw0 qw1 qr0 qr1 q0w q0r mw mr""".split()
        s = {n: sem("s_" + n) for n in names}
        block = ctx.enter_context(nc.Block())

        ovw = out.rearrange("b (t p) d -> b p t d", p=P)

        def cm(w, p=CH):
            return w.rearrange("(c p) n -> p c n", p=p)

        def stack(scr, c, part):
            return scr[part, c * CH:(c + 1) * CH, :].rearrange("(h p) n -> p h n", p=DH)

        loads = []

        @block.sync
        def _(sp):
            n = [0]

            def load(dst, src):
                sp.dma_start(dst, src, allow_slow_non_contiguous=True).then_inc(s["loaded"], 16)
                n[0] += 1

            load(win[:], cm(A["L0_attn_W_in"]))
            load(wout[:], cm(A["L0_attn_W_out"]))
            load(convw[:], A["L0_attn_conv_w"].rearrange("(c p) a k -> p c (a k)", p=CH))
            for i, name in enumerate(["L0_attn_conv_b", "L0_attn_D", "L0_ffn_g1", "L0_ffn_b1", "L0_ffn_g2", "L0_ffn_b2"]):
                load(cols[:, :, i], A[name].rearrange("(c p) -> p c", p=CH))
            load(bmat[:], cm(A["L0_attn_B"]))
            load(cmat[:], cm(A["L0_attn_C"]))
            load(wr[0:CH, :, 0], A["L0_ffn_Wr"].rearrange("(c p) -> p c", p=CH))
            load(wr[CH:CH + 1, 1, :], A["L0_ffn_br"].rearrange("(a n) -> a n", a=1))
            for w, wn, bn in ((wq, "L0_ffn_Wq", "L0_ffn_bq"), (wk, "L0_ffn_Wk", "L0_ffn_bk"), (wv, "L0_ffn_Wv", "L0_ffn_bv"),
                              (wo, "L0_ffn_Wo", "L0_ffn_bo"), (wm, "L0_ffn_Wm", "L0_ffn_bm"), (wf1, "L0_ffn_W1", "L0_ffn_bf1"),
                              (wat, "L1_attn_w_attn", "L1_attn_b_attn"), (wal, "L1_attn_w_alpha", "L1_attn_b_alpha"),
                              (wpr, "L1_attn_w_proj", "L1_attn_b_proj")):
                load(w[0:CH, :, :], cm(A[wn]))
                load(w[CH:CH + 1, 1, :], A[bn].rearrange("(a n) -> a n", a=1))
            load(wf2[:], cm(A["L0_ffn_W2"], P))
            load(bf2[:], A["L0_ffn_bf2"].rearrange("(a n) -> a n", a=1))
            load(g1bc[:], A["L1_ffn_g1"].partition_broadcast(P))
            load(g2bc[:], A["L1_ffn_g2"].partition_broadcast(P))
            load(memn[:], A["L1_attn_memory_features"][0])
            load(XT[0:CH, :, 0:2 * D], cm(A["L1_attn_w_mem"]))
            load(XT[CH:CH + 1, 1, 0:2 * D], A["L1_attn_b_mem"].rearrange("(a n) -> a n", a=1))
            load(X[:, 0:FC, :], cm(A["L1_ffn_w1"], P))
            load(HG[0:CH, 0:2, :], cm(A["L1_ffn_w2"]))
            loads.append(n[0])

            sp.wait_ge(s["pd"], 2)
            for c in range(2):
                sp.dma_start(scr_m[:, c * CH:(c + 1) * CH, :].rearrange("a r n -> r a n"), splm[:, :, c, :]).then_inc(s["mw"], 16)
            sp.wait_ge(s["mw"], 32)
            for c in range(2):
                for j in range(6):
                    sp.dma_start(ksm[DH * j:DH * j + DH, 6 * c:6 * c + 6, :], stack(scr_m, c, K_PARTS[j])).then_inc(s["mr"], 16)

            def restack(b, src, scr, dst, parts, group, kw, kr, uses, use):
                for c in range(2):
                    sp.wait_ge(s["lo"], b * 14 + group + 2 * c + 2)
                    sp.dma_start(scr[:, c * CH:(c + 1) * CH, :].rearrange("a r n -> r a n"), src[:, :, c, :]).then_inc(s[kw[c]], 16)
                for c in range(2):
                    sp.wait_ge(s[kw[c]], (b * uses + use + 1) * 16)
                    for j in range(6):
                        sp.dma_start(dst[DH * j:DH * j + DH, 6 * c:6 * c + 6, :], stack(scr, c, parts[j])).then_inc(s[kr[c]], 16)

            with sp.Fori(0, NB) as b:
                restack(b, spl, scr_k, KS, K_PARTS, 0, ("kw0", "kw1"), ("kr0", "kr1"), 2, 0)
                sp.wait_ge(s["lo"], b * 14 + 6)
                for c in range(2):
                    sp.dma_start(scr_q0[:, c * CH:(c + 1) * CH, :].rearrange("a r n -> r a n"), spl0[:, :, c, :]).then_inc(s["q0w"], 16)
                sp.wait_ge(s["q0w"], b * 32 + 32)
                for c in range(2):
                    for j in range(6):
                        sp.dma_start(QS0[DH * j:DH * j + DH, 6 * c:6 * c + 6, :], stack(scr_q0, c, Q_PARTS[j])).then_inc(s["q0r"], 16)
                restack(b, spl, scr_k, KS, K_PARTS, 6, ("kw0", "kw1"), ("kr0", "kr1"), 2, 1)
                restack(b, spl, scr_q, QS, Q_PARTS, 10, ("qw0", "qw1"), ("qr0", "qr1"), 1, 0)

        LOADED = loads[0] * 16

        @block.gpsimd
        def _(g):
            k = [0]

            def link(ins):
                k[0] += 1
                ins.then_inc(s["plink"], 1)
                g.wait_ge(s["plink"], k[0])

            made = [0]

            def const(ins):
                made[0] += 1
                ins.then_inc(s["consts"], 1)
                g.wait_ge(s["consts"], made[0])

            link(g.memset(ident[:], 0.0))
            link(g.affine_select(out=ident[:], in_=ident[:], compare_op=ALU.not_equal, fill=1.0, base=0, pattern=[[-1, P]], channel_multiplier=1))
            const(g.tensor_copy(identb[:], ident[:]))
            link(g.memset(earlier[:], 1.0))
            const(g.affine_select(out=earlier[:], in_=earlier[:], compare_op=ALU.is_gt, fill=0.0, base=0, pattern=[[-1, P]], channel_multiplier=1))
            const(g.memset(ones[:], 1.0))
            const(g.memset(neghalf[:], -0.5))
            link(g.iota(slot_i[:], pattern=[[QC, 2], [1, QP]], base=0, channel_multiplier=0))
            const(g.tensor_copy(slot[:], slot_i[:]))
            link(g.iota(rowslot_i[:], pattern=[[QC, 2]], base=0, channel_multiplier=1))
            const(g.tensor_copy(rowslot[:], rowslot_i[:]))
            const(g.memset(V[:, :, :, DH:VW], 1.0))
            const(g.memset(vm[:, :, DH:VW], 1.0))
            const(g.memset(NTS[CH:CH + 1, :, :], 1.0))
            const(g.memset(CXT[CH:CH + 1, :, :], 1.0))
            const(g.memset(memt[CH:CH + 1, :, :], 1.0))
            const(g.memset(splm[:], 0.0))
            link(g.memset(KS[KP:KP + 4, :, :], 0.0))
            const(g.memset(KS[KP:KP + 2, :, :], 1.0))
            link(g.memset(ksm[KP:KP + 4, :, :], 1.0))
            const(g.memset(ksm[KP:KP + 2, :, :], 0.0))
            link(g.memset(QS0[KP:KP + 4, :, :], 0.0))
            const(g.memset(cnt[:], 0.0))
            g.dma_start(tok_i[:], A["x"].rearrange("b (t p) -> p (b t)", p=P), allow_slow_non_contiguous=True).then_inc(s["tokens"], 16)

            def rsqrt(dst, src, eps):
                link(g.tensor_scalar(tp[:], src, eps, None, ALU.add))
                return g.tensor_tensor(dst, tp[:], neghalf[:], ALU.pow)

            def inverse_deviation(b, n, second=None):
                g.wait_ge(s["stats"], b * 5 + n + 1)
                ins = rsqrt(rn[:], mv[:, :, 1], LN_EPS)
                if second is None:
                    ins.then_inc(s["rstd"], 1)
                    return
                link(ins)
                link(g.tensor_tensor(tp[:], mv[:, :, 1], rn[:], ALU.mult))
                link(g.tensor_tensor(rnn[:], tp[:], rn[:], ALU.mult))
                link(rsqrt(rnn[:], rnn[:], second))
                g.tensor_tensor(rnn[:], rnn[:], rn[:], ALU.mult).then_inc(s["rstd"], 1)

            for b in range(NB):
                if b == 0:
                    g.wait_ge(s["tokens"], 16)
                else:
                    g.wait_ge(s["h1"], b * 4)
                for t in range(T):
                    g.indirect_dma_start(G[:, t, :], None, A["L0_tok_embed_matrix"][:],
                                         bass.IndirectOffsetOnAxis(ap=tok_i[:, b * T + t:b * T + t + 1], axis=0)).then_inc(s["gathered"], 16)
                inverse_deviation(b, 0)
                inverse_deviation(b, 1, LN_EPS)
                inverse_deviation(b, 2)
                inverse_deviation(b, 3)
                inverse_deviation(b, 4, RMS_EPS)
                g.wait_ge(s["hss"], b * 8 + 8)
                link(g.tensor_scalar(tp[:], ss[:], 1.0 / F, None, ALU.mult))
                rsqrt(rn[:], tp[:], RMS_EPS).then_inc(s["hrms"], 1)

        @block.tensor
        def _(pe):
            pe.wait_ge(s["consts"], 15)
            pe.wait_ge(s["loaded"], LOADED)
            for c in range(2):
                nc.tensor.transpose(S[0][0:CH, c * P:c * P + MS], memn[:, c * CH:(c + 1) * CH], ident[0:MS, 0:MS]).then_inc(s["pp"], 1)
            pe.wait_ge(s["pa"], 1)
            for m in range(2):
                for c in range(2):
                    r = CH + c
                    ins = nc.tensor.matmul(S[1][0:CH, m * P:m * P + MS], XT[0:r, c, m * CH:(m + 1) * CH], memt[0:r, c, :], start=c == 0, stop=c == 1)
            ins.then_inc(s["pp"], 1)
            for c in range(2):
                ins = nc.tensor.matmul(ST[0][0:MS, 0:D], memt[0:CH + c, c, :], XT[0:CH + c, c, D:2 * D], start=c == 0, stop=c == 1)
            ins.then_inc(s["pp"], 1)
            pe.wait_ge(s["pd"], 3)
            nc.tensor.matmul(PV[:, 0:1], ones[:], wsum[:, 0:1], start=True, stop=True)
            nc.tensor.matmul(PV[:, 1:2], ones[0:CH, :], wsum[0:CH, 1:2], start=True, stop=True).then_inc(s["pp"], 1)
            pe.wait_ge(s["pd"], 5)
            t1 = ST[1][:, 0:HALF].bitcast(BF16)
            t2 = ST[1][:, HALF:2 * HALF].bitcast(BF16)
            t3 = [ST[0][:, 0:HALF].bitcast(BF16), ST[0][:, HALF:2 * HALF].bitcast(BF16)]
            pe.wait_ge(s["pa"], 3)
            for f in range(FC):
                for c in range(2):
                    nc.tensor.transpose((t1, t2)[c][0:CH, f * P:(f + 1) * P], XQ[:, f, c * CH:(c + 1) * CH], identb[:])
            for f in range(FC):
                for c in range(2):
                    ins = nc.tensor.transpose(t3[f // 3][:, (f % 3) * D + c * CH:(f % 3) * D + (c + 1) * CH], HQT[0:CH, c, f * P:(f + 1) * P], identb[0:CH, 0:CH])
            ins.then_inc(s["pp"], 1)
            pe.wait_ge(s["pa"], 4)

            def turn(b, job, src, ready, counts):
                for i in range(4):
                    half, c = i // 2, i % 2
                    if c == 0:
                        pe.wait_ge(s[ready], b * counts[0] + counts[1 + half])
                    pe.wait_ge(s["evac"], b * 28 + 4 * job + i + 1)
                    for t in range(4):
                        ins = nc.tensor.transpose(S[i % 2][0:CH, t * P:(t + 1) * P], src[:, 4 * half + t, c * CH:(c + 1) * CH], ident[:])
                    ins.then_inc(s["turned"], 1)

            def rows(dst, lhs, w, cs, bias):
                n = len(cs)
                for i, (x, wt, c) in enumerate(cs):
                    r = CH + (1 if bias and c == 1 else 0)
                    ins = nc.tensor.matmul(dst, x[0:r], wt[0:r], start=i == 0, stop=i == n - 1)
                return ins

            def project(b, group, w, off, src, width, spans):
                i = group
                for m in range(2):
                    for j in range(spans):
                        if i >= 4:
                            pe.wait_ge(s["resid"], b * 14 + i - 3)
                        for c in range(2):
                            r = CH + c
                            ins = nc.tensor.matmul(ring4[i % 4][0:CH, 0:width], w[0:r, c, off + m * CH:off + (m + 1) * CH],
                                                   src[0:r, c, j * width:(j + 1) * width], start=c == 0, stop=c == 1)
                        ins.then_inc(s["proj"], 1)
                        i += 1

            def values(b, use, w, off):
                for i in range(4):
                    n = 4 * use + i
                    if i >= 2:
                        pe.wait_ge(s["vcopied"], b * 8 + n - 1)
                    for t in (2 * i, 2 * i + 1):
                        for c in range(2):
                            r = CH + c
                            ins = nc.tensor.matmul(O[i % 2][:, (t % 2) * D:(t % 2 + 1) * D], XT[0:r, c, t * P:(t + 1) * P],
                                                   w[0:r, c, off:off + D], start=c == 0, stop=c == 1)
                    ins.then_inc(s["vproj"], 1)

            with pe.Fori(0, NB) as b:
                turn(b, 0, X, "xnorm", (8, 1, 2))
                pe.wait_ge(s["evac"], b * 28 + 4 + 2)
                for i in range(8):
                    m, half = i // 2, i % 2
                    if i >= 4:
                        pe.wait_ge(s["inproj_out"], b * 8 + i - 3)
                    for c in range(2):
                        ins = nc.tensor.matmul(ring4[i % 4][0:CH, :], win[:, c, m * CH:(m + 1) * CH], XT[0:CH, c, half * HALF:(half + 1) * HALF],
                                               start=c == 0, stop=c == 1)
                    ins.then_inc(s["inproj"], 1)
                pe.wait_ge(s["gated"], b * 2 + 2)
                for i in range(4):
                    if i >= 2:
                        pe.wait_ge(s["h1"], b * 4 + i - 1)
                    for t in (2 * i, 2 * i + 1):
                        for c in range(2):
                            ins = nc.tensor.matmul(O[i % 2][:, (t % 2) * D:(t % 2 + 1) * D], CUM[:, c, t * P:(t + 1) * P], wout[:, c, :],
                                                   start=c == 0, stop=c == 1)
                    ins.then_inc(s["outproj"], 1)
                turn(b, 1, X, "xnorm", (8, 3, 4))
                pe.wait_ge(s["evac"], b * 28 + 8 + 2)
                for t in range(T):
                    for c in range(2):
                        r = CH + c
                        ins = nc.tensor.matmul(PV[:, t:t + 1], XT[0:r, c, t * P:(t + 1) * P], wr[0:r, c, :], start=c == 0, stop=c == 1)
                ins.then_inc(s["logit"], 1)
                project(b, 0, wk, 0, XT, HALF, 2)
                pe.wait_ge(s["score"], b * 1 + 1)
                for t in range(T):
                    if t == 0:
                        pe.wait_ge(s["resid"], b * 14 + 4)
                    ins = nc.tensor.transpose(ST[0][:, t * P:(t + 1) * P], sc[:, t:t + 1].to_broadcast([P, P]), ident[:])
                ins.then_inc(s["srow_turned"], 1)
                for j in range(3):
                    for t in range(T):
                        lhs = X[:, t, j * CH:(j + 1) * CH] if j < 2 else ones[:, 0:CH]
                        ins = nc.tensor.matmul(ST[1][0:CH, j:j + 1], lhs, sc[:, t:t + 1], start=t == 0, stop=t == T - 1)
                ins.then_inc(s["pooled"], 1)
                values(b, 0, wv, 0)
                pe.wait_ge(s["picks"], b * 2 + 1)
                pe.wait_ge(s["srow_copied"], b * 1 + 1)
                for t in range(T):
                    ins = nc.tensor.transpose(ST[0][:, t * P:(t + 1) * P], rank[:, t:t + 1].to_broadcast([P, P]), ident[:])
                ins.then_inc(s["rank_turned"], 1)
                pe.wait_ge(s["picks"], b * 2 + 2)
                for c in range(2):
                    for t in range(T):
                        ins = nc.tensor.matmul(S[0][0:CH, c * 2 * QP:(c + 1) * 2 * QP], X[:, t, c * CH:(c + 1) * CH], PSEL[:, t, :],
                                               start=t == 0, stop=t == T - 1)
                ins.then_inc(s["gathersel"], 1)
                pe.wait_ge(s["nts"], b * 2 + 2)
                pe.wait_ge(s["pt"], b * 1 + 1)
                project(b, 4, wq, 0, NTS, 2 * QP, 1)

                def units0(h):
                    for u in range(4):
                        n = 4 * h + u
                        pe.wait_ge(s["reduced"], b * 264 + n + 1)
                        nc.tensor.matmul(S[n % 2][0:QP, :], QS0[0:KP, h, (u // 2) * QP:(u // 2 + 1) * QP],
                                         KS[0:KP, h, (u % 2) * HALF:(u % 2 + 1) * HALF], start=True, stop=True).then_inc(s["units"], 1)

                def maxrow0(h):
                    pe.wait_ge(s["rowmax"], b * 24 + h + 1)
                    pe.wait_ge(s["mcopied"], b * 24 + h + 1)
                    for q in range(2):
                        ins = nc.tensor.transpose(MT[KP:KP + 2, q * QP:(q + 1) * QP], nms[0:QP, h % 2, q, 0, :], identb[0:QP, 0:QP])
                    ins.then_inc(s["mturned"], 1)

                def exps0(h):
                    pe.wait_ge(s["mcopied"], b * 24 + h + 2)
                    for i in range(3):
                        n = 3 * h + i
                        pe.wait_ge(s["ex0"], b * 36 + n + 1)
                        for kt in range(3 * i, min(3 * i + 3, T)):
                            ins = nc.tensor.matmul(ring4[n % 4][:, (kt - 3 * i) * 2 * QP:(kt - 3 * i + 1) * 2 * QP], KS[0:KP + 2, h, kt * P:(kt + 1) * P],
                                                   QS0[0:KP + 2, h, :], start=True, stop=True)
                        ins.then_inc(s["st0"], 1)

                def pv0(h):
                    pe.wait_ge(s["ex0"], b * 36 + 3 * h + 3 + 4)
                    for q in range(2):
                        for kt in range(T):
                            ins = nc.tensor.matmul(PV[0:QP, q * H * VW + h * VW:q * H * VW + (h + 1) * VW], E0[:, h % 2, kt * 2 * QP + q * QP:kt * 2 * QP + (q + 1) * QP],
                                                   V[:, kt, h, :], start=kt == 0, stop=kt == T - 1)
                    ins.then_inc(s["pv0"], 1)

                pe.wait_ge(s["q0r"], b * 192 + 192)
                pe.wait_ge(s["kr0"], b * 192 + 96)
                pe.wait_ge(s["vcopied"], b * 8 + 4)
                pe.wait_ge(s["resid"], b * 14 + 6)
                units0(0)
                units0(1)
                maxrow0(0)
                for h in range(H):
                    exps0(h)
                    if h + 2 == 6:
                        pe.wait_ge(s["kr1"], b * 192 + 96)
                    if h + 2 < H:
                        units0(h + 2)
                    if h >= 1:
                        pv0(h - 1)
                    if h + 1 < H:
                        maxrow0(h + 1)
                pv0(H - 1)
                pe.wait_ge(s["ctxn"], b * 1 + 1)
                for c in range(2):
                    for q in range(2):
                        ins = nc.tensor.transpose(ST[0][0:CH, (2 * c + q) * QP:(2 * c + q + 1) * QP], CX[:, q, c * CH:(c + 1) * CH], ident[0:QP, 0:QP])
                ins.then_inc(s["ctxt"], 1)
                pe.wait_ge(s["ctxtc"], b * 1 + 1)
                for q in range(2):
                    for c in range(2):
                        r = CH + c
                        ins = nc.tensor.matmul(ST[1][0:QP, q * D:(q + 1) * D], CXT[0:r, c, q * QP:(q + 1) * QP], wo[0:r, c, :], start=c == 0, stop=c == 1)
                ins.then_inc(s["att"], 1)
                pe.wait_ge(s["mixin"], b * 2 + 2)
                pe.wait_ge(s["atts"], b * 1 + 1)
                for t in range(T):
                    if t >= 2:
                        pe.wait_ge(s["merged"], b * 8 + t - 1)
                    o = O[t % 2]
                    for c in range(2):
                        r = CH + c
                        nc.tensor.matmul(o[:, 0:D], XT[0:r, c, t * P:(t + 1) * P], wm[0:r, c, :], start=c == 0, stop=c == 1)
                    for q in range(2):
                        ins = nc.tensor.matmul(o[:, D:2 * D], PT[0:QC, q, t * P:(t + 1) * P], ATS[0:QC, q, :], start=q == 0, stop=q == 1)
                    ins.then_inc(s["mixed"], 1)
                turn(b, 2, X, "xnorm", (8, 5, 6))
                pe.wait_ge(s["evac"], b * 28 + 12 + 2)
                for half in range(NH):
                    for f in range(FC):
                        i = half * FC + f
                        if i >= 4:
                            pe.wait_ge(s["gelu"], b * 12 + i - 3)
                        for c in range(2):
                            r = CH + c
                            ins = nc.tensor.matmul(ring4[i % 4], wf1[0:r, c, f * P:(f + 1) * P], XT[0:r, c, half * HALF:(half + 1) * HALF], start=c == 0, stop=c == 1)
                        ins.then_inc(s["hidden"], 1)
                for i in range(4):
                    pe.wait_ge(s["gelu"], b * 12 + (6 if i < 2 else 12))
                    if i >= 2:
                        pe.wait_ge(s["h2"], b * 4 + i - 1)
                    for t in (2 * i, 2 * i + 1):
                        o = O[i % 2][:, (t % 2) * D:(t % 2 + 1) * D]
                        for f in range(FC):
                            nc.tensor.matmul(o, hid[:, f, t * P:(t + 1) * P], wf2[:, f, :], start=f == 0, stop=False)
                        ins = nc.tensor.matmul(o, ones[0:1, :], bf2[:], start=False, stop=True)
                    ins.then_inc(s["ffn"], 1)
                turn(b, 3, X, "xnorm", (8, 7, 8))
                pe.wait_ge(s["evac"], b * 28 + 16 + 2)
                project(b, 6, wat, D, XT, HALF, 2)
                project(b, 10, wat, 0, XT, HALF, 2)
                values(b, 1, wat, 2 * D)

                def unit(n):
                    h, u = n // 18, n % 18
                    pe.wait_ge(s["reduced"], b * 264 + 48 + n + 1)
                    if u < 16:
                        ins = nc.tensor.matmul(S[n % 2][:, :], QS[0:KP, h, (u // 2) * P:(u // 2 + 1) * P], KS[0:KP, h, (u % 2) * HALF:(u % 2 + 1) * HALF],
                                               start=True, stop=True)
                    else:
                        for t in range(4):
                            qt = 4 * (u - 16) + t
                            ins = nc.tensor.matmul(S[n % 2][:, t * MSP:t * MSP + MS], QS[0:KP, h, qt * P:(qt + 1) * P], ksm[0:KP, h, 0:MS], start=True, stop=True)
                    ins.then_inc(s["units"], 1)

                def maxrow(h):
                    pe.wait_ge(s["rowmax"], b * 24 + 12 + h + 1)
                    pe.wait_ge(s["mcopied"], b * 24 + 12 + h + 1)
                    for t in range(T):
                        ins = nc.tensor.transpose(MT[KP:KP + 4, t * P:(t + 1) * P], nms[:, h % 2, t, :, :].rearrange("p a c -> p (a c)"), identb[:])
                    ins.then_inc(s["mturned"], 1)

                def scores(i):
                    h, kt = i // 9, i % 9
                    pe.wait_ge(s["exps"], b * 108 + i + 1)
                    if kt == 0:
                        pe.wait_ge(s["mcopied"], b * 24 + 12 + h + 2)
                    keys, m = (KS[0:KP + 4, h, kt * P:(kt + 1) * P], P) if kt < T else (ksm[0:KP + 4, h, 0:MS], MS)
                    for half in range(NH):
                        ins = nc.tensor.matmul(ST[i % 2][0:m, half * HALF:(half + 1) * HALF], keys, QS[0:KP + 4, h, half * HALF:(half + 1) * HALF],
                                               start=True, stop=True)
                    ins.then_inc(s["stile"], 1)

                def weigh(i):
                    h, kt = i // 9, i % 9
                    pe.wait_ge(s["exps"], b * 108 + i + 3)
                    if kt == 0:
                        pe.wait_ge(s["normed"], b * 12 + h + 1)
                    for qt in range(T):
                        if kt < T:
                            ins = nc.tensor.matmul(PV[:, qt * VW:(qt + 1) * VW], E[:, i % 3, qt * P:(qt + 1) * P], V[:, kt, h, :],
                                                   start=(kt == 0 and qt == 0), stop=kt == T - 1, skip_group_check=True)
                        else:
                            ins = nc.tensor.matmul(PV[:, (T + qt) * VW:(T + qt + 1) * VW], E[0:MS, i % 3, qt * P:(qt + 1) * P], vm[:, h, :],
                                                   start=False, stop=True, skip_group_check=True)
                    ins.then_inc(s["pv"], 1)

                pe.wait_ge(s["kr0"], b * 192 + 192)
                pe.wait_ge(s["qr0"], b * 96 + 96)
                pe.wait_ge(s["vcopied"], b * 8 + 8)
                pe.wait_ge(s["mr"], 192)
                pe.wait_ge(s["resid"], b * 14 + 14)
                for n in range(36):
                    unit(n)
                maxrow(0)
                for i in range(9 * H):
                    h, kt = i // 9, i % 9
                    scores(i)
                    if h + 2 == 6 and kt == 0:
                        pe.wait_ge(s["kr1"], b * 192 + 192)
                        pe.wait_ge(s["qr1"], b * 96 + 96)
                    if h + 2 < H:
                        unit(36 + 2 * i)
                        unit(36 + 2 * i + 1)
                    if i >= 1:
                        weigh(i - 1)
                    if kt == 4 and h + 1 < H:
                        maxrow(h + 1)
                weigh(9 * H - 1)
                turn(b, 4, U, "normed", (12, 13, 13))
                turn(b, 5, HP, "normed", (12, 13, 13))
                pe.wait_ge(s["evac"], b * 28 + 24 + 2)
                for i in range(4):
                    if i >= 2:
                        pe.wait_ge(s["alphae"], b * 4 + i - 1)
                    for t in (2 * i, 2 * i + 1):
                        o = O[i % 2][:, (t % 2) * D:(t % 2 + 1) * D]
                        for c in range(4):
                            r = CH + (1 if c == 1 else 0)
                            x = XT[0:r, c, t * P:(t + 1) * P] if c < 2 else BT[:, c - 2, t * P:(t + 1) * P]
                            ins = nc.tensor.matmul(o, x, wal[0:r, c, :], start=c == 0, stop=c == 3)
                    ins.then_inc(s["alpha"], 1)
                turn(b, 6, X, "fusedx", (4, 2, 4))
                pe.wait_ge(s["evac"], b * 28 + 28 + 2)
                for i in range(4):
                    if i >= 2:
                        pe.wait_ge(s["h3"], b * 4 + i - 1)
                    for t in (2 * i, 2 * i + 1):
                        for c in range(2):
                            r = CH + c
                            ins = nc.tensor.matmul(O[i % 2][:, (t % 2) * D:(t % 2 + 1) * D], XT[0:r, c, t * P:(t + 1) * P], wpr[0:r, c, :], start=c == 0, stop=c == 1)
                    ins.then_inc(s["fproj"], 1)
                for i in range(4):
                    half, c = i // 2, i % 2
                    pe.wait_ge(s["quant"], b * 8 + 4 * half + 4)
                    if i >= 2:
                        pe.wait_ge(s["qcopied"], b * 4 + i - 1)
                    sb16 = S[i % 2][:, :].bitcast(BF16)
                    for t in range(4):
                        ins = nc.tensor.transpose(sb16[0:CH, t * P:(t + 1) * P], XQ[:, 4 * half + t, c * CH:(c + 1) * CH], identb[:])
                    ins.then_inc(s["qturned"], 1)
                pe.wait_ge(s["qcopied"], b * 4 + 4)
                for t in range(T):
                    if t >= 2:
                        pe.wait_ge(s["bgelu"], b * 8 + t - 1)
                    for n0, n1 in ((0, HALF), (HALF, F)):
                        for c in range(2):
                            ins = nc.tensor.matmul(ST[t % 2][:, n0:n1], XQT[:, c, t * P:(t + 1) * P], wb1[:, c, n0:n1], start=c == 0, stop=c == 1)
                    ins.then_inc(s["bhid"], 1)
                for t in range(T):
                    pe.wait_ge(s["hquant"], b * 8 + t + 1)
                    if t >= 2:
                        pe.wait_ge(s["hcopied"], b * 8 + t - 1)
                    sb16 = S[t % 2][:, :].bitcast(BF16)
                    for f in range(FC):
                        ins = nc.tensor.transpose(sb16[:, f * P:(f + 1) * P], HQ[:, (t % 2) * F + f * P:(t % 2) * F + (f + 1) * P], identb[:])
                    ins.then_inc(s["hturned"], 1)
                    pe.wait_ge(s["hcopied"], b * 8 + t + 1)
                    if t >= 4:
                        pe.wait_ge(s["outs"], b * 4 + t // 2 - 1)
                    for f in range(FC):
                        ins = nc.tensor.matmul(O[(t // 2) % 2][:, (t % 2) * D:(t % 2 + 1) * D], HQT[:, t % 2, f * P:(f + 1) * P], wb2[:, f, :], start=f == 0, stop=f == FC - 1)
                    ins.then_inc(s["bout"], 1)

        @block.scalar
        def _(act):
            A_ = nc.scalar.activation
            act.wait_ge(s["consts"], 15)
            act.wait_ge(s["pp"], 2)
            A_(memt[0:CH, :, :], S[0][0:CH, 0:2 * P].rearrange("p (c n) -> p c n", c=2)[:, :, 0:MS], ACT.Copy).then_inc(s["pa"], 1)
            act.wait_ge(s["pp"], 3)
            A_(splm[:, 0, :, 0:MS], S[1][0:CH, 0:2 * P].rearrange("p (c n) -> p c n", c=2)[:, :, 0:MS], ACT.Copy).then_inc(s["hi"], 1)
            act.wait_ge(s["pp"], 4)
            A_(vm[:, :, 0:DH], ST[0][0:MS, 0:D].rearrange("p (h d) -> p h d", h=H), ACT.Copy).then_inc(s["pa"], 1)
            act.wait_ge(s["pd"], 1)
            A_(splm[:, 1, :, 0:MS], R1[:, 0, 0:2 * MSP].rearrange("p (c n) -> p c n", c=2)[:, :, 0:MS], ACT.Copy).then_inc(s["pa"], 1)
            act.wait_ge(s["pp"], 6)
            A_(wb1[:, 0, :], ST[1][0:CH, 0:HALF].bitcast(BF16)[:, 0:F], ACT.Copy)
            A_(wb1[:, 1, :], ST[1][0:CH, HALF:2 * HALF].bitcast(BF16)[:, 0:F], ACT.Copy)
            A_(wb2[:, 0:3, :], ST[0][:, 0:HALF].bitcast(BF16)[:, 0:3 * D].rearrange("p (f d) -> p f d", f=3), ACT.Copy)
            A_(wb2[:, 3:6, :], ST[0][:, HALF:2 * HALF].bitcast(BF16)[:, 0:3 * D].rearrange("p (f d) -> p f d", f=3), ACT.Copy).then_inc(s["evac"], 2)

            def evac(b, job, dst, scale=None, bias=None):
                for i in range(4):
                    half, c = i // 2, i % 2
                    act.wait_ge(s["turned"], b * 28 + 4 * job + i + 1)
                    o = dst[0:CH, c, half * HALF:(half + 1) * HALF]
                    if scale is None:
                        ins = A_(o, S[i % 2][0:CH, :], ACT.Copy)
                    else:
                        ins = A_(o, S[i % 2][0:CH, :], ACT.Identity, scale=cols[:, c, scale:scale + 1], bias=cols[:, c, bias:bias + 1])
                    ins.then_inc(s["evac"], 1)

            def cut(b, group, dst, width, spans, waits=None):
                def mid(i):
                    m, j = (i - group) // spans, (i - group) % spans
                    act.wait_ge(s["resid"], b * 14 + i + 1)
                    A_(dst[:, 1, m, j * width:(j + 1) * width], R1[:, i % 2, 0:width], ACT.Copy).then_inc(s["mid"], 1)
                for i in range(group, group + 2 * spans):
                    m, j = (i - group) // spans, (i - group) % spans
                    act.wait_ge(s["proj"], b * 14 + i + 1)
                    A_(dst[:, 0, m, j * width:(j + 1) * width], ring4[i % 4][0:CH, 0:width], ACT.Copy).then_inc(s["hi"], 1)
                    if i > group:
                        mid(i - 1)
                mid(group + 2 * spans - 1)

            def vcopy(b, use):
                for i in range(4):
                    act.wait_ge(s["vproj"], b * 8 + 4 * use + i + 1)
                    A_(V[:, 2 * i:2 * i + 2, :, 0:DH], O[i % 2][:, 0:2 * D].rearrange("p (t h d) -> p t h d", t=2, h=H), ACT.Copy).then_inc(s["vcopied"], 1)

            with act.Fori(0, NB) as b:
                evac(b, 0, XT)
                for i in range(8):
                    m, half = i // 2, i % 2
                    act.wait_ge(s["inproj"], b * 8 + i + 1)
                    if m < 2:
                        A_(XC[:, m, 2 + half * HALF:2 + (half + 1) * HALF], ring4[i % 4][0:CH, :], ACT.Copy).then_inc(s["inproj_out"], 1)
                    else:
                        A_(Z[:, m - 2, half * HALF:(half + 1) * HALF], ring4[i % 4][0:CH, :], ACT.Silu).then_inc(s["inproj_out"], 1)
                for c in range(2):
                    act.wait_ge(s["conv"], b * 2 + c + 1)
                    A_(XS[:, c, :], Y1[:, c, :], ACT.Silu).then_inc(s["silu"], 1)
                evac(b, 1, XT, 2, 3)
                act.wait_ge(s["logit"], b + 1)
                A_(sc1[:], PV[:, 0:T], ACT.Exp, scale=-1.0).then_inc(s["expz"], 1)
                cut(b, 0, spl, HALF, 2)
                act.wait_ge(s["srow_turned"], b + 1)
                A_(srow[:], ST[0][:, :], ACT.Copy).then_inc(s["srow_copied"], 1)
                vcopy(b, 0)
                act.wait_ge(s["gathersel"], b + 1)
                for c in range(2):
                    A_(NTS[0:CH, c, :], S[0][0:CH, c * 2 * QP:(c + 1) * 2 * QP], ACT.Identity, scale=cols[:, c, 2:3], bias=cols[:, c, 3:4]).then_inc(s["nts"], 1)
                cut(b, 4, spl0, 2 * QP, 1)

                def mcopy0(h):
                    act.wait_ge(s["mturned"], b * 24 + h + 1)
                    A_(QS0[KP:KP + 2, h, :], MT[KP:KP + 2, 0:2 * QP], ACT.Copy).then_inc(s["mcopied"], 1)

                mcopy0(0)
                act.wait_ge(s["kw0"], (b * 2 + 1) * 16)
                act.wait_ge(s["kw1"], (b * 2 + 1) * 16)
                for h in range(H):
                    for i in range(3):
                        n = 3 * h + i
                        w = (3 if i < 2 else 2) * 2 * QP
                        act.wait_ge(s["st0"], b * 36 + n + 1)
                        act.wait_ge(s["pv0"], b * H + h + 1)
                        A_(E0[:, h % 2, i * 6 * QP:i * 6 * QP + w], ring4[n % 4][:, 0:w], ACT.Exp, scale=float(DH) ** -0.5).then_inc(s["ex0"], 1)
                    if h + 1 < H:
                        mcopy0(h + 1)
                act.wait_ge(s["ctxt"], b + 1)
                A_(CXT[0:CH, :, :], ST[0][0:CH, 0:4 * QP].rearrange("p (c n) -> p c n", c=2), ACT.Copy).then_inc(s["ctxtc"], 1)
                act.wait_ge(s["att"], b + 1)
                A_(ATS[:, :, :], ST[1][0:QP, 0:2 * D].rearrange("p (q d) -> p q d", q=2), ACT.Copy).then_inc(s["atts"], 1)
                evac(b, 2, XT, 4, 5)
                for i in range(12):
                    act.wait_ge(s["hidden"], b * 12 + i + 1)
                    A_(hid[:, i % FC, (i // FC) * HALF:(i // FC + 1) * HALF], ring4[i % 4], ACT.Gelu).then_inc(s["gelu"], 1)
                evac(b, 3, XT)
                act.wait_ge(s["kw0"], (b * 2 + 1) * 16)
                act.wait_ge(s["kw1"], (b * 2 + 1) * 16)
                cut(b, 6, spl, HALF, 2)
                act.wait_ge(s["kw0"], (b * 2 + 2) * 16)
                act.wait_ge(s["kw1"], (b * 2 + 2) * 16)
                cut(b, 10, spl, HALF, 2)
                vcopy(b, 1)

                def mcopy(h):
                    act.wait_ge(s["mturned"], b * 24 + 12 + h + 1)
                    A_(QS[KP:KP + 4, h, :], MT[KP:KP + 4, :], ACT.Copy).then_inc(s["mcopied"], 1)

                mcopy(0)
                for i in range(9 * H):
                    h, kt = i // 9, i % 9
                    m = P if kt < T else MS
                    act.wait_ge(s["stile"], b * 108 + i + 1)
                    act.wait_ge(s["pv"], b * 108 + i + 1)
                    A_(E[0:m, i % 3, :], ST[i % 2][0:m, :], ACT.Exp).then_inc(s["exps"], 1)
                    if kt == 5 and h + 1 < H:
                        mcopy(h + 1)
                evac(b, 4, XT)
                evac(b, 5, BT)
                for i in range(4):
                    act.wait_ge(s["alpha"], b * 4 + i + 1)
                    if i >= 2:
                        act.wait_ge(s["fusedx"], b * 4 + i - 1)
                    A_(e2[:, i % 2, :, :], O[i % 2][:, 0:2 * D].rearrange("p (t d) -> p t d", t=2), ACT.Exp, scale=-1.0).then_inc(s["alphae"], 1)
                evac(b, 6, XT)
                for i in range(4):
                    half, c = i // 2, i % 2
                    act.wait_ge(s["qturned"], b * 4 + i + 1)
                    A_(XQT[:, c, half * HALF:(half + 1) * HALF], S[i % 2][0:CH, :].bitcast(BF16)[:, 0:HALF], ACT.Copy).then_inc(s["qcopied"], 1)
                for t in range(T):
                    act.wait_ge(s["bhid"], b * 8 + t + 1)
                    A_(HG[:, t, :], ST[t % 2][:, 0:F], ACT.Gelu, scale=gsc[:, t:t + 1]).then_inc(s["bgelu"], 1)
                    act.wait_ge(s["bgelu"], b * 8 + t + 1)
                    if t >= 1:
                        act.wait_ge(s["hss"], b * 8 + t)
                    A_(junk[:, 0:F], HG[:, t, :], ACT.Square, accum_out=ss[:, t:t + 1]).then_inc(s["hss"], 1)
                for t in range(T):
                    act.wait_ge(s["hturned"], b * 8 + t + 1)
                    A_(HQT[:, t % 2, :], S[t % 2][:, :].bitcast(BF16)[:, 0:F], ACT.Copy).then_inc(s["hcopied"], 1)
                act.wait_ge(s["outs"], b * 4 + 4)
                act.dma_start(ovw[b], HS[:, :, :]).then_inc(s["stored"], 16)
            act.wait_ge(s["stored"], NB * 16 + 16)

        @block.vector
        def _(ve):
            v = nc.vector
            k = [0]
            at = {"b": None, "base": 0}

            def link(ins):
                k[0] += 1
                ins.then_inc(s["vlink"], 1)
                if at["b"] is None:
                    ve.wait_ge(s["vlink"], k[0])
                else:
                    ve.wait_ge(s["vlink"], at["b"] * VEC_LINKS + at["base"] + k[0])

            v.memset(nmp[:], 0.0).then_inc(s["reduced"], 2)
            v.memset(nm[:], 0.0).then_inc(s["normed"], 1)
            v.memset(nms[:].rearrange("p a t c d -> p (a t c d)"), 0.0).then_inc(s["mcopied"], 1)
            v.memset(rec[:], 0.0).then_inc(s["ex0"], 4)
            v.memset(e2[:, 0, 0, 0:8], 0.0).then_inc(s["exps"], 2)
            v.memset(e2[:, 0, 0, 8:16], 0.0).then_inc(s["pv"], 3)
            v.memset(e2[:, 0, 0, 16:24], 0.0).then_inc(s["pv0"], 2)
            v.memset(CX[:, 0, 0:8], 0.0).then_inc(s["stored"], 16)
            ve.wait_ge(s["consts"], 15)
            ve.wait_ge(s["loaded"], LOADED)
            link(v.tensor_tensor(bmat[:], bmat[:], cmat[:], ALU.mult))
            link(v.tensor_reduce(cols[:, :, 6], bmat[:], AX.X, ALU.add))
            ve.wait_ge(s["hi"], 1)
            kmem = S[1][0:CH, 0:2 * P].rearrange("p (c n) -> p c n", c=2)[:, :, 0:MS]
            res = R1[:, 0, 0:2 * MSP].rearrange("p (c n) -> p c n", c=2)[:, :, 0:MS]
            v.tensor_tensor(res, kmem, splm[:, 0, :, 0:MS], ALU.subtract).then_inc(s["pd"], 1)
            ve.wait_ge(s["pa"], 3)
            v.tensor_tensor(splm[:, 2, :, 0:MS], res, splm[:, 1, :, 0:MS], ALU.subtract).then_inc(s["pd"], 1)
            w1, w2 = X[:, 0:FC, :], HG[0:CH, 0:2, :]
            v.tensor_reduce(wsum[:, 0:1], w1, AX.XY, ALU.add, apply_absolute_value=True)
            v.tensor_reduce(wsum[0:CH, 1:2], w2, AX.XY, ALU.add, apply_absolute_value=True).then_inc(s["pd"], 1)
            ve.wait_ge(s["pp"], 5)
            link(v.tensor_scalar(wsinv[:], PV[:, 0:2], 1.0 / (D * F), 1e-5, ALU.mult, ALU.max))
            link(v.reciprocal(wscale[:], wsinv[:]))
            for w, q, n, c in ((w1, XQ[:, 0:FC, :], P, 0), (w2, HQT[0:CH, :, :], CH, 1)):
                link(v.tensor_scalar(w, w, wscale[0:n, c:c + 1], MAGIC, ALU.mult, ALU.add))
                link(v.tensor_scalar(w, w, MAGIC, -1.0, ALU.subtract, ALU.max))
                v.tensor_scalar(q, w, 1.0, None, ALU.min).then_inc(s["pd"], 1)
            ve.wait_ge(s["pp"], 6)
            v.memset(XT[CH:CH + 1, 1, :], 1.0).then_inc(s["pa"], 1)
            at["base"] = k[0]
            k[0] = 0

            def stats(b, n, src):
                for t in range(T):
                    ins = v.bn_stats(st[:, t, :], src[:, t, :])
                link(ins)
                v.memset(rec[:, 0:1], 0.0)
                for t in range(T):
                    ins = v.bn_aggr(mv[:, t, :], st[:, t, :])
                ins.then_inc(s["stats"], 1)
                ve.wait_ge(s["rstd"], b * 5 + n + 1)

            def normalise(job, src, scale):
                for t in range(T):
                    ins = v.tensor_scalar(X[:, t, :], src[:, t, :], mv[:, t, 0:1], scale[:, t:t + 1], ALU.subtract, ALU.mult)
                    if t % 4 == 3:
                        ins.then_inc(s["xnorm"], 1)

            def cut(b, group, dst, width, spans):
                def low(i):
                    m, j = (i - group) // spans, (i - group) % spans
                    ve.wait_ge(s["mid"], b * 14 + i + 1)
                    v.tensor_tensor(dst[:, 2, m, j * width:(j + 1) * width], R1[:, i % 2, 0:width], dst[:, 1, m, j * width:(j + 1) * width],
                                    ALU.subtract).then_inc(s["lo"], 1)
                for i in range(group, group + 2 * spans):
                    m, j = (i - group) // spans, (i - group) % spans
                    ve.wait_ge(s["hi"], b * 14 + i + 2)
                    if i >= 2:
                        ve.wait_ge(s["lo"], b * 14 + i - 1)
                    v.tensor_tensor(R1[:, i % 2, 0:width], ring4[i % 4][0:CH, 0:width], dst[:, 0, m, j * width:(j + 1) * width],
                                    ALU.subtract).then_inc(s["resid"], 1)
                    if i > group:
                        low(i - 1)
                low(group + 2 * spans - 1)

            with ve.Fori(0, NB) as b:
                at["b"] = b
                ve.wait_ge(s["gathered"], b * 128 + 128)
                stats(b, 0, G)
                normalise(0, G, rn)
                for c in range(2):
                    ve.wait_ge(s["inproj_out"], b * 8 + 2 * c + 2)
                    if c == 0:
                        link(v.memset(XC[:, :, 0:2], 0.0))
                    link(v.tensor_scalar(Y1[:, c, :], XC[:, c, 2:L + 2], convw[:, c, 2:3], cols[:, c, 0:1], ALU.mult, ALU.add))
                    link(v.scalar_tensor_tensor(out=Y1[:, c, :], in0=XC[:, c, 1:L + 1], scalar=convw[:, c, 1:2], in1=Y1[:, c, :], op0=ALU.mult, op1=ALU.add))
                    v.scalar_tensor_tensor(out=Y1[:, c, :], in0=XC[:, c, 0:L], scalar=convw[:, c, 0:1], in1=Y1[:, c, :], op0=ALU.mult, op1=ALU.add).then_inc(s["conv"], 1)
                for c in range(2):
                    ve.wait_ge(s["silu"], b * 2 + c + 1)
                    v.tensor_scalar(Y1[:, c, :], XS[:, c, :], cols[:, c, 1:2], None, ALU.mult)
                    link(v.tensor_tensor_scan(CUM[:, c, :], XS[:, c, :], XS[:, c, :], 0.0, ALU.add, ALU.bypass))
                    link(v.scalar_tensor_tensor(out=CUM[:, c, :], in0=CUM[:, c, :], scalar=cols[:, c, 6:7], in1=Y1[:, c, :], op0=ALU.mult, op1=ALU.add))
                    if c == 0:
                        ve.wait_ge(s["inproj_out"], b * 8 + 8)
                    v.tensor_tensor(CUM[:, c, :], CUM[:, c, :], Z[:, c, :], ALU.mult).then_inc(s["gated"], 1)
                ve.wait_ge(s["stored"], b * 16 + 16)
                for i in range(4):
                    ve.wait_ge(s["outproj"], b * 4 + i + 1)
                    v.tensor_tensor(HS[:, 2 * i:2 * i + 2, :], O[i % 2][:, 0:2 * D].rearrange("p (t d) -> p t d", t=2), G[:, 2 * i:2 * i + 2, :], ALU.add).then_inc(s["h1"], 1)
                ve.wait_ge(s["h1"], b * 4 + 4)
                stats(b, 1, HS)
                normalise(1, HS, rnn)
                for t in range(T):
                    v.tensor_scalar(U[:, t, :], HS[:, t, :], mv[:, t, 0:1], rn[:, t:t + 1], ALU.subtract, ALU.mult)
                ve.wait_ge(s["expz"], b + 1)
                link(v.tensor_scalar(sc1[:], sc1[:], 1.0, None, ALU.add))
                v.reciprocal(sc[:], sc1[:]).then_inc(s["score"], 1)
                ve.wait_ge(s["score"], b + 1)
                cut(b, 0, spl, HALF, 2)
                ve.wait_ge(s["srow_copied"], b + 1)
                for t in range(T):
                    v.tensor_scalar(junk[:, 0:L - t * P], srow[:, t * P:L], sc[:, t:t + 1], 0.0, ALU.is_lt, ALU.add, accum_out=cnt[:, 0, t:t + 1])
                    if t > 0:
                        v.tensor_scalar(junk[:, L - t * P:L], srow[:, 0:t * P], sc[:, t:t + 1], 0.0, ALU.is_le, ALU.add, accum_out=cnt[:, 1, t:t + 1])
                    link(v.scalar_tensor_tensor(out=junk2[:], in0=srow[:, t * P:(t + 1) * P], scalar=sc[:, t:t + 1], in1=earlier[:], op0=ALU.is_equal, op1=ALU.mult,
                                                accum_out=cnt[:, 2, t:t + 1]))
                link(v.tensor_tensor(rank[:], cnt[:, 0, :], cnt[:, 1, :], ALU.add))
                v.tensor_tensor(rank[:], rank[:], cnt[:, 2, :], ALU.add).then_inc(s["picks"], 1)
                ve.wait_ge(s["picks"], b * 2 + 1)
                v.tensor_scalar(notsel[:], rank[:], float(NSEL), None, ALU.is_ge)
                for t in range(T):
                    ins = v.tensor_scalar(PSEL[:, t, :], slot[:].rearrange("p a n -> p (a n)"), rank[:, t:t + 1], None, ALU.is_equal)
                ins.then_inc(s["picks"], 1)
                ve.wait_ge(s["rank_turned"], b + 1)
                for q in range(2):
                    ins = v.tensor_scalar(PT[0:QC, q, :], ST[0][0:QC, :], rowslot[0:QC, q:q + 1], None, ALU.is_equal)
                ins.then_inc(s["pt"], 1)
                ve.wait_ge(s["pooled"], b + 1)
                link(v.tensor_scalar(pool3[:, 0:1], ST[1][0:CH, 2:3], 1e-6, None, ALU.add))
                link(v.reciprocal(pool3[:, 1:2], pool3[:, 0:1]))
                link(v.tensor_scalar(pool3[:, 2:5], ST[1][0:CH, 0:3], pool3[:, 1:2], None, ALU.mult))
                link(v.tensor_tensor(pool3[:, 5:7], pool3[:, 2:4], cols[:, :, 2], ALU.mult))
                for c in range(2):
                    link(v.scalar_tensor_tensor(out=pool3[:, 5 + c:6 + c], in0=cols[:, c, 3:4], scalar=pool3[:, 4:5], in1=pool3[:, 5 + c:6 + c], op0=ALU.mult, op1=ALU.add))
                cut(b, 4, spl0, 2 * QP, 1)
                ve.wait_ge(s["gathersel"], b + 1)
                for c in range(2):
                    v.scalar_tensor_tensor(out=XT[0:CH, c, :], in0=srow[0:CH, :], scalar=pool3[:, 5 + c:6 + c], in1=XT[0:CH, c, :], op0=ALU.mult, op1=ALU.add).then_inc(s["mixin"], 1)

                def chain(h, n, rows, tiles, kinds):
                    if n > 0:
                        ve.wait_ge(s["rowmax"], b * 24 + n)
                    link(v.tensor_reduce(nm[0:rows, 0:tiles, 0:1], nmp[0:rows, 0:tiles, :], AX.X, ALU.max, negate=True))
                    link(v.tensor_copy(nms[0:rows, h % 2, 0:tiles, 0:kinds, 0], nm[0:rows, 0:tiles, 0:kinds]))
                    v.tensor_tensor(nms[0:rows, h % 2, 0:tiles, 0:kinds, 1], nm[0:rows, 0:tiles, 0:kinds], nms[0:rows, h % 2, 0:tiles, 0:kinds, 0],
                                    ALU.subtract).then_inc(s["rowmax"], 1)

                for h in range(H):
                    for u in range(4):
                        n = 4 * h + u
                        ve.wait_ge(s["units"], b * 264 + n + 1)
                        v.tensor_reduce(nmp[0:QP, u // 2, u % 2:u % 2 + 1], S[n % 2][0:QP, :], AX.X, ALU.max).then_inc(s["reduced"], 1)
                    ve.wait_ge(s["reduced"], b * 264 + 4 * h + 6)
                    if h >= 2:
                        ve.wait_ge(s["mturned"], b * 24 + h - 1)
                    chain(h, h, QP, 2, 1)
                ve.wait_ge(s["pv0"], b * H + H + 2)
                ctxv = PV[0:QP, 0:2 * H * VW].rearrange("p (q h d) -> p q h d", q=2, h=H)
                for q in range(2):
                    link(v.reciprocal(rec[0:QP, 0:H], ctxv[:, q, :, DH]))
                    ins = v.tensor_tensor(CX[:, q, :].rearrange("p (h d) -> p h d", h=H), ctxv[:, q, :, 0:DH],
                                          rec[0:QP, 0:H].unsqueeze(2).to_broadcast([QP, H, DH]), ALU.mult)
                    if q == 0:
                        link(ins)
                ins.then_inc(s["ctxn"], 1)
                for t in range(T):
                    ve.wait_ge(s["mixed"], b * 8 + t + 1)
                    o = O[t % 2]
                    link(v.scalar_tensor_tensor(out=HP[:, t, :], in0=o[:, 0:D], scalar=notsel[:, t:t + 1], in1=U[:, t, :], op0=ALU.mult, op1=ALU.add))
                    v.tensor_tensor(HP[:, t, :], HP[:, t, :], o[:, D:2 * D], ALU.add).then_inc(s["merged"], 1)
                ve.wait_ge(s["merged"], b * 8 + 8)
                stats(b, 2, HP)
                normalise(2, HP, rn)
                link(v.tensor_tensor(HS[:], HS[:], HP[:], ALU.add))
                for i in range(4):
                    ve.wait_ge(s["ffn"], b * 4 + i + 1)
                    v.tensor_tensor(HS[:, 2 * i:2 * i + 2, :], O[i % 2][:, 0:2 * D].rearrange("p (t d) -> p t d", t=2), HS[:, 2 * i:2 * i + 2, :], ALU.add).then_inc(s["h2"], 1)
                ve.wait_ge(s["h2"], b * 4 + 4)
                stats(b, 3, HS)
                normalise(3, HS, rn)
                cut(b, 6, spl, HALF, 2)
                cut(b, 10, spl, HALF, 2)

                def unit(n):
                    h, u = n // 18, n % 18
                    ve.wait_ge(s["units"], b * 264 + 48 + n + 1)
                    if u < 16:
                        v.tensor_reduce(nmp[:, u // 2, u % 2:u % 2 + 1], S[n % 2][:, :], AX.X, ALU.max).then_inc(s["reduced"], 1)
                    else:
                        j = 4 * (u - 16)
                        if j == 0:
                            ve.wait_ge(s["rowmax"], b * 24 + H + h)
                        v.tensor_reduce(nm[:, j:j + 4, 1], S[n % 2][:, 0:4 * MSP].rearrange("p (t n) -> p t n", t=4)[:, :, 0:MS], AX.X, ALU.max,
                                        negate=True).then_inc(s["reduced"], 1)

                def norm(h):
                    ve.wait_ge(s["pv"], b * 108 + 9 * h + 9 + 3)
                    pvv = PV[:, 0:2 * T * VW].rearrange("p (t d) -> p t d", d=VW)
                    ve.wait_ge(s["normed"], b * 12 + h + 1)
                    link(v.reciprocal(rec[:], pvv[:, :, DH]))
                    for dst, j in ((U, 0), (HP, T)):
                        ins = v.tensor_tensor(dst[:, :, h * DH:(h + 1) * DH], pvv[:, j:j + T, 0:DH],
                                              rec[:, j:j + T].unsqueeze(2).to_broadcast([P, T, DH]), ALU.mult)
                    ins.then_inc(s["normed"], 1)

                for h in range(H):
                    for u in range(18):
                        unit(18 * h + u)
                        if u == 2 and h >= 3:
                            norm(h - 3)
                    ve.wait_ge(s["reduced"], b * 264 + 48 + 18 * h + 18 + 2)
                    if h >= 2:
                        ve.wait_ge(s["mturned"], b * 24 + 12 + h - 1)
                    else:
                        ve.wait_ge(s["mturned"], b * 24 + 12)
                    chain(h, H + h, P, T, 2)
                for h in range(H - 3, H):
                    norm(h)
                ve.wait_ge(s["normed"], b * 12 + 13)
                for i in range(4):
                    ve.wait_ge(s["alphae"], b * 4 + i + 1)
                    e = e2[:, i % 2, :, :]
                    a, a1, x = U[:, 2 * i:2 * i + 2, :], HP[:, 2 * i:2 * i + 2, :], X[:, 2 * i:2 * i + 2, :]
                    v.tensor_scalar(e, e, 1.0, None, ALU.add)
                    link(v.tensor_tensor(a, a, a1, ALU.subtract))
                    link(v.reciprocal(e, e))
                    link(v.tensor_tensor(a, a, e, ALU.mult))
                    v.tensor_tensor(x, a, a1, ALU.add).then_inc(s["fusedx"], 1)
                for i in range(4):
                    ve.wait_ge(s["fproj"], b * 4 + i + 1)
                    v.tensor_tensor(HS[:, 2 * i:2 * i + 2, :], O[i % 2][:, 0:2 * D].rearrange("p (t d) -> p t d", t=2), HS[:, 2 * i:2 * i + 2, :], ALU.add).then_inc(s["h3"], 1)
                ve.wait_ge(s["h3"], b * 4 + 4)
                stats(b, 4, HS)
                for t in range(T):
                    ins = v.tensor_scalar(X[:, t, :], HS[:, t, :], mv[:, t, 0:1], rnn[:, t:t + 1], ALU.subtract, ALU.mult)
                link(ins)
                link(v.tensor_tensor(X[:], X[:], g1bc[:].unsqueeze(1).to_broadcast([P, T, D]), ALU.mult))
                link(v.tensor_reduce(amax[:], X[:], AX.X, ALU.max, apply_absolute_value=True))
                link(v.tensor_scalar(qinv[:], amax[:], 1e-5, 1.0 / 127.0, ALU.max, ALU.mult))
                v.tensor_scalar(gsc[:], qinv[:], wsinv[:, 0:1], None, ALU.mult)
                link(v.reciprocal(qsc[:], qinv[:]))
                for t in range(T):
                    link(v.tensor_scalar(X[:, t, :], X[:, t, :], qsc[:, t:t + 1], MAGIC, ALU.mult, ALU.add))
                    v.tensor_scalar(XQ[:, t, :], X[:, t, :], MAGIC, None, ALU.subtract).then_inc(s["quant"], 1)
                for t in range(T):
                    ve.wait_ge(s["hss"], b * 8 + t + 1)
                    link(v.tensor_tensor(HG[:, t, :], HG[:, t, :], g2bc[:], ALU.mult))
                    link(v.tensor_reduce(amax[:, t:t + 1], HG[:, t, :], AX.X, ALU.max, apply_absolute_value=True))
                ve.wait_ge(s["hrms"], b + 1)
                link(v.tensor_tensor(amax[:], amax[:], rn[:], ALU.mult))
                link(v.tensor_scalar(qinv[:], amax[:], 1e-5, 1.0 / 127.0, ALU.max, ALU.mult))
                link(v.reciprocal(qsc[:], qinv[:]))
                link(v.tensor_tensor(qsc[:], qsc[:], rn[:], ALU.mult))
                link(v.tensor_scalar(gsc[:], qinv[:], wsinv[:, 1:2], None, ALU.mult))

                def store(i):
                    ve.wait_ge(s["bout"], b * 8 + 2 * i + 2)
                    for t in (2 * i, 2 * i + 1):
                        ins = v.scalar_tensor_tensor(out=HS[:, t, :], in0=O[i % 2][:, (t % 2) * D:(t % 2 + 1) * D], scalar=gsc[:, t:t + 1], in1=HS[:, t, :],
                                                     op0=ALU.mult, op1=ALU.add)
                    ins.then_inc(s["outs"], 1)

                for t in range(T):
                    link(v.tensor_scalar(HG[:, t, :], HG[:, t, :], qsc[:, t:t + 1], MAGIC, ALU.mult, ALU.add))
                    if t >= 2:
                        ve.wait_ge(s["hturned"], b * 8 + t - 1)
                    v.tensor_scalar(HQ[:, (t % 2) * F:(t % 2 + 1) * F], HG[:, t, :], MAGIC, None, ALU.subtract).then_inc(s["hquant"], 1)
                    if t % 2 == 1 and t >= 3:
                        store(t // 2 - 1)
                store(3)
            assert k[0] == VEC_LINKS, k[0]


_INS = ['x', 'L0_tok_embed_matrix', 'L0_attn_W_in', 'L0_attn_conv_w', 'L0_attn_conv_b', 'L0_attn_B', 'L0_attn_C', 'L0_attn_D',
        'L0_attn_W_out', 'L0_ffn_g1', 'L0_ffn_b1', 'L0_ffn_g2', 'L0_ffn_b2', 'L0_ffn_Wr', 'L0_ffn_br', 'L0_ffn_Wq', 'L0_ffn_bq',
        'L0_ffn_Wk', 'L0_ffn_bk', 'L0_ffn_Wv', 'L0_ffn_bv', 'L0_ffn_Wo', 'L0_ffn_bo', 'L0_ffn_Wm', 'L0_ffn_bm', 'L0_ffn_W1',
        'L0_ffn_bf1', 'L0_ffn_W2', 'L0_ffn_bf2', 'L1_attn_w_attn', 'L1_attn_b_attn', 'L1_attn_w_proj', 'L1_attn_b_proj',
        'L1_attn_w_mem', 'L1_attn_b_mem', 'L1_attn_w_alpha', 'L1_attn_b_alpha', 'L1_attn_memory_features', 'L1_ffn_w1',
        'L1_ffn_g1', 'L1_ffn_w2', 'L1_ffn_g2']


def kernel(**inputs):
    import numpy as _np
    import concourse.bacc as _bacc
    from concourse import mybir as _mybir
    from concourse.bass_utils import run_bass_kernel_spmd as _run

    nc = _bacc.Bacc("TRN2", target_bir_lowering=False, num_devices=1)
    arrays, aps = {}, {}
    for name in _INS:
        a = _np.ascontiguousarray(inputs[name])
        arrays[f"in_{name}_dram"] = a
        aps[name] = nc.dram_tensor(f"in_{name}_dram", a.shape, _mybir.dt.from_np(a.dtype), kind="ExternalInput").ap()
    out = nc.dram_tensor("out_0_dram", (NB, L, D), _mybir.dt.float32, kind="ExternalOutput").ap()
    build(nc, aps, out)
    r = _run(nc, [arrays], core_ids=[0])
    return r.results[0]["out_0_dram"]
```

```python
from contextlib import ExitStack

import concourse.bass as bass
from concourse import mybir

F32 = mybir.dt.float32
BF16 = mybir.dt.bfloat16
I32 = mybir.dt.int32
ALU = mybir.AluOpType
ACT = mybir.ActivationFunctionType
AX = mybir.AxisListType

P = 128
D = 192
CH = 96
NB = 4
L = 1024
T = L // P
HALF = 512
H = 12
DH = D // H
VW = 32
F = 768
FC = F // P
MS = 100
MSP = 104
NSEL = max(1, int(round(0.15 * L)))
QC = NSEL // 2
QP = 80
MAGIC = 12582912.0
LN_EPS = 1e-5
RMS_EPS = 1e-6
Q_PARTS = (0, 0, 1, 0, 2, 1)
K_PARTS = (0, 1, 0, 2, 0, 1)
KP = 6 * DH
NH = 2
STEPS = 5
NSTEP = H * NH * STEPS
SCORE_UNITS = 18
UNITS0 = 4 * H
VEC_LINKS = 170


def plan_units():
    first = [("max", h, u) for h in range(2) for u in range(SCORE_UNITS)]
    steps = []
    for i in range(NSTEP):
        h, j = i // 10, i % 10
        units = []
        if h + 2 < H and j < 9:
            units += [("max", h + 2, 2 * j), ("max", h + 2, 2 * j + 1)]
        if j == 7:
            units.append(("ctx", h, 0))
        if j == 2 and h > 0:
            units.append(("ctx", h - 1, 1))
        steps.append(units)
    return first, steps, [("ctx", H - 1, 1)]


FIRST_UNITS, STEP_UNITS, LAST_UNITS = plan_units()
ALL_UNITS = FIRST_UNITS + sum(STEP_UNITS, []) + LAST_UNITS
NUNITS = UNITS0 + len(ALL_UNITS)
UNIT_AT = {u: UNITS0 + n for n, u in enumerate(ALL_UNITS)}


def build(nc, A, out):
    ctx = ExitStack()
    with ctx:
        def sb(name, shape, dt=F32):
            return ctx.enter_context(nc.sbuf_tensor(name, shape, dt))

        def pb(name, shape, dt=F32):
            return ctx.enter_context(nc.psum_tensor(name, shape, dt))

        def sem(name):
            return ctx.enter_context(nc.semaphore(name))

        ident = sb("ident", [P, P])
        identb = sb("identb", [P, P], BF16)
        earlier = sb("earlier", [P, P])
        ones = sb("ones", [P, P])
        neghalf = sb("neghalf", [P, T])
        slot_i = sb("slot_i", [P, 2, QP], I32)
        slot = sb("slot", [P, 2, QP])
        rowslot_i = sb("rowslot_i", [P, 2], I32)
        rowslot = sb("rowslot", [P, 2])
        tok_i = sb("tok_i", [P, NB * T], I32)
        win = sb("win", [CH, 2, 2 * D])
        wout = sb("wout", [CH, 2, D])
        convw = sb("convw", [CH, 2, 3])
        cols = sb("cols", [CH, 2, 8])
        bmat = sb("bmat", [CH, 2, 8])
        cmat = sb("cmat", [CH, 2, 8])
        wr = sb("wr", [CH + 1, 2, 1])
        wq = sb("wq", [CH + 1, 2, D])
        wk = sb("wk", [CH + 1, 2, D])
        wv = sb("wv", [CH + 1, 2, D])
        wo = sb("wo", [CH + 1, 2, D])
        wm = sb("wm", [CH + 1, 2, D])
        wf1 = sb("wf1", [CH + 1, 2, F])
        wf2 = sb("wf2", [P, FC, D])
        bf2 = sb("bf2", [1, D])
        wat = sb("wat", [CH + 1, 2, 3 * D])
        wal = sb("wal", [CH + 1, 4, D])
        wpr = sb("wpr", [CH + 1, 2, D])
        g1bc = sb("g1bc", [P, D])
        g2bc = sb("g2bc", [P, F])
        wb1 = sb("wb1", [CH, 2, F], BF16)
        wb2 = sb("wb2", [P, FC, D], BF16)
        wscale = sb("wscale", [P, 2])
        wsinv = sb("wsinv", [P, 2])
        ksm = sb("ksm", [KP + 4, H, MSP], BF16)
        vm = sb("vm", [MS, H, VW])

        G = sb("G", [P, T, D])
        X = sb("X", [P, T, D])
        U = sb("U", [P, T, D])
        HP = sb("HP", [P, T, D])
        HS = sb("HS", [P, T, D])
        st = sb("st", [P, T, 6])
        mv = sb("mv", [P, T, 2])
        rn = sb("rn", [P, T])
        rnn = sb("rnn", [P, T])
        tp = sb("tp", [P, T])
        V = sb("V", [P, T, H, VW])
        XT = sb("XT", [CH + 1, 2, L])
        big = sb("big", [P, T * F + 4])
        XC = big[0:CH, 0:2 * (L + 2)].rearrange("p (c n) -> p c n", c=2)
        XS = big[0:CH, 2052:2052 + 2 * L].rearrange("p (c n) -> p c n", c=2)
        CUM = big[0:CH, 4100:4100 + 2 * L].rearrange("p (c n) -> p c n", c=2)
        hid = big[:, 0:FC * L].rearrange("p (f n) -> p f n", f=FC)
        BT = big[0:CH, 0:2 * L].rearrange("p (c n) -> p c n", c=2)
        HG = big[:, 0:T * F].rearrange("p (t f) -> p t f", t=T)
        rawq = sb("rawq", [P, H * L // 2])
        QS = rawq[0:KP + 4, :].bitcast(BF16).rearrange("p (h n) -> p h n", h=H)
        Y1 = rawq[0:CH, 0:2 * L].rearrange("p (c n) -> p c n", c=2)
        Z = rawq[0:CH, 2 * L:4 * L].rearrange("p (c n) -> p c n", c=2)
        PSEL = rawq[:, 4 * L:4 * L + T * 2 * QP].rearrange("p (t n) -> p t n", t=T)
        KS = sb("KS", [KP + 4, H, L], BF16)
        QS0 = sb("QS0", [KP + 4, H, 2 * QP], BF16)
        spl0 = sb("spl0", [CH, 3, 2, 2 * QP], BF16)
        acc_out = sb("acc_out", [P, 2, HALF])
        acc0 = acc_out[:, 0, 0:3 * 2 * QP]
        R1 = acc_out[0:CH, :, :]
        E = sb("E", [P, 3, L])
        spl = E[0:CH, :, :].rearrange("p a n -> p (a n)").bitcast(BF16).rearrange("p (a c n) -> p a c n", a=3, c=2)
        E0 = E[:, :, :].rearrange("p a n -> p (a n)")[:, 0:2 * T * 2 * QP].rearrange("p (a n) -> p a n", a=2)
        srow = sb("srow", [P, L])
        PT = rawq[:, 0:2 * L].rearrange("p (q n) -> p q n", q=2)
        XQ = rawq[:, 0:768].bitcast(BF16).rearrange("p (t d) -> p t d", t=T)
        XQT = rawq[0:CH, 768:1792].bitcast(BF16).rearrange("p (c n) -> p c n", c=2)
        HQ = rawq[:, 2560:3328].bitcast(BF16)
        HQT = rawq[:, 1792:2560].bitcast(BF16).rearrange("p (t f) -> p t f", t=2)
        NTS = sb("NTS", [CH + 1, 2, 2 * QP])
        CX = sb("CX", [QP, 2, D])
        CXT = sb("CXT", [CH + 1, 2, 2 * QP])
        ATS = sb("ATS", [QP, 2, D])
        sc = sb("sc", [P, T])
        sc1 = sb("sc1", [P, T])
        cnt = sb("cnt", [P, 3, T])
        rank = sb("rank", [P, T])
        notsel = sb("notsel", [P, T])
        junk = sb("junk", [P, L])
        junk2 = sb("junk2", [P, P])
        pool3 = sb("pool3", [CH, 8])
        nmp = sb("nmp", [P, T, 2])
        nm = sb("nm", [P, T, 2])
        nms = sb("nms", [P, 2, T, 2, 2], BF16)
        rec = sb("rec", [P, 2 * T])
        e2 = rawq[:, 3328:3328 + 4 * D].rearrange("p (i t d) -> p i t d", i=2, t=2)
        amax = sb("amax", [P, T])
        qsc = sb("qsc", [P, T])
        qinv = sb("qinv", [P, T])
        gsc = sb("gsc", [P, T])
        ss = sb("ss", [P, T])
        wsum = sb("wsum", [P, 2])
        memt = junk[0:CH + 1, 0:2 * MS].rearrange("p (c n) -> p c n", c=2)
        memn = junk[0:MS, 2 * P:2 * P + D]
        splm = srow[0:CH, 0:3 * MSP].bitcast(BF16).rearrange("p (a c n) -> p a c n", a=3, c=2)

        ST = [pb("ST0", [P, 2 * HALF]), pb("ST1", [P, 2 * HALF])]
        S = [pb("S0", [P, HALF]), pb("S1", [P, HALF])]
        PV = pb("PV", [P, HALF])
        MT = pb("MT", [P, 2 * HALF], BF16)
        MTf = MT[:, :].bitcast(F32)
        ring4 = [ST[0][:, 0:HALF], ST[0][:, HALF:2 * HALF], ST[1][:, 0:HALF], ST[1][:, HALF:2 * HALF]]
        O = [PV[:, :], MTf]

        scr_k = nc.dram_tensor("scr_k", (3, D, L), BF16, kind="Internal").ap()
        scr_q = nc.dram_tensor("scr_q", (3, D, L), BF16, kind="Internal").ap()
        scr_q0 = nc.dram_tensor("scr_q0", (3, D, 2 * QP), BF16, kind="Internal").ap()
        scr_m = nc.dram_tensor("scr_m", (3, D, MSP), BF16, kind="Internal").ap()

        names = """loaded consts tokens gathered stats rstd xnorm turned evac inproj inproj_out conv silu
            gated outproj h1 logit expz score srow_turned srow_copied picks rank_turned pt gathersel nts
            proj hi resid mid lo vproj vcopied units reduced rowmax mturned mcopied acc0 ctxr accout st0 ex0 pv0 ctx ctxn
            ctxt ctxtc att atts pooled pooledv mixin mixed merged hidden gelu ffn h2 stile exps pv normed
            alpha alphae fusedx fproj h3 quant qturned qcopied bhid bgelu hss hrms hquant hturned hcopied
            bout outs stored vlink plink xpose pp pa pd kw0 kw1 kr0 kr1 qw0 qw1 qr0 qr1 q0w q0r mw mr""".split()
        s = {n: sem("s_" + n) for n in names}
        block = ctx.enter_context(nc.Block())

        ovw = out.rearrange("b (t p) d -> b p t d", p=P)

        def cm(w, p=CH):
            return w.rearrange("(c p) n -> p c n", p=p)

        def stack(scr, c, part):
            return scr[part, c * CH:(c + 1) * CH, :].rearrange("(h p) n -> p h n", p=DH)

        loads = []

        @block.sync
        def _(sp):
            n = [0]

            def load(dst, src):
                sp.dma_start(dst, src, allow_slow_non_contiguous=True).then_inc(s["loaded"], 16)
                n[0] += 1

            load(win[:], cm(A["L0_attn_W_in"]))
            load(wout[:], cm(A["L0_attn_W_out"]))
            load(convw[:], A["L0_attn_conv_w"].rearrange("(c p) a k -> p c (a k)", p=CH))
            for i, name in enumerate(["L0_attn_conv_b", "L0_attn_D", "L0_ffn_g1", "L0_ffn_b1", "L0_ffn_g2", "L0_ffn_b2"]):
                load(cols[:, :, i], A[name].rearrange("(c p) -> p c", p=CH))
            load(bmat[:], cm(A["L0_attn_B"]))
            load(cmat[:], cm(A["L0_attn_C"]))
            load(wr[0:CH, :, 0], A["L0_ffn_Wr"].rearrange("(c p) -> p c", p=CH))
            load(wr[CH:CH + 1, 1, :], A["L0_ffn_br"].rearrange("(a n) -> a n", a=1))
            for w, wn, bn in ((wq, "L0_ffn_Wq", "L0_ffn_bq"), (wk, "L0_ffn_Wk", "L0_ffn_bk"), (wv, "L0_ffn_Wv", "L0_ffn_bv"),
                              (wo, "L0_ffn_Wo", "L0_ffn_bo"), (wm, "L0_ffn_Wm", "L0_ffn_bm"), (wf1, "L0_ffn_W1", "L0_ffn_bf1"),
                              (wat, "L1_attn_w_attn", "L1_attn_b_attn"), (wal, "L1_attn_w_alpha", "L1_attn_b_alpha"),
                              (wpr, "L1_attn_w_proj", "L1_attn_b_proj")):
                load(w[0:CH, :, :], cm(A[wn]))
                load(w[CH:CH + 1, 1, :], A[bn].rearrange("(a n) -> a n", a=1))
            load(wf2[:], cm(A["L0_ffn_W2"], P))
            load(bf2[:], A["L0_ffn_bf2"].rearrange("(a n) -> a n", a=1))
            load(g1bc[:], A["L1_ffn_g1"].partition_broadcast(P))
            load(g2bc[:], A["L1_ffn_g2"].partition_broadcast(P))
            load(memn, A["L1_attn_memory_features"][0])
            load(XT[0:CH, :, 0:2 * D], cm(A["L1_attn_w_mem"]))
            load(XT[CH:CH + 1, 1, 0:2 * D], A["L1_attn_b_mem"].rearrange("(a n) -> a n", a=1))
            load(X[:, 0:FC, :], cm(A["L1_ffn_w1"], P))
            load(HG[0:CH, 0:2, :], cm(A["L1_ffn_w2"]))
            loads.append(n[0])

            sp.wait_ge(s["pd"], 2)
            for c in range(2):
                sp.dma_start(scr_m[:, c * CH:(c + 1) * CH, :].rearrange("a r n -> r a n"), splm[:, :, c, :]).then_inc(s["mw"], 16)
            sp.wait_ge(s["mw"], 32)
            for c in range(2):
                for j in range(6):
                    sp.dma_start(ksm[DH * j:DH * j + DH, 6 * c:6 * c + 6, :], stack(scr_m, c, K_PARTS[j])).then_inc(s["mr"], 16)

            def restack(b, src, scr, dst, parts, group, kw, kr, uses, use):
                for c in range(2):
                    sp.wait_ge(s["lo"], b * 14 + group + 2 * c + 2)
                    sp.dma_start(scr[:, c * CH:(c + 1) * CH, :].rearrange("a r n -> r a n"), src[:, :, c, :]).then_inc(s[kw[c]], 16)
                for c in range(2):
                    sp.wait_ge(s[kw[c]], (b * uses + use + 1) * 16)
                    for j in range(6):
                        sp.dma_start(dst[DH * j:DH * j + DH, 6 * c:6 * c + 6, :], stack(scr, c, parts[j])).then_inc(s[kr[c]], 16)

            with sp.Fori(0, NB) as b:
                restack(b, spl, scr_k, KS, K_PARTS, 0, ("kw0", "kw1"), ("kr0", "kr1"), 2, 0)
                sp.wait_ge(s["lo"], b * 14 + 6)
                for c in range(2):
                    sp.dma_start(scr_q0[:, c * CH:(c + 1) * CH, :].rearrange("a r n -> r a n"), spl0[:, :, c, :]).then_inc(s["q0w"], 16)
                sp.wait_ge(s["q0w"], b * 32 + 32)
                for c in range(2):
                    for j in range(6):
                        sp.dma_start(QS0[DH * j:DH * j + DH, 6 * c:6 * c + 6, :], stack(scr_q0, c, Q_PARTS[j])).then_inc(s["q0r"], 16)
                restack(b, spl, scr_k, KS, K_PARTS, 6, ("kw0", "kw1"), ("kr0", "kr1"), 2, 1)
                restack(b, spl, scr_q, QS, Q_PARTS, 10, ("qw0", "qw1"), ("qr0", "qr1"), 1, 0)

        LOADED = loads[0] * 16

        @block.gpsimd
        def _(g):
            k = [0]

            def link(ins):
                k[0] += 1
                ins.then_inc(s["plink"], 1)
                g.wait_ge(s["plink"], k[0])

            made = [0]

            def const(ins):
                made[0] += 1
                ins.then_inc(s["consts"], 1)
                g.wait_ge(s["consts"], made[0])

            link(g.memset(ident[:], 0.0))
            link(g.affine_select(out=ident[:], in_=ident[:], compare_op=ALU.not_equal, fill=1.0, base=0, pattern=[[-1, P]], channel_multiplier=1))
            const(g.tensor_copy(identb[:], ident[:]))
            link(g.memset(earlier[:], 1.0))
            const(g.affine_select(out=earlier[:], in_=earlier[:], compare_op=ALU.is_gt, fill=0.0, base=0, pattern=[[-1, P]], channel_multiplier=1))
            const(g.memset(ones[:], 1.0))
            const(g.memset(neghalf[:], -0.5))
            link(g.iota(slot_i[:], pattern=[[QC, 2], [1, QP]], base=0, channel_multiplier=0))
            const(g.tensor_copy(slot[:], slot_i[:]))
            link(g.iota(rowslot_i[:], pattern=[[QC, 2]], base=0, channel_multiplier=1))
            const(g.tensor_copy(rowslot[:], rowslot_i[:]))
            link(g.memset(V[:], 0.0))
            const(g.memset(V[:, :, :, DH:DH + 1], 1.0))
            link(g.memset(vm[:], 0.0))
            const(g.memset(vm[:, :, DH:DH + 1], 1.0))
            const(g.memset(NTS[CH:CH + 1, :, :], 1.0))
            const(g.memset(CXT[CH:CH + 1, :, :], 1.0))
            const(g.memset(junk[CH:CH + 1, 0:2 * MS], 1.0))
            const(g.memset(srow[:], 0.0))
            link(g.memset(KS[KP:KP + 4, :, :], 0.0))
            const(g.memset(KS[KP:KP + 2, :, :], 1.0))
            link(g.memset(ksm[KP:KP + 4, :, :], 1.0))
            const(g.memset(ksm[KP:KP + 2, :, :], 0.0))
            link(g.memset(QS0[KP:KP + 4, :, :], 0.0))
            const(g.memset(cnt[:], 0.0))
            g.dma_start(tok_i[:], A["x"].rearrange("b (t p) -> p (b t)", p=P), allow_slow_non_contiguous=True).then_inc(s["tokens"], 16)

            def rsqrt(dst, src, eps):
                link(g.tensor_scalar(tp[:], src, eps, None, ALU.add))
                return g.tensor_tensor(dst, tp[:], neghalf[:], ALU.pow)

            def inverse_deviation(b, n, second=None):
                g.wait_ge(s["stats"], b * 5 + n + 1)
                ins = rsqrt(rn[:], mv[:, :, 1], LN_EPS)
                if second is None:
                    ins.then_inc(s["rstd"], 1)
                    return
                link(ins)
                link(g.tensor_tensor(tp[:], mv[:, :, 1], rn[:], ALU.mult))
                link(g.tensor_tensor(rnn[:], tp[:], rn[:], ALU.mult))
                link(rsqrt(rnn[:], rnn[:], second))
                g.tensor_tensor(rnn[:], rnn[:], rn[:], ALU.mult).then_inc(s["rstd"], 1)

            for b in range(NB):
                if b == 0:
                    g.wait_ge(s["tokens"], 16)
                else:
                    g.wait_ge(s["h1"], b * 4)
                for t in range(T):
                    g.indirect_dma_start(G[:, t, :], None, A["L0_tok_embed_matrix"][:],
                                         bass.IndirectOffsetOnAxis(ap=tok_i[:, b * T + t:b * T + t + 1], axis=0)).then_inc(s["gathered"], 16)
                inverse_deviation(b, 0)
                inverse_deviation(b, 1, LN_EPS)
                inverse_deviation(b, 2)
                inverse_deviation(b, 3)
                inverse_deviation(b, 4, RMS_EPS)
                g.wait_ge(s["hss"], b * 8 + 8)
                link(g.tensor_scalar(tp[:], ss[:], 1.0 / F, None, ALU.mult))
                rsqrt(rn[:], tp[:], RMS_EPS).then_inc(s["hrms"], 1)

        @block.tensor
        def _(pe):
            pe.wait_ge(s["consts"], 15)
            pe.wait_ge(s["loaded"], LOADED)
            for c in range(2):
                nc.tensor.transpose(S[0][0:CH, c * P:c * P + MS], memn[:, c * CH:(c + 1) * CH], ident[0:MS, 0:MS]).then_inc(s["pp"], 1)
            pe.wait_ge(s["pa"], 1)
            for m in range(2):
                for c in range(2):
                    r = CH + c
                    ins = nc.tensor.matmul(S[1][0:CH, m * P:m * P + MS], XT[0:r, c, m * CH:(m + 1) * CH], memt[0:r, c, :], start=c == 0, stop=c == 1)
            ins.then_inc(s["pp"], 1)
            for c in range(2):
                ins = nc.tensor.matmul(ST[0][0:MS, 0:D], memt[0:CH + c, c, :], XT[0:CH + c, c, D:2 * D], start=c == 0, stop=c == 1)
            ins.then_inc(s["pp"], 1)
            pe.wait_ge(s["pd"], 3)
            nc.tensor.matmul(PV[:, 0:1], ones[:], wsum[:, 0:1], start=True, stop=True)
            nc.tensor.matmul(PV[:, 1:2], ones[0:CH, :], wsum[0:CH, 1:2], start=True, stop=True).then_inc(s["pp"], 1)
            pe.wait_ge(s["pd"], 5)
            t1 = ST[1][:, 0:HALF].bitcast(BF16)
            t2 = ST[1][:, HALF:2 * HALF].bitcast(BF16)
            t3 = [ST[0][:, 0:HALF].bitcast(BF16), ST[0][:, HALF:2 * HALF].bitcast(BF16)]
            pe.wait_ge(s["pa"], 3)
            for f in range(FC):
                for c in range(2):
                    nc.tensor.transpose((t1, t2)[c][0:CH, f * P:(f + 1) * P], XQ[:, f, c * CH:(c + 1) * CH], identb[:])
            for f in range(FC):
                for c in range(2):
                    ins = nc.tensor.transpose(t3[f // 3][:, (f % 3) * D + c * CH:(f % 3) * D + (c + 1) * CH], HQT[0:CH, c, f * P:(f + 1) * P], identb[0:CH, 0:CH])
            ins.then_inc(s["pp"], 1)
            pe.wait_ge(s["pa"], 4)

            def turn(b, job, src, ready, counts):
                for i in range(4):
                    half, c = i // 2, i % 2
                    if c == 0:
                        pe.wait_ge(s[ready], b * counts[0] + counts[1 + half])
                    pe.wait_ge(s["evac"], b * 28 + 4 * job + i + 1)
                    for t in range(4):
                        ins = nc.tensor.transpose(S[i % 2][0:CH, t * P:(t + 1) * P], src[:, 4 * half + t, c * CH:(c + 1) * CH], ident[:])
                    ins.then_inc(s["turned"], 1)

            def rows(dst, lhs, w, cs, bias):
                n = len(cs)
                for i, (x, wt, c) in enumerate(cs):
                    r = CH + (1 if bias and c == 1 else 0)
                    ins = nc.tensor.matmul(dst, x[0:r], wt[0:r], start=i == 0, stop=i == n - 1)
                return ins

            def project(b, group, w, off, src, width, spans):
                i = group
                for m in range(2):
                    for j in range(spans):
                        if i >= 4:
                            pe.wait_ge(s["resid"], b * 14 + i - 3)
                        for c in range(2):
                            r = CH + c
                            ins = nc.tensor.matmul(ring4[i % 4][0:CH, 0:width], w[0:r, c, off + m * CH:off + (m + 1) * CH],
                                                   src[0:r, c, j * width:(j + 1) * width], start=c == 0, stop=c == 1)
                        ins.then_inc(s["proj"], 1)
                        i += 1

            def values(b, use, w, off):
                for i in range(4):
                    n = 4 * use + i
                    if i >= 2:
                        pe.wait_ge(s["vcopied"], b * 8 + n - 1)
                    for t in (2 * i, 2 * i + 1):
                        for c in range(2):
                            r = CH + c
                            ins = nc.tensor.matmul(O[i % 2][:, (t % 2) * D:(t % 2 + 1) * D], XT[0:r, c, t * P:(t + 1) * P],
                                                   w[0:r, c, off:off + D], start=c == 0, stop=c == 1)
                    ins.then_inc(s["vproj"], 1)

            with pe.Fori(0, NB) as b:
                turn(b, 0, X, "xnorm", (8, 1, 2))
                pe.wait_ge(s["evac"], b * 28 + 4 + 2)
                for i in range(8):
                    m, half = i // 2, i % 2
                    if i >= 4:
                        pe.wait_ge(s["inproj_out"], b * 8 + i - 3)
                    for c in range(2):
                        ins = nc.tensor.matmul(ring4[i % 4][0:CH, :], win[:, c, m * CH:(m + 1) * CH], XT[0:CH, c, half * HALF:(half + 1) * HALF],
                                               start=c == 0, stop=c == 1)
                    ins.then_inc(s["inproj"], 1)
                pe.wait_ge(s["gated"], b * 2 + 2)
                for i in range(4):
                    if i >= 2:
                        pe.wait_ge(s["h1"], b * 4 + i - 1)
                    for t in (2 * i, 2 * i + 1):
                        for c in range(2):
                            ins = nc.tensor.matmul(O[i % 2][:, (t % 2) * D:(t % 2 + 1) * D], CUM[:, c, t * P:(t + 1) * P], wout[:, c, :],
                                                   start=c == 0, stop=c == 1)
                    ins.then_inc(s["outproj"], 1)
                turn(b, 1, X, "xnorm", (8, 3, 4))
                pe.wait_ge(s["evac"], b * 28 + 8 + 2)
                for t in range(T):
                    for c in range(2):
                        r = CH + c
                        ins = nc.tensor.matmul(PV[:, t:t + 1], XT[0:r, c, t * P:(t + 1) * P], wr[0:r, c, :], start=c == 0, stop=c == 1)
                ins.then_inc(s["logit"], 1)
                project(b, 0, wk, 0, XT, HALF, 2)
                pe.wait_ge(s["score"], b * 1 + 1)
                for t in range(T):
                    if t == 0:
                        pe.wait_ge(s["resid"], b * 14 + 4)
                    ins = nc.tensor.transpose(ST[0][:, t * P:(t + 1) * P], sc[:, t:t + 1].to_broadcast([P, P]), ident[:])
                ins.then_inc(s["srow_turned"], 1)
                for j in range(3):
                    for t in range(T):
                        lhs = X[:, t, j * CH:(j + 1) * CH] if j < 2 else ones[:, 0:CH]
                        ins = nc.tensor.matmul(ST[1][0:CH, j:j + 1], lhs, sc[:, t:t + 1], start=t == 0, stop=t == T - 1)
                ins.then_inc(s["pooled"], 1)
                values(b, 0, wv, 0)
                pe.wait_ge(s["picks"], b * 2 + 1)
                pe.wait_ge(s["srow_copied"], b * 1 + 1)
                for t in range(T):
                    ins = nc.tensor.transpose(ST[0][:, t * P:(t + 1) * P], rank[:, t:t + 1].to_broadcast([P, P]), ident[:])
                ins.then_inc(s["rank_turned"], 1)
                pe.wait_ge(s["picks"], b * 2 + 2)
                for c in range(2):
                    for t in range(T):
                        ins = nc.tensor.matmul(S[0][0:CH, c * 2 * QP:(c + 1) * 2 * QP], X[:, t, c * CH:(c + 1) * CH], PSEL[:, t, :],
                                               start=t == 0, stop=t == T - 1)
                ins.then_inc(s["gathersel"], 1)
                pe.wait_ge(s["nts"], b * 2 + 2)
                pe.wait_ge(s["pt"], b * 1 + 1)
                project(b, 4, wq, 0, NTS, 2 * QP, 1)

                def units0(h):
                    for u in range(4):
                        n = 4 * h + u
                        pe.wait_ge(s["reduced"], b * NUNITS + n + 1)
                        nc.tensor.matmul(S[n % 2][0:QP, :], QS0[0:KP, h, (u // 2) * QP:(u // 2 + 1) * QP],
                                         KS[0:KP, h, (u % 2) * HALF:(u % 2 + 1) * HALF], start=True, stop=True).then_inc(s["units"], 1)

                def maxrow0(h):
                    pe.wait_ge(s["rowmax"], b * 24 + h + 1)
                    pe.wait_ge(s["mcopied"], b * 24 + h + 1)
                    for q in range(2):
                        ins = nc.tensor.transpose(MT[KP:KP + 2, q * QP:(q + 1) * QP], nms[0:QP, h % 2, q, 0, :], identb[0:QP, 0:QP])
                    ins.then_inc(s["mturned"], 1)

                def exps0(h):
                    pe.wait_ge(s["mcopied"], b * 24 + h + 2)
                    for i in range(3):
                        n = 3 * h + i
                        pe.wait_ge(s["ex0"], b * 36 + n + 1)
                        for kt in range(3 * i, min(3 * i + 3, T)):
                            ins = nc.tensor.matmul(ring4[n % 4][:, (kt - 3 * i) * 2 * QP:(kt - 3 * i + 1) * 2 * QP], KS[0:KP + 2, h, kt * P:(kt + 1) * P],
                                                   QS0[0:KP + 2, h, :], start=True, stop=True)
                        ins.then_inc(s["st0"], 1)

                def pv0(h):
                    pe.wait_ge(s["ex0"], b * 36 + 3 * h + 3 + 4)
                    for kt in range(T):
                        ins = nc.tensor.matmul(PV[h // 3 * VW:(h // 3 + 1) * VW, (h % 3) * 2 * QP:(h % 3 + 1) * 2 * QP], V[:, kt, h, :],
                                               E0[:, h % 2, kt * 2 * QP:(kt + 1) * 2 * QP], start=kt == 0, stop=kt == T - 1)
                    ins.then_inc(s["pv0"], 1)

                pe.wait_ge(s["q0r"], b * 192 + 192)
                pe.wait_ge(s["kr0"], b * 192 + 96)
                pe.wait_ge(s["vcopied"], b * 8 + 4)
                pe.wait_ge(s["resid"], b * 14 + 6)
                units0(0)
                units0(1)
                maxrow0(0)
                for h in range(H):
                    exps0(h)
                    if h + 2 == 6:
                        pe.wait_ge(s["kr1"], b * 192 + 96)
                    if h + 2 < H:
                        units0(h + 2)
                    if h >= 1:
                        pv0(h - 1)
                    if h + 1 < H:
                        maxrow0(h + 1)
                pv0(H - 1)
                pe.wait_ge(s["acc0"], b * 1 + 1)
                for j in range(3):
                    for q in range(2):
                        o = (S[0][0:QP, (2 * j + q) * P:(2 * j + q + 1) * P] if j < 2 else S[1][0:QP, q * P:(q + 1) * P])
                        ins = nc.tensor.transpose(o, acc0[:, j * 2 * QP + q * QP:j * 2 * QP + (q + 1) * QP], ident[:])
                ins.then_inc(s["ctxr"], 1)
                pe.wait_ge(s["ctxn"], b * 1 + 1)
                for c in range(2):
                    for q in range(2):
                        ins = nc.tensor.transpose(ST[0][0:CH, (2 * c + q) * QP:(2 * c + q + 1) * QP], CX[:, q, c * CH:(c + 1) * CH], ident[0:QP, 0:QP])
                ins.then_inc(s["ctxt"], 1)
                pe.wait_ge(s["ctxtc"], b * 1 + 1)
                for q in range(2):
                    for c in range(2):
                        r = CH + c
                        ins = nc.tensor.matmul(ST[1][0:QP, q * D:(q + 1) * D], CXT[0:r, c, q * QP:(q + 1) * QP], wo[0:r, c, :], start=c == 0, stop=c == 1)
                ins.then_inc(s["att"], 1)
                pe.wait_ge(s["mixin"], b * 2 + 2)
                pe.wait_ge(s["atts"], b * 1 + 1)
                for t in range(T):
                    if t >= 2:
                        pe.wait_ge(s["merged"], b * 8 + t - 1)
                    o = O[t % 2]
                    for c in range(2):
                        r = CH + c
                        nc.tensor.matmul(o[:, 0:D], XT[0:r, c, t * P:(t + 1) * P], wm[0:r, c, :], start=c == 0, stop=c == 1)
                    for q in range(2):
                        ins = nc.tensor.matmul(o[:, D:2 * D], PT[0:QC, q, t * P:(t + 1) * P], ATS[0:QC, q, :], start=q == 0, stop=q == 1)
                    ins.then_inc(s["mixed"], 1)
                turn(b, 2, X, "xnorm", (8, 5, 6))
                pe.wait_ge(s["evac"], b * 28 + 12 + 2)
                for half in range(NH):
                    for f in range(FC):
                        i = half * FC + f
                        if i >= 4:
                            pe.wait_ge(s["gelu"], b * 12 + i - 3)
                        for c in range(2):
                            r = CH + c
                            ins = nc.tensor.matmul(ring4[i % 4], wf1[0:r, c, f * P:(f + 1) * P], XT[0:r, c, half * HALF:(half + 1) * HALF], start=c == 0, stop=c == 1)
                        ins.then_inc(s["hidden"], 1)
                for i in range(4):
                    pe.wait_ge(s["gelu"], b * 12 + (6 if i < 2 else 12))
                    if i >= 2:
                        pe.wait_ge(s["h2"], b * 4 + i - 1)
                    for t in (2 * i, 2 * i + 1):
                        o = O[i % 2][:, (t % 2) * D:(t % 2 + 1) * D]
                        for f in range(FC):
                            nc.tensor.matmul(o, hid[:, f, t * P:(t + 1) * P], wf2[:, f, :], start=f == 0, stop=False)
                        ins = nc.tensor.matmul(o, ones[0:1, :], bf2[:], start=False, stop=True)
                    ins.then_inc(s["ffn"], 1)
                turn(b, 3, X, "xnorm", (8, 7, 8))
                pe.wait_ge(s["evac"], b * 28 + 16 + 2)
                project(b, 6, wat, D, XT, HALF, 2)
                project(b, 10, wat, 0, XT, HALF, 2)
                values(b, 1, wat, 2 * D)

                def unit(what):
                    n = UNIT_AT[what]
                    kind, h, u = what
                    if kind == "ctx":
                        pe.wait_ge(s["accout"], b * 2 * H + 2 * h + u + 1)
                    pe.wait_ge(s["reduced"], b * NUNITS + n + 1)
                    if kind == "ctx":
                        for t in range(4):
                            ins = nc.tensor.transpose(S[n % 2][:, t * P:(t + 1) * P], acc_out[:, u, t * P:(t + 1) * P], ident[:])
                    elif u < 16:
                        ins = nc.tensor.matmul(S[n % 2][:, :], QS[0:KP, h, (u // 2) * P:(u // 2 + 1) * P], KS[0:KP, h, (u % 2) * HALF:(u % 2 + 1) * HALF],
                                               start=True, stop=True)
                    else:
                        for t in range(4):
                            qt = 4 * (u - 16) + t
                            ins = nc.tensor.matmul(S[n % 2][:, t * MSP:t * MSP + MS], QS[0:KP, h, qt * P:(qt + 1) * P], ksm[0:KP, h, 0:MS], start=True, stop=True)
                    ins.then_inc(s["units"], 1)

                def maxrow(h):
                    pe.wait_ge(s["rowmax"], b * 24 + 12 + h + 1)
                    pe.wait_ge(s["mcopied"], b * 24 + 12 + h + 1)
                    for t in range(T):
                        ins = nc.tensor.transpose(MT[KP:KP + 4, t * P:(t + 1) * P], nms[:, h % 2, t, :, :].rearrange("p a c -> p (a c)"), identb[:])
                    ins.then_inc(s["mturned"], 1)

                def scores(i):
                    h, half, k = i // 10, i // 5 % 2, i % 5
                    pe.wait_ge(s["exps"], b * NSTEP + i + 1)
                    if i % 10 == 0:
                        pe.wait_ge(s["mcopied"], b * 24 + 12 + h + 2)
                    queries = QS[0:KP + 4, h, half * HALF:(half + 1) * HALF]
                    if k < 4:
                        for kt in (2 * k, 2 * k + 1):
                            ins = nc.tensor.matmul(ST[i % 2][:, (kt % 2) * HALF:(kt % 2 + 1) * HALF], KS[0:KP + 4, h, kt * P:(kt + 1) * P], queries, start=True, stop=True)
                    else:
                        ins = nc.tensor.matmul(ST[i % 2][0:MS, 0:HALF], ksm[0:KP + 4, h, 0:MS], queries, start=True, stop=True)
                    ins.then_inc(s["stile"], 1)

                def weigh(i):
                    h, half, k = i // 10, i // 5 % 2, i % 5
                    pe.wait_ge(s["exps"], b * NSTEP + i + 3)
                    if k == 0:
                        if i:
                            pe.wait_ge(s["accout"], b * 2 * H + i // 5)
                        for kt in (0, 1):
                            ins = nc.tensor.matmul(PV[0:VW, :], V[:, kt, h, :], E[:, i % 3, kt * HALF:(kt + 1) * HALF], start=kt == 0, stop=False)
                    elif k < 4:
                        for kt in (2 * k, 2 * k + 1):
                            ins = nc.tensor.matmul(PV[0:VW, :], V[:, kt, h, :], E[:, i % 3, (kt % 2) * HALF:(kt % 2 + 1) * HALF], start=False, stop=kt == T - 1)
                    else:
                        ins = nc.tensor.matmul(PV[VW:2 * VW, :], vm[:, h, :], E[0:MS, i % 3, 0:HALF], start=True, stop=True)
                    ins.then_inc(s["pv"], 1)

                pe.wait_ge(s["kr0"], b * 192 + 192)
                pe.wait_ge(s["qr0"], b * 96 + 96)
                pe.wait_ge(s["vcopied"], b * 8 + 8)
                pe.wait_ge(s["mr"], 192)
                pe.wait_ge(s["resid"], b * 14 + 14)
                for what in FIRST_UNITS:
                    unit(what)
                maxrow(0)
                for i in range(NSTEP):
                    h, j = i // 10, i % 10
                    scores(i)
                    if h + 2 == 6 and j == 0:
                        pe.wait_ge(s["kr1"], b * 192 + 192)
                        pe.wait_ge(s["qr1"], b * 96 + 96)
                    for what in STEP_UNITS[i]:
                        unit(what)
                    if i >= 1:
                        weigh(i - 1)
                    if j == 4 and h + 1 < H:
                        maxrow(h + 1)
                weigh(NSTEP - 1)
                unit(LAST_UNITS[0])
                turn(b, 4, U, "reduced", (NUNITS, NUNITS + 2, NUNITS + 2))
                turn(b, 5, HP, "reduced", (NUNITS, NUNITS + 2, NUNITS + 2))
                pe.wait_ge(s["evac"], b * 28 + 24 + 2)
                for i in range(4):
                    if i >= 2:
                        pe.wait_ge(s["alphae"], b * 4 + i - 1)
                    for t in (2 * i, 2 * i + 1):
                        o = O[i % 2][:, (t % 2) * D:(t % 2 + 1) * D]
                        for c in range(4):
                            r = CH + (1 if c == 1 else 0)
                            x = XT[0:r, c, t * P:(t + 1) * P] if c < 2 else BT[:, c - 2, t * P:(t + 1) * P]
                            ins = nc.tensor.matmul(o, x, wal[0:r, c, :], start=c == 0, stop=c == 3)
                    ins.then_inc(s["alpha"], 1)
                turn(b, 6, X, "fusedx", (4, 2, 4))
                pe.wait_ge(s["evac"], b * 28 + 28 + 2)
                for i in range(4):
                    if i >= 2:
                        pe.wait_ge(s["h3"], b * 4 + i - 1)
                    for t in (2 * i, 2 * i + 1):
                        for c in range(2):
                            r = CH + c
                            ins = nc.tensor.matmul(O[i % 2][:, (t % 2) * D:(t % 2 + 1) * D], XT[0:r, c, t * P:(t + 1) * P], wpr[0:r, c, :], start=c == 0, stop=c == 1)
                    ins.then_inc(s["fproj"], 1)
                for i in range(4):
                    half, c = i // 2, i % 2
                    pe.wait_ge(s["quant"], b * 8 + 4 * half + 4)
                    if i >= 2:
                        pe.wait_ge(s["qcopied"], b * 4 + i - 1)
                    sb16 = S[i % 2][:, :].bitcast(BF16)
                    for t in range(4):
                        ins = nc.tensor.transpose(sb16[0:CH, t * P:(t + 1) * P], XQ[:, 4 * half + t, c * CH:(c + 1) * CH], identb[:])
                    ins.then_inc(s["qturned"], 1)
                pe.wait_ge(s["qcopied"], b * 4 + 4)
                for t in range(T):
                    if t >= 2:
                        pe.wait_ge(s["bgelu"], b * 8 + t - 1)
                    for n0, n1 in ((0, HALF), (HALF, F)):
                        for c in range(2):
                            ins = nc.tensor.matmul(ST[t % 2][:, n0:n1], XQT[:, c, t * P:(t + 1) * P], wb1[:, c, n0:n1], start=c == 0, stop=c == 1)
                    ins.then_inc(s["bhid"], 1)
                for t in range(T):
                    pe.wait_ge(s["hquant"], b * 8 + t + 1)
                    if t >= 2:
                        pe.wait_ge(s["hcopied"], b * 8 + t - 1)
                    sb16 = S[t % 2][:, :].bitcast(BF16)
                    for f in range(FC):
                        ins = nc.tensor.transpose(sb16[:, f * P:(f + 1) * P], HQ[:, (t % 2) * F + f * P:(t % 2) * F + (f + 1) * P], identb[:])
                    ins.then_inc(s["hturned"], 1)
                    pe.wait_ge(s["hcopied"], b * 8 + t + 1)
                    if t >= 4:
                        pe.wait_ge(s["outs"], b * 4 + t // 2 - 1)
                    for f in range(FC):
                        ins = nc.tensor.matmul(O[(t // 2) % 2][:, (t % 2) * D:(t % 2 + 1) * D], HQT[:, t % 2, f * P:(f + 1) * P], wb2[:, f, :], start=f == 0, stop=f == FC - 1)
                    ins.then_inc(s["bout"], 1)

        @block.scalar
        def _(act):
            A_ = nc.scalar.activation
            act.wait_ge(s["consts"], 15)
            act.wait_ge(s["pp"], 2)
            A_(memt[0:CH, :, :], S[0][0:CH, 0:2 * P].rearrange("p (c n) -> p c n", c=2)[:, :, 0:MS], ACT.Copy).then_inc(s["pa"], 1)
            act.wait_ge(s["pp"], 3)
            A_(splm[:, 0, :, 0:MS], S[1][0:CH, 0:2 * P].rearrange("p (c n) -> p c n", c=2)[:, :, 0:MS], ACT.Copy).then_inc(s["hi"], 1)
            act.wait_ge(s["pp"], 4)
            A_(vm[:, :, 0:DH], ST[0][0:MS, 0:D].rearrange("p (h d) -> p h d", h=H), ACT.Copy).then_inc(s["pa"], 1)
            act.wait_ge(s["pd"], 1)
            A_(splm[:, 1, :, 0:MS], R1[:, 0, 0:2 * MSP].rearrange("p (c n) -> p c n", c=2)[:, :, 0:MS], ACT.Copy).then_inc(s["pa"], 1)
            act.wait_ge(s["pp"], 6)
            A_(wb1[:, 0, :], ST[1][0:CH, 0:HALF].bitcast(BF16)[:, 0:F], ACT.Copy)
            A_(wb1[:, 1, :], ST[1][0:CH, HALF:2 * HALF].bitcast(BF16)[:, 0:F], ACT.Copy)
            A_(wb2[:, 0:3, :], ST[0][:, 0:HALF].bitcast(BF16)[:, 0:3 * D].rearrange("p (f d) -> p f d", f=3), ACT.Copy)
            A_(wb2[:, 3:6, :], ST[0][:, HALF:2 * HALF].bitcast(BF16)[:, 0:3 * D].rearrange("p (f d) -> p f d", f=3), ACT.Copy).then_inc(s["evac"], 2)

            def evac(b, job, dst, scale=None, bias=None):
                for i in range(4):
                    half, c = i // 2, i % 2
                    act.wait_ge(s["turned"], b * 28 + 4 * job + i + 1)
                    o = dst[0:CH, c, half * HALF:(half + 1) * HALF]
                    if scale is None:
                        ins = A_(o, S[i % 2][0:CH, :], ACT.Copy)
                    else:
                        ins = A_(o, S[i % 2][0:CH, :], ACT.Identity, scale=cols[:, c, scale:scale + 1], bias=cols[:, c, bias:bias + 1])
                    ins.then_inc(s["evac"], 1)

            def cut(b, group, dst, width, spans, waits=None):
                def mid(i):
                    m, j = (i - group) // spans, (i - group) % spans
                    act.wait_ge(s["resid"], b * 14 + i + 1)
                    A_(dst[:, 1, m, j * width:(j + 1) * width], R1[:, i % 2, 0:width], ACT.Copy).then_inc(s["mid"], 1)
                for i in range(group, group + 2 * spans):
                    m, j = (i - group) // spans, (i - group) % spans
                    act.wait_ge(s["proj"], b * 14 + i + 1)
                    A_(dst[:, 0, m, j * width:(j + 1) * width], ring4[i % 4][0:CH, 0:width], ACT.Copy).then_inc(s["hi"], 1)
                    if i > group:
                        mid(i - 1)
                mid(group + 2 * spans - 1)

            def vcopy(b, use):
                for i in range(4):
                    act.wait_ge(s["vproj"], b * 8 + 4 * use + i + 1)
                    A_(V[:, 2 * i:2 * i + 2, :, 0:DH], O[i % 2][:, 0:2 * D].rearrange("p (t h d) -> p t h d", t=2, h=H), ACT.Copy).then_inc(s["vcopied"], 1)

            act.wait_ge(s["mw"], 32)
            with act.Fori(0, NB) as b:
                evac(b, 0, XT)
                for i in range(8):
                    m, half = i // 2, i % 2
                    act.wait_ge(s["inproj"], b * 8 + i + 1)
                    if m < 2:
                        A_(XC[:, m, 2 + half * HALF:2 + (half + 1) * HALF], ring4[i % 4][0:CH, :], ACT.Copy).then_inc(s["inproj_out"], 1)
                    else:
                        A_(Z[:, m - 2, half * HALF:(half + 1) * HALF], ring4[i % 4][0:CH, :], ACT.Silu).then_inc(s["inproj_out"], 1)
                for c in range(2):
                    act.wait_ge(s["conv"], b * 2 + c + 1)
                    A_(XS[:, c, :], Y1[:, c, :], ACT.Silu).then_inc(s["silu"], 1)
                evac(b, 1, XT, 2, 3)
                act.wait_ge(s["logit"], b + 1)
                A_(sc1[:], PV[:, 0:T], ACT.Exp, scale=-1.0).then_inc(s["expz"], 1)
                cut(b, 0, spl, HALF, 2)
                act.wait_ge(s["srow_turned"], b + 1)
                A_(srow[:], ST[0][:, :], ACT.Copy).then_inc(s["srow_copied"], 1)
                vcopy(b, 0)
                act.wait_ge(s["gathersel"], b + 1)
                for c in range(2):
                    A_(NTS[0:CH, c, :], S[0][0:CH, c * 2 * QP:(c + 1) * 2 * QP], ACT.Identity, scale=cols[:, c, 2:3], bias=cols[:, c, 3:4]).then_inc(s["nts"], 1)
                cut(b, 4, spl0, 2 * QP, 1)

                def mcopy0(h):
                    act.wait_ge(s["mturned"], b * 24 + h + 1)
                    A_(QS0[KP:KP + 2, h, :], MT[KP:KP + 2, 0:2 * QP], ACT.Copy).then_inc(s["mcopied"], 1)

                mcopy0(0)
                act.wait_ge(s["kw0"], (b * 2 + 1) * 16)
                act.wait_ge(s["kw1"], (b * 2 + 1) * 16)
                for h in range(H):
                    for i in range(3):
                        n = 3 * h + i
                        w = (3 if i < 2 else 2) * 2 * QP
                        act.wait_ge(s["st0"], b * 36 + n + 1)
                        act.wait_ge(s["pv0"], b * H + h + 1)
                        A_(E0[:, h % 2, i * 6 * QP:i * 6 * QP + w], ring4[n % 4][:, 0:w], ACT.Exp, scale=float(DH) ** -0.5).then_inc(s["ex0"], 1)
                    if h + 1 < H:
                        mcopy0(h + 1)
                act.wait_ge(s["pv0"], b * H + H + 2)
                A_(acc0, PV[:, 0:3 * 2 * QP], ACT.Copy).then_inc(s["acc0"], 1)
                act.wait_ge(s["ctxt"], b + 1)
                A_(CXT[0:CH, :, :], ST[0][0:CH, 0:4 * QP].rearrange("p (c n) -> p c n", c=2), ACT.Copy).then_inc(s["ctxtc"], 1)
                act.wait_ge(s["att"], b + 1)
                A_(ATS[:, :, :], ST[1][0:QP, 0:2 * D].rearrange("p (q d) -> p q d", q=2), ACT.Copy).then_inc(s["atts"], 1)
                evac(b, 2, XT, 4, 5)
                for i in range(12):
                    act.wait_ge(s["hidden"], b * 12 + i + 1)
                    A_(hid[:, i % FC, (i // FC) * HALF:(i // FC + 1) * HALF], ring4[i % 4], ACT.Gelu).then_inc(s["gelu"], 1)
                evac(b, 3, XT)
                act.wait_ge(s["kw0"], (b * 2 + 1) * 16)
                act.wait_ge(s["kw1"], (b * 2 + 1) * 16)
                cut(b, 6, spl, HALF, 2)
                act.wait_ge(s["kw0"], (b * 2 + 2) * 16)
                act.wait_ge(s["kw1"], (b * 2 + 2) * 16)
                cut(b, 10, spl, HALF, 2)
                vcopy(b, 1)

                def mcopy(h):
                    act.wait_ge(s["mturned"], b * 24 + 12 + h + 1)
                    A_(QS[KP:KP + 4, h, :], MT[KP:KP + 4, :], ACT.Copy).then_inc(s["mcopied"], 1)

                def out_sums(j):
                    act.wait_ge(s["pv"], b * NSTEP + STEPS * (j + 1) + 3)
                    if j >= 2:
                        act.wait_ge(s["units"], b * NUNITS + UNIT_AT["ctx", (j - 2) // 2, j % 2] + 1)
                    A_(acc_out[:, j % 2, :], PV[:, :], ACT.Copy).then_inc(s["accout"], 1)

                mcopy(0)
                for i in range(NSTEP):
                    h, k = i // 10, i % 5
                    m, width = (P, 2 * HALF) if k < 4 else (MS, HALF)
                    act.wait_ge(s["stile"], b * NSTEP + i + 1)
                    act.wait_ge(s["pv"], b * NSTEP + i + 1)
                    A_(E[0:m, i % 3, 0:width], ST[i % 2][0:m, 0:width], ACT.Exp).then_inc(s["exps"], 1)
                    if k == 0 and i > 0:
                        out_sums(i // 5 - 1)
                    if i % 10 == 6 and h + 1 < H:
                        mcopy(h + 1)
                out_sums(2 * H - 1)
                evac(b, 4, XT)
                evac(b, 5, BT)
                for i in range(4):
                    act.wait_ge(s["alpha"], b * 4 + i + 1)
                    if i >= 2:
                        act.wait_ge(s["fusedx"], b * 4 + i - 1)
                    A_(e2[:, i % 2, :, :], O[i % 2][:, 0:2 * D].rearrange("p (t d) -> p t d", t=2), ACT.Exp, scale=-1.0).then_inc(s["alphae"], 1)
                evac(b, 6, XT)
                for i in range(4):
                    half, c = i // 2, i % 2
                    act.wait_ge(s["qturned"], b * 4 + i + 1)
                    A_(XQT[:, c, half * HALF:(half + 1) * HALF], S[i % 2][0:CH, :].bitcast(BF16)[:, 0:HALF], ACT.Copy).then_inc(s["qcopied"], 1)
                for t in range(T):
                    act.wait_ge(s["bhid"], b * 8 + t + 1)
                    A_(HG[:, t, :], ST[t % 2][:, 0:F], ACT.Gelu, scale=gsc[:, t:t + 1]).then_inc(s["bgelu"], 1)
                    act.wait_ge(s["bgelu"], b * 8 + t + 1)
                    if t >= 1:
                        act.wait_ge(s["hss"], b * 8 + t)
                    A_(junk[:, 0:F], HG[:, t, :], ACT.Square, accum_out=ss[:, t:t + 1]).then_inc(s["hss"], 1)
                for t in range(T):
                    act.wait_ge(s["hturned"], b * 8 + t + 1)
                    A_(HQT[:, t % 2, :], S[t % 2][:, :].bitcast(BF16)[:, 0:F], ACT.Copy).then_inc(s["hcopied"], 1)
                act.wait_ge(s["outs"], b * 4 + 4)
                act.dma_start(ovw[b], HS[:, :, :]).then_inc(s["stored"], 16)
            act.wait_ge(s["stored"], NB * 16 + 16)

        @block.vector
        def _(ve):
            v = nc.vector
            k = [0]
            at = {"b": None, "base": 0}

            def link(ins):
                k[0] += 1
                ins.then_inc(s["vlink"], 1)
                if at["b"] is None:
                    ve.wait_ge(s["vlink"], k[0])
                else:
                    ve.wait_ge(s["vlink"], at["b"] * VEC_LINKS + at["base"] + k[0])

            v.memset(nmp[:], 0.0).then_inc(s["reduced"], 2)
            v.memset(nms[:].rearrange("p a t c d -> p (a t c d)"), 0.0).then_inc(s["mcopied"], 1)
            v.memset(rec[:], 0.0).then_inc(s["ex0"], 4)
            v.memset(e2[:, 0, 0, 0:8], 0.0).then_inc(s["exps"], 2)
            v.memset(e2[:, 0, 0, 8:16], 0.0).then_inc(s["pv"], 3)
            v.memset(e2[:, 0, 0, 16:24], 0.0).then_inc(s["pv0"], 2)
            v.memset(CX[:, 0, 0:8], 0.0).then_inc(s["stored"], 16)
            ve.wait_ge(s["consts"], 15)
            ve.wait_ge(s["loaded"], LOADED)
            link(v.memset(PV[:, :], 0.0))
            link(v.tensor_tensor(bmat[:], bmat[:], cmat[:], ALU.mult))
            link(v.tensor_reduce(cols[:, :, 6], bmat[:], AX.X, ALU.add))
            ve.wait_ge(s["hi"], 1)
            kmem = S[1][0:CH, 0:2 * P].rearrange("p (c n) -> p c n", c=2)[:, :, 0:MS]
            res = R1[:, 0, 0:2 * MSP].rearrange("p (c n) -> p c n", c=2)[:, :, 0:MS]
            v.tensor_tensor(res, kmem, splm[:, 0, :, 0:MS], ALU.subtract).then_inc(s["pd"], 1)
            ve.wait_ge(s["pa"], 3)
            v.tensor_tensor(splm[:, 2, :, 0:MS], res, splm[:, 1, :, 0:MS], ALU.subtract).then_inc(s["pd"], 1)
            w1, w2 = X[:, 0:FC, :], HG[0:CH, 0:2, :]
            v.tensor_reduce(wsum[:, 0:1], w1, AX.XY, ALU.add, apply_absolute_value=True)
            v.tensor_reduce(wsum[0:CH, 1:2], w2, AX.XY, ALU.add, apply_absolute_value=True).then_inc(s["pd"], 1)
            ve.wait_ge(s["pp"], 5)
            link(v.tensor_scalar(wsinv[:], PV[:, 0:2], 1.0 / (D * F), 1e-5, ALU.mult, ALU.max))
            link(v.reciprocal(wscale[:], wsinv[:]))
            for w, q, n, c in ((w1, XQ[:, 0:FC, :], P, 0), (w2, HQT[0:CH, :, :], CH, 1)):
                link(v.tensor_scalar(w, w, wscale[0:n, c:c + 1], MAGIC, ALU.mult, ALU.add))
                link(v.tensor_scalar(w, w, MAGIC, -1.0, ALU.subtract, ALU.max))
                v.tensor_scalar(q, w, 1.0, None, ALU.min).then_inc(s["pd"], 1)
            ve.wait_ge(s["pp"], 6)
            v.memset(XT[CH:CH + 1, 1, :], 1.0).then_inc(s["pa"], 1)
            at["base"] = k[0]
            k[0] = 0

            def stats(b, n, src):
                for t in range(T):
                    ins = v.bn_stats(st[:, t, :], src[:, t, :])
                link(ins)
                v.memset(rec[:, 0:1], 0.0)
                for t in range(T):
                    ins = v.bn_aggr(mv[:, t, :], st[:, t, :])
                ins.then_inc(s["stats"], 1)
                ve.wait_ge(s["rstd"], b * 5 + n + 1)

            def normalise(job, src, scale):
                for t in range(T):
                    ins = v.tensor_scalar(X[:, t, :], src[:, t, :], mv[:, t, 0:1], scale[:, t:t + 1], ALU.subtract, ALU.mult)
                    if t % 4 == 3:
                        ins.then_inc(s["xnorm"], 1)

            def cut(b, group, dst, width, spans):
                def low(i):
                    m, j = (i - group) // spans, (i - group) % spans
                    ve.wait_ge(s["mid"], b * 14 + i + 1)
                    v.tensor_tensor(dst[:, 2, m, j * width:(j + 1) * width], R1[:, i % 2, 0:width], dst[:, 1, m, j * width:(j + 1) * width],
                                    ALU.subtract).then_inc(s["lo"], 1)
                for i in range(group, group + 2 * spans):
                    m, j = (i - group) // spans, (i - group) % spans
                    ve.wait_ge(s["hi"], b * 14 + i + 2)
                    if i >= 2:
                        ve.wait_ge(s["lo"], b * 14 + i - 1)
                    v.tensor_tensor(R1[:, i % 2, 0:width], ring4[i % 4][0:CH, 0:width], dst[:, 0, m, j * width:(j + 1) * width],
                                    ALU.subtract).then_inc(s["resid"], 1)
                    if i > group:
                        low(i - 1)
                low(group + 2 * spans - 1)

            with ve.Fori(0, NB) as b:
                at["b"] = b
                ve.wait_ge(s["gathered"], b * 128 + 128)
                stats(b, 0, G)
                normalise(0, G, rn)
                for c in range(2):
                    ve.wait_ge(s["inproj_out"], b * 8 + 2 * c + 2)
                    if c == 0:
                        link(v.memset(XC[:, :, 0:2], 0.0))
                    link(v.tensor_scalar(Y1[:, c, :], XC[:, c, 2:L + 2], convw[:, c, 2:3], cols[:, c, 0:1], ALU.mult, ALU.add))
                    link(v.scalar_tensor_tensor(out=Y1[:, c, :], in0=XC[:, c, 1:L + 1], scalar=convw[:, c, 1:2], in1=Y1[:, c, :], op0=ALU.mult, op1=ALU.add))
                    v.scalar_tensor_tensor(out=Y1[:, c, :], in0=XC[:, c, 0:L], scalar=convw[:, c, 0:1], in1=Y1[:, c, :], op0=ALU.mult, op1=ALU.add).then_inc(s["conv"], 1)
                for c in range(2):
                    ve.wait_ge(s["silu"], b * 2 + c + 1)
                    v.tensor_scalar(Y1[:, c, :], XS[:, c, :], cols[:, c, 1:2], None, ALU.mult)
                    link(v.tensor_tensor_scan(CUM[:, c, :], XS[:, c, :], XS[:, c, :], 0.0, ALU.add, ALU.bypass))
                    link(v.scalar_tensor_tensor(out=CUM[:, c, :], in0=CUM[:, c, :], scalar=cols[:, c, 6:7], in1=Y1[:, c, :], op0=ALU.mult, op1=ALU.add))
                    if c == 0:
                        ve.wait_ge(s["inproj_out"], b * 8 + 8)
                    v.tensor_tensor(CUM[:, c, :], CUM[:, c, :], Z[:, c, :], ALU.mult).then_inc(s["gated"], 1)
                ve.wait_ge(s["stored"], b * 16 + 16)
                for i in range(4):
                    ve.wait_ge(s["outproj"], b * 4 + i + 1)
                    v.tensor_tensor(HS[:, 2 * i:2 * i + 2, :], O[i % 2][:, 0:2 * D].rearrange("p (t d) -> p t d", t=2), G[:, 2 * i:2 * i + 2, :], ALU.add).then_inc(s["h1"], 1)
                ve.wait_ge(s["h1"], b * 4 + 4)
                stats(b, 1, HS)
                normalise(1, HS, rnn)
                for t in range(T):
                    v.tensor_scalar(U[:, t, :], HS[:, t, :], mv[:, t, 0:1], rn[:, t:t + 1], ALU.subtract, ALU.mult)
                ve.wait_ge(s["expz"], b + 1)
                link(v.tensor_scalar(sc1[:], sc1[:], 1.0, None, ALU.add))
                v.reciprocal(sc[:], sc1[:]).then_inc(s["score"], 1)
                ve.wait_ge(s["score"], b + 1)
                cut(b, 0, spl, HALF, 2)
                ve.wait_ge(s["srow_copied"], b + 1)
                for t in range(T):
                    v.tensor_scalar(junk[:, 0:L - t * P], srow[:, t * P:L], sc[:, t:t + 1], 0.0, ALU.is_lt, ALU.add, accum_out=cnt[:, 0, t:t + 1])
                    if t > 0:
                        v.tensor_scalar(junk[:, L - t * P:L], srow[:, 0:t * P], sc[:, t:t + 1], 0.0, ALU.is_le, ALU.add, accum_out=cnt[:, 1, t:t + 1])
                    link(v.scalar_tensor_tensor(out=junk2[:], in0=srow[:, t * P:(t + 1) * P], scalar=sc[:, t:t + 1], in1=earlier[:], op0=ALU.is_equal, op1=ALU.mult,
                                                accum_out=cnt[:, 2, t:t + 1]))
                link(v.tensor_tensor(rank[:], cnt[:, 0, :], cnt[:, 1, :], ALU.add))
                v.tensor_tensor(rank[:], rank[:], cnt[:, 2, :], ALU.add).then_inc(s["picks"], 1)
                ve.wait_ge(s["picks"], b * 2 + 1)
                v.tensor_scalar(notsel[:], rank[:], float(NSEL), None, ALU.is_ge)
                for t in range(T):
                    ins = v.tensor_scalar(PSEL[:, t, :], slot[:].rearrange("p a n -> p (a n)"), rank[:, t:t + 1], None, ALU.is_equal)
                ins.then_inc(s["picks"], 1)
                ve.wait_ge(s["rank_turned"], b + 1)
                for q in range(2):
                    ins = v.tensor_scalar(PT[0:QC, q, :], ST[0][0:QC, :], rowslot[0:QC, q:q + 1], None, ALU.is_equal)
                ins.then_inc(s["pt"], 1)
                ve.wait_ge(s["pooled"], b + 1)
                link(v.tensor_scalar(pool3[:, 0:1], ST[1][0:CH, 2:3], 1e-6, None, ALU.add))
                link(v.reciprocal(pool3[:, 1:2], pool3[:, 0:1]))
                link(v.tensor_scalar(pool3[:, 2:5], ST[1][0:CH, 0:3], pool3[:, 1:2], None, ALU.mult))
                link(v.tensor_tensor(pool3[:, 5:7], pool3[:, 2:4], cols[:, :, 2], ALU.mult))
                for c in range(2):
                    link(v.scalar_tensor_tensor(out=pool3[:, 5 + c:6 + c], in0=cols[:, c, 3:4], scalar=pool3[:, 4:5], in1=pool3[:, 5 + c:6 + c], op0=ALU.mult, op1=ALU.add))
                cut(b, 4, spl0, 2 * QP, 1)
                ve.wait_ge(s["gathersel"], b + 1)
                for c in range(2):
                    v.scalar_tensor_tensor(out=XT[0:CH, c, :], in0=srow[0:CH, :], scalar=pool3[:, 5 + c:6 + c], in1=XT[0:CH, c, :], op0=ALU.mult, op1=ALU.add).then_inc(s["mixin"], 1)

                def chain(h, n, rows, tiles, kinds):
                    if n > 0:
                        ve.wait_ge(s["rowmax"], b * 24 + n)
                    link(v.tensor_reduce(nm[0:rows, 0:tiles, 0:1], nmp[0:rows, 0:tiles, :], AX.X, ALU.max, negate=True))
                    link(v.tensor_copy(nms[0:rows, h % 2, 0:tiles, 0:kinds, 0], nm[0:rows, 0:tiles, 0:kinds]))
                    v.tensor_tensor(nms[0:rows, h % 2, 0:tiles, 0:kinds, 1], nm[0:rows, 0:tiles, 0:kinds], nms[0:rows, h % 2, 0:tiles, 0:kinds, 0],
                                    ALU.subtract).then_inc(s["rowmax"], 1)

                for h in range(H):
                    for u in range(4):
                        n = 4 * h + u
                        ve.wait_ge(s["units"], b * NUNITS + n + 1)
                        v.tensor_reduce(nmp[0:QP, u // 2, u % 2:u % 2 + 1], S[n % 2][0:QP, :], AX.X, ALU.max).then_inc(s["reduced"], 1)
                    ve.wait_ge(s["reduced"], b * NUNITS + 4 * h + 6)
                    if h >= 2:
                        ve.wait_ge(s["mturned"], b * 24 + h - 1)
                    chain(h, h, QP, 2, 1)
                ve.wait_ge(s["ctxr"], b + 1)
                for j in range(3):
                    src = (S[0][0:QP, j * 2 * P:(j + 1) * 2 * P] if j < 2 else S[1][0:QP, 0:2 * P]).rearrange("p (q a d) -> p q a d", q=2, a=4)
                    link(v.reciprocal(rec[0:QP, 0:8].rearrange("p (q a) -> p q a", q=2), src[:, :, :, DH]))
                    for q in range(2):
                        ins = v.tensor_tensor(CX[:, q, :].rearrange("p (a j d) -> p a j d", a=4, j=3)[:, :, j, :], src[:, q, :, 0:DH],
                                              rec[0:QP, 4 * q:4 * q + 4].unsqueeze(2).to_broadcast([QP, 4, DH]), ALU.mult)
                    if j < 2:
                        link(ins)
                ins.then_inc(s["ctxn"], 1)
                for t in range(T):
                    ve.wait_ge(s["mixed"], b * 8 + t + 1)
                    o = O[t % 2]
                    link(v.scalar_tensor_tensor(out=HP[:, t, :], in0=o[:, 0:D], scalar=notsel[:, t:t + 1], in1=U[:, t, :], op0=ALU.mult, op1=ALU.add))
                    v.tensor_tensor(HP[:, t, :], HP[:, t, :], o[:, D:2 * D], ALU.add).then_inc(s["merged"], 1)
                ve.wait_ge(s["merged"], b * 8 + 8)
                stats(b, 2, HP)
                normalise(2, HP, rn)
                link(v.tensor_tensor(HS[:], HS[:], HP[:], ALU.add))
                for i in range(4):
                    ve.wait_ge(s["ffn"], b * 4 + i + 1)
                    v.tensor_tensor(HS[:, 2 * i:2 * i + 2, :], O[i % 2][:, 0:2 * D].rearrange("p (t d) -> p t d", t=2), HS[:, 2 * i:2 * i + 2, :], ALU.add).then_inc(s["h2"], 1)
                ve.wait_ge(s["h2"], b * 4 + 4)
                stats(b, 3, HS)
                normalise(3, HS, rn)
                cut(b, 6, spl, HALF, 2)
                cut(b, 10, spl, HALF, 2)

                def unit(what):
                    n = UNIT_AT[what]
                    kind, h, u = what
                    ve.wait_ge(s["units"], b * NUNITS + n + 1)
                    if kind == "ctx":
                        if h or u:
                            last = UNIT_AT["ctx", h - 1 + u, 1 - u]
                            ve.wait_ge(s["reduced"], b * NUNITS + last + 3)
                        src = S[n % 2][:, :].rearrange("p (t a d) -> p t a d", t=4, a=4)[:, :, 0:2, :]
                        link(v.reciprocal(rec[:, 0:8].rearrange("p (t a) -> p t a", t=4), src[:, :, :, DH]))
                        inv = rec[:, 0:8].rearrange("p (t a) -> p t a", t=4)
                        v.tensor_tensor(U[:, 4 * u:4 * u + 4, h * DH:(h + 1) * DH], src[:, :, 0, 0:DH], inv[:, :, 0:1].to_broadcast([P, 4, DH]), ALU.mult)
                        v.tensor_tensor(HP[:, 4 * u:4 * u + 4, h * DH:(h + 1) * DH], src[:, :, 1, 0:DH], inv[:, :, 1:2].to_broadcast([P, 4, DH]), ALU.mult).then_inc(s["reduced"], 1)
                    elif u < 16:
                        v.tensor_reduce(nmp[:, u // 2, u % 2:u % 2 + 1], S[n % 2][:, :], AX.X, ALU.max).then_inc(s["reduced"], 1)
                    else:
                        j = 4 * (u - 16)
                        if j == 0:
                            ve.wait_ge(s["rowmax"], b * 24 + H + h)
                        v.tensor_reduce(nm[:, j:j + 4, 1], S[n % 2][:, 0:4 * MSP].rearrange("p (t n) -> p t n", t=4)[:, :, 0:MS], AX.X, ALU.max,
                                        negate=True).then_inc(s["reduced"], 1)
                    if kind == "max" and u == SCORE_UNITS - 1:
                        ve.wait_ge(s["reduced"], b * NUNITS + n + 3)
                        ve.wait_ge(s["mturned"], b * 24 + 12 + max(h - 1, 0))
                        chain(h, H + h, P, T, 2)

                for what in ALL_UNITS:
                    unit(what)
                ve.wait_ge(s["reduced"], b * NUNITS + NUNITS + 2)
                for i in range(4):
                    ve.wait_ge(s["alphae"], b * 4 + i + 1)
                    e = e2[:, i % 2, :, :]
                    a, a1, x = U[:, 2 * i:2 * i + 2, :], HP[:, 2 * i:2 * i + 2, :], X[:, 2 * i:2 * i + 2, :]
                    v.tensor_scalar(e, e, 1.0, None, ALU.add)
                    link(v.tensor_tensor(a, a, a1, ALU.subtract))
                    link(v.reciprocal(e, e))
                    link(v.tensor_tensor(a, a, e, ALU.mult))
                    v.tensor_tensor(x, a, a1, ALU.add).then_inc(s["fusedx"], 1)
                for i in range(4):
                    ve.wait_ge(s["fproj"], b * 4 + i + 1)
                    v.tensor_tensor(HS[:, 2 * i:2 * i + 2, :], O[i % 2][:, 0:2 * D].rearrange("p (t d) -> p t d", t=2), HS[:, 2 * i:2 * i + 2, :], ALU.add).then_inc(s["h3"], 1)
                ve.wait_ge(s["h3"], b * 4 + 4)
                stats(b, 4, HS)
                for t in range(T):
                    ins = v.tensor_scalar(X[:, t, :], HS[:, t, :], mv[:, t, 0:1], rnn[:, t:t + 1], ALU.subtract, ALU.mult)
                link(ins)
                link(v.tensor_tensor(X[:], X[:], g1bc[:].unsqueeze(1).to_broadcast([P, T, D]), ALU.mult))
                link(v.tensor_reduce(amax[:], X[:], AX.X, ALU.max, apply_absolute_value=True))
                link(v.tensor_scalar(qinv[:], amax[:], 1e-5, 1.0 / 127.0, ALU.max, ALU.mult))
                v.tensor_scalar(gsc[:], qinv[:], wsinv[:, 0:1], None, ALU.mult)
                link(v.reciprocal(qsc[:], qinv[:]))
                for t in range(T):
                    link(v.tensor_scalar(X[:, t, :], X[:, t, :], qsc[:, t:t + 1], MAGIC, ALU.mult, ALU.add))
                    v.tensor_scalar(XQ[:, t, :], X[:, t, :], MAGIC, None, ALU.subtract).then_inc(s["quant"], 1)
                for t in range(T):
                    ve.wait_ge(s["hss"], b * 8 + t + 1)
                    link(v.tensor_tensor(HG[:, t, :], HG[:, t, :], g2bc[:], ALU.mult))
                    link(v.tensor_reduce(amax[:, t:t + 1], HG[:, t, :], AX.X, ALU.max, apply_absolute_value=True))
                ve.wait_ge(s["hrms"], b + 1)
                link(v.tensor_tensor(amax[:], amax[:], rn[:], ALU.mult))
                link(v.tensor_scalar(qinv[:], amax[:], 1e-5, 1.0 / 127.0, ALU.max, ALU.mult))
                link(v.reciprocal(qsc[:], qinv[:]))
                link(v.tensor_tensor(qsc[:], qsc[:], rn[:], ALU.mult))
                link(v.tensor_scalar(gsc[:], qinv[:], wsinv[:, 1:2], None, ALU.mult))

                def store(i):
                    ve.wait_ge(s["bout"], b * 8 + 2 * i + 2)
                    for t in (2 * i, 2 * i + 1):
                        ins = v.scalar_tensor_tensor(out=HS[:, t, :], in0=O[i % 2][:, (t % 2) * D:(t % 2 + 1) * D], scalar=gsc[:, t:t + 1], in1=HS[:, t, :],
                                                     op0=ALU.mult, op1=ALU.add)
                    ins.then_inc(s["outs"], 1)

                for t in range(T):
                    link(v.tensor_scalar(HG[:, t, :], HG[:, t, :], qsc[:, t:t + 1], MAGIC, ALU.mult, ALU.add))
                    if t >= 2:
                        ve.wait_ge(s["hturned"], b * 8 + t - 1)
                    v.tensor_scalar(HQ[:, (t % 2) * F:(t % 2 + 1) * F], HG[:, t, :], MAGIC, None, ALU.subtract).then_inc(s["hquant"], 1)
                    if t % 2 == 1 and t >= 3:
                        store(t // 2 - 1)
                store(3)
            assert k[0] == VEC_LINKS, k[0]


_INS = ['x', 'L0_tok_embed_matrix', 'L0_attn_W_in', 'L0_attn_conv_w', 'L0_attn_conv_b', 'L0_attn_B', 'L0_attn_C', 'L0_attn_D',
        'L0_attn_W_out', 'L0_ffn_g1', 'L0_ffn_b1', 'L0_ffn_g2', 'L0_ffn_b2', 'L0_ffn_Wr', 'L0_ffn_br', 'L0_ffn_Wq', 'L0_ffn_bq',
        'L0_ffn_Wk', 'L0_ffn_bk', 'L0_ffn_Wv', 'L0_ffn_bv', 'L0_ffn_Wo', 'L0_ffn_bo', 'L0_ffn_Wm', 'L0_ffn_bm', 'L0_ffn_W1',
        'L0_ffn_bf1', 'L0_ffn_W2', 'L0_ffn_bf2', 'L1_attn_w_attn', 'L1_attn_b_attn', 'L1_attn_w_proj', 'L1_attn_b_proj',
        'L1_attn_w_mem', 'L1_attn_b_mem', 'L1_attn_w_alpha', 'L1_attn_b_alpha', 'L1_attn_memory_features', 'L1_ffn_w1',
        'L1_ffn_g1', 'L1_ffn_w2', 'L1_ffn_g2']


def kernel(**inputs):
    import numpy as _np
    import concourse.bacc as _bacc
    from concourse import mybir as _mybir
    from concourse.bass_utils import run_bass_kernel_spmd as _run

    nc = _bacc.Bacc("TRN2", target_bir_lowering=False, num_devices=1)
    arrays, aps = {}, {}
    for name in _INS:
        a = _np.ascontiguousarray(inputs[name])
        arrays[f"in_{name}_dram"] = a
        aps[name] = nc.dram_tensor(f"in_{name}_dram", a.shape, _mybir.dt.from_np(a.dtype), kind="ExternalInput").ap()
    out = nc.dram_tensor("out_0_dram", (NB, L, D), _mybir.dt.float32, kind="ExternalOutput").ap()
    build(nc, aps, out)
    r = _run(nc, [arrays], core_ids=[0])
    return r.results[0]["out_0_dram"]
```

```python
from contextlib import ExitStack

import concourse.bass as bass
from concourse import mybir

F32 = mybir.dt.float32
BF16 = mybir.dt.bfloat16
I32 = mybir.dt.int32
ALU = mybir.AluOpType
ACT = mybir.ActivationFunctionType
AX = mybir.AxisListType

P = 128
D = 192
CH = 96
NB = 4
L = 1024
T = L // P
HALF = 512
H = 12
DH = D // H
VP = 64
VONE = 3 * DH
VW = 32
F = 768
FC = F // P
MS = 100
MSP = 104
NSEL = max(1, int(round(0.15 * L)))
QC = NSEL // 2
QP = 80
MAGIC = 12582912.0
LN_EPS = 1e-5
RMS_EPS = 1e-6
Q_PARTS = (0, 0, 1, 0, 2, 1)
K_PARTS = (0, 1, 0, 2, 0, 1)
KP = 6 * DH
NH = 2
STEPS = 5
NSTEP = H * NH * STEPS
LAG = 3
RING = LAG + 1
NCUT = H * NH * 4
SCORE_UNITS = 18
UNITS0 = 4 * H
MAX_PATTERN = (2, 2, 3, 3, 1, 0, 3, 2, 2, 0)
SUMS_AT = LAG - 1
MAX_AT = 6
VEC_LINKS = 193


def plan_units():
    first = [("max", 0, u) for u in range(SCORE_UNITS)]
    maxima = [("max", h, u) for h in range(1, H) for u in range(SCORE_UNITS)]
    steps = []
    for i in range(NSTEP):
        h, j = i // 10, i % 10
        count = 3 if i < 6 else MAX_PATTERN[j]
        units, maxima = maxima[:count], maxima[count:]
        if j == 9:
            units.append(("ctx", h, 0))
        if j == 4 and h > 0:
            units.append(("ctx", h - 1, 1))
        steps.append(units)
    assert not maxima
    return first, steps, [("ctx", H - 1, 1)]


FIRST_UNITS, STEP_UNITS, LAST_UNITS = plan_units()
ALL_UNITS = FIRST_UNITS + sum(STEP_UNITS, []) + LAST_UNITS
NUNITS = UNITS0 + len(ALL_UNITS)
UNIT_AT = {u: UNITS0 + n for n, u in enumerate(ALL_UNITS)}


def cut_of(i):
    return i // STEPS * 4 + i % STEPS, i % STEPS < 3


def step_of(cut):
    return cut // 4 * STEPS + cut % 4


def lows(i):
    cut, pool = cut_of(i)
    return ("plow", cut // 4 * 3 + cut % 4 + 1) if pool else ("vlow", cut // 4 + 1)


LOWS = {"plow": NCUT * 3 // 4, "vlow": NCUT // 4}


def build(nc, A, out):
    ctx = ExitStack()
    with ctx:
        def sb(name, shape, dt=F32):
            return ctx.enter_context(nc.sbuf_tensor(name, shape, dt))

        def pb(name, shape, dt=F32):
            return ctx.enter_context(nc.psum_tensor(name, shape, dt))

        def sem(name):
            return ctx.enter_context(nc.semaphore(name))

        ident = sb("ident", [P, P])
        identb = sb("identb", [P, P], BF16)
        earlier = sb("earlier", [P, P])
        ones = sb("ones", [P, P])
        neghalf = sb("neghalf", [P, T])
        slot_i = sb("slot_i", [P, 2, QP], I32)
        slot = sb("slot", [P, 2, QP])
        rowslot_i = sb("rowslot_i", [P, 2], I32)
        rowslot = sb("rowslot", [P, 2])
        tok_i = sb("tok_i", [P, NB * T], I32)
        win = sb("win", [CH, 2, 2 * D])
        wout = sb("wout", [CH, 2, D])
        convw = sb("convw", [CH, 2, 3])
        cols = sb("cols", [CH, 2, 8])
        bmat = sb("bmat", [CH, 2, 8])
        cmat = sb("cmat", [CH, 2, 8])
        wr = sb("wr", [CH + 1, 2, 1])
        wq = sb("wq", [CH + 1, 2, D])
        wk = sb("wk", [CH + 1, 2, D])
        wv = sb("wv", [CH + 1, 2, D])
        wo = sb("wo", [CH + 1, 2, D])
        wm = sb("wm", [CH + 1, 2, D])
        wf1 = sb("wf1", [CH + 1, 2, F])
        wf2 = sb("wf2", [P, FC, D])
        bf2 = sb("bf2", [1, D])
        wat = sb("wat", [CH + 1, 2, 3 * D])
        wal = sb("wal", [CH + 1, 4, D])
        wpr = sb("wpr", [CH + 1, 2, D])
        g1bc = sb("g1bc", [P, D])
        g2bc = sb("g2bc", [P, F])
        wb1 = sb("wb1", [CH, 2, F], BF16)
        wb2 = sb("wb2", [P, FC, D], BF16)
        wscale = sb("wscale", [P, 2])
        wsinv = sb("wsinv", [P, 2])
        ksm = sb("ksm", [KP + 4, H, MSP], BF16)
        vm = sb("vm", [MS, H, VW])

        G = sb("G", [P, T, D])
        X = sb("X", [P, T, D])
        U = sb("U", [P, T, D])
        HP = sb("HP", [P, T, D])
        HS = sb("HS", [P, T, D])
        st = sb("st", [P, T, 6])
        mv = sb("mv", [P, T, 2])
        rn = sb("rn", [P, T])
        rnn = sb("rnn", [P, T])
        tp = sb("tp", [P, T])
        V = sb("V", [P, T, H, VP], BF16)
        XT = sb("XT", [CH + 1, 2, L])
        big = sb("big", [P, T * F + 4])
        XC = big[0:CH, 0:2 * (L + 2)].rearrange("p (c n) -> p c n", c=2)
        XS = big[0:CH, 2052:2052 + 2 * L].rearrange("p (c n) -> p c n", c=2)
        CUM = big[0:CH, 4100:4100 + 2 * L].rearrange("p (c n) -> p c n", c=2)
        hid = big[:, 0:FC * L].rearrange("p (f n) -> p f n", f=FC)
        BT = big[0:CH, 0:2 * L].rearrange("p (c n) -> p c n", c=2)
        HG = big[:, 0:T * F].rearrange("p (t f) -> p t f", t=T)
        rawq = sb("rawq", [P, H * L // 2])
        QS = rawq[0:KP + 4, :].bitcast(BF16).rearrange("p (h n) -> p h n", h=H)
        Y1 = rawq[0:CH, 0:2 * L].rearrange("p (c n) -> p c n", c=2)
        Z = rawq[0:CH, 2 * L:4 * L].rearrange("p (c n) -> p c n", c=2)
        PSEL = rawq[:, 4 * L:4 * L + T * 2 * QP].rearrange("p (t n) -> p t n", t=T)
        KS = sb("KS", [KP + 4, H, L], BF16)
        QS0 = sb("QS0", [KP + 4, H, 2 * QP], BF16)
        spl0 = sb("spl0", [CH, 3, 2, 2 * QP], BF16)
        acc_out = sb("acc_out", [P, 2, HALF])
        acc0 = acc_out[:, :, 0:3 * 2 * QP]
        RV = acc_out[:, :, 0:2 * D]
        R1 = acc_out[0:CH, :, :]
        spl = sb("spl", [CH, 3, 2, L], BF16)
        splq = big[0:CH, 3 * L:6 * L].bitcast(BF16).rearrange("p (a c n) -> p a c n", a=3, c=2)
        def weights(at, ring, width, dt):
            n = ring * width * (2 if dt is F32 else 1) // 2
            x = big[:, at:at + n]
            return (x if dt is F32 else x.bitcast(BF16)).rearrange("p (r n) -> p r n", r=ring)

        E = weights(0, 2, L, F32)
        EH = weights(2 * L, RING, L, BF16)
        EL = weights(2 * L + RING * L // 2, RING, L, BF16)
        W0 = T * 2 * QP
        E0 = weights(0, 2, W0, F32)
        E0H = weights(2 * W0, 2, W0, BF16)
        E0L = weights(3 * W0, 2, W0, BF16)
        srow = sb("srow", [P, L])
        PT = rawq[:, 0:2 * L].rearrange("p (q n) -> p q n", q=2)
        XQ = rawq[:, 0:768].bitcast(BF16).rearrange("p (t d) -> p t d", t=T)
        XQT = rawq[0:CH, 768:1792].bitcast(BF16).rearrange("p (c n) -> p c n", c=2)
        HQ = rawq[:, 2560:3328].bitcast(BF16)
        HQT = rawq[:, 1792:2560].bitcast(BF16).rearrange("p (t f) -> p t f", t=2)
        NTS = sb("NTS", [CH + 1, 2, 2 * QP])
        CX = sb("CX", [QP, 2, D])
        CXT = sb("CXT", [CH + 1, 2, 2 * QP])
        ATS = sb("ATS", [QP, 2, D])
        sc = sb("sc", [P, T])
        sc1 = sb("sc1", [P, T])
        cnt = sb("cnt", [P, 3, T])
        rank = sb("rank", [P, T])
        notsel = sb("notsel", [P, T])
        junk = sb("junk", [P, L])
        junk2 = sb("junk2", [P, P])
        pool3 = sb("pool3", [CH, 8])
        nmp = sb("nmp", [P, T, 2])
        nm = sb("nm", [P, T, 2])
        vsum = junk2[:, 0:4 * DH].rearrange("p (t d) -> p t d", t=4)
        nms = sb("nms", [P, 2, T, 2, 2], BF16)
        sum0 = HP[0:QP, 0:2, :].rearrange("p t d -> p (t d)")[:, 0:24 * DH].rearrange("p (n d) -> p n d", d=DH)
        rec0 = HP[0:QP, 2, 0:24]
        rec = sb("rec", [P, 2 * T])
        e2 = rawq[:, 3328:3328 + 4 * D].rearrange("p (i t d) -> p i t d", i=2, t=2)
        amax = sb("amax", [P, T])
        qsc = sb("qsc", [P, T])
        qinv = sb("qinv", [P, T])
        gsc = sb("gsc", [P, T])
        ss = sb("ss", [P, T])
        wsum = sb("wsum", [P, 2])
        memt = junk[0:CH + 1, 0:2 * MS].rearrange("p (c n) -> p c n", c=2)
        memn = junk[0:MS, 2 * P:2 * P + D]
        splm = srow[0:CH, 0:3 * MSP].bitcast(BF16).rearrange("p (a c n) -> p a c n", a=3, c=2)

        ST = [pb("ST0", [P, 2 * HALF]), pb("ST1", [P, 2 * HALF])]
        S = [pb("S0", [P, HALF]), pb("S1", [P, HALF])]
        PV = pb("PV", [P, HALF])
        MT = pb("MT", [P, 2 * HALF], BF16)
        MTf = MT[:, :].bitcast(F32)
        ring4 = [ST[0][:, 0:HALF], ST[0][:, HALF:2 * HALF], ST[1][:, 0:HALF], ST[1][:, HALF:2 * HALF]]
        O = [PV[:, :], MTf]

        scr_k = nc.dram_tensor("scr_k", (3, D, L), BF16, kind="Internal").ap()
        scr_q = nc.dram_tensor("scr_q", (3, D, L), BF16, kind="Internal").ap()
        scr_q0 = nc.dram_tensor("scr_q0", (3, D, 2 * QP), BF16, kind="Internal").ap()
        scr_m = nc.dram_tensor("scr_m", (3, D, MSP), BF16, kind="Internal").ap()

        names = """loaded consts tokens gathered stats rstd xnorm turned evac inproj inproj_out conv silu
            gated outproj h1 logit expz score srow_turned srow_copied picks rank_turned pt gathersel nts
            proj hi resid mid lo vproj vcopied units reduced rowmax mturned mcopied plow vlow low0 vhi vres vmid acc0 ctxr accout st0 ex0 pv0 ctx ctxn
            ctxt ctxtc att atts pooled pooledv mixin mixed merged hidden gelu ffn h2 stile exps pv normed
            alpha alphae fusedx fproj h3 quant qturned qcopied bhid bgelu hss hrms hquant hturned hcopied
            bout outs stored vlink plink filled pp pa pd kw0 kw1 kr0 kr1 qw0 qw1 qr0 qr1 q0w q0r mw mr""".split()
        s = {n: sem("s_" + n) for n in names}
        block = ctx.enter_context(nc.Block())

        ovw = out.rearrange("b (t p) d -> b p t d", p=P)

        def cm(w, p=CH):
            return w.rearrange("(c p) n -> p c n", p=p)

        def stack(scr, c, part):
            return scr[part, c * CH:(c + 1) * CH, :].rearrange("(h p) n -> p h n", p=DH)

        PIECES_K0 = [(spl, m, j) for m in range(2) for j in range(NH)]
        PIECES_Q0 = [(spl0, m, 0) for m in range(2)]
        PIECES_1 = [(dst, m, j) for m in range(2) for dst in (spl, splq) for j in range(NH)]
        loads = []

        @block.sync
        def _(sp):
            n = [0]

            def load(dst, src):
                sp.dma_start(dst, src, allow_slow_non_contiguous=True).then_inc(s["loaded"], 16)
                n[0] += 1

            load(win[:], cm(A["L0_attn_W_in"]))
            load(wout[:], cm(A["L0_attn_W_out"]))
            load(convw[:], A["L0_attn_conv_w"].rearrange("(c p) a k -> p c (a k)", p=CH))
            for i, name in enumerate(["L0_attn_conv_b", "L0_attn_D", "L0_ffn_g1", "L0_ffn_b1", "L0_ffn_g2", "L0_ffn_b2"]):
                load(cols[:, :, i], A[name].rearrange("(c p) -> p c", p=CH))
            load(bmat[:], cm(A["L0_attn_B"]))
            load(cmat[:], cm(A["L0_attn_C"]))
            load(wr[0:CH, :, 0], A["L0_ffn_Wr"].rearrange("(c p) -> p c", p=CH))
            load(wr[CH:CH + 1, 1, :], A["L0_ffn_br"].rearrange("(a n) -> a n", a=1))
            for w, wn, bn in ((wq, "L0_ffn_Wq", "L0_ffn_bq"), (wk, "L0_ffn_Wk", "L0_ffn_bk"), (wv, "L0_ffn_Wv", "L0_ffn_bv"),
                              (wo, "L0_ffn_Wo", "L0_ffn_bo"), (wm, "L0_ffn_Wm", "L0_ffn_bm"), (wf1, "L0_ffn_W1", "L0_ffn_bf1"),
                              (wat, "L1_attn_w_attn", "L1_attn_b_attn"), (wal, "L1_attn_w_alpha", "L1_attn_b_alpha"),
                              (wpr, "L1_attn_w_proj", "L1_attn_b_proj")):
                load(w[0:CH, :, :], cm(A[wn]))
                load(w[CH:CH + 1, 1, :], A[bn].rearrange("(a n) -> a n", a=1))
            load(wf2[:], cm(A["L0_ffn_W2"], P))
            load(bf2[:], A["L0_ffn_bf2"].rearrange("(a n) -> a n", a=1))
            load(g1bc[:], A["L1_ffn_g1"].partition_broadcast(P))
            load(g2bc[:], A["L1_ffn_g2"].partition_broadcast(P))
            load(memn, A["L1_attn_memory_features"][0])
            load(XT[0:CH, :, 0:2 * D], cm(A["L1_attn_w_mem"]))
            load(XT[CH:CH + 1, 1, 0:2 * D], A["L1_attn_b_mem"].rearrange("(a n) -> a n", a=1))
            load(X[:, 0:FC, :], cm(A["L1_ffn_w1"], P))
            load(HG[0:CH, 0:2, :], cm(A["L1_ffn_w2"]))
            loads.append(n[0])

            sp.wait_ge(s["pd"], 2)
            for c in range(2):
                sp.dma_start(scr_m[:, c * CH:(c + 1) * CH, :].rearrange("a r n -> r a n"), splm[:, :, c, :]).then_inc(s["mw"], 16)
            sp.wait_ge(s["mw"], 32)
            for c in range(2):
                for j in range(6):
                    sp.dma_start(ksm[DH * j:DH * j + DH, 6 * c:6 * c + 6, :], stack(scr_m, c, K_PARTS[j])).then_inc(s["mr"], 16)

            def restack(b, src, scr, dst, parts, group, kw, kr, uses, use):
                for c in range(2):
                    sp.wait_ge(s["lo"], b * 14 + group + 2 * c + 2)
                    sp.dma_start(scr[:, c * CH:(c + 1) * CH, :].rearrange("a r n -> r a n"), src[:, :, c, :]).then_inc(s[kw[c]], 16)
                for c in range(2):
                    sp.wait_ge(s[kw[c]], (b * uses + use + 1) * 16)
                    for j in range(6):
                        sp.dma_start(dst[DH * j:DH * j + DH, 6 * c:6 * c + 6, :], stack(scr, c, parts[j])).then_inc(s[kr[c]], 16)

            with sp.Fori(0, NB) as b:
                restack(b, spl, scr_k, KS, K_PARTS, 0, ("kw0", "kw1"), ("kr0", "kr1"), 2, 0)
                sp.wait_ge(s["lo"], b * 14 + 6)
                for c in range(2):
                    sp.dma_start(scr_q0[:, c * CH:(c + 1) * CH, :].rearrange("a r n -> r a n"), spl0[:, :, c, :]).then_inc(s["q0w"], 16)
                sp.wait_ge(s["q0w"], b * 32 + 32)
                for c in range(2):
                    for j in range(6):
                        sp.dma_start(QS0[DH * j:DH * j + DH, 6 * c:6 * c + 6, :], stack(scr_q0, c, Q_PARTS[j])).then_inc(s["q0r"], 16)
                for c in range(2):
                    for src, scr, count, w in ((spl, scr_k, 8, ("kw0", "kw1")), (splq, scr_q, 10, ("qw0", "qw1"))):
                        sp.wait_ge(s["lo"], b * 14 + count + 4 * c)
                        sp.dma_start(scr[:, c * CH:(c + 1) * CH, :].rearrange("a r n -> r a n"), src[:, :, c, :]).then_inc(s[w[c]], 16)
                    for scr, dst, parts, w, count, rd in ((scr_k, KS, K_PARTS, ("kw0", "kw1"), b * 32 + 32, ("kr0", "kr1")),
                                                          (scr_q, QS, Q_PARTS, ("qw0", "qw1"), b * 16 + 16, ("qr0", "qr1"))):
                        sp.wait_ge(s[w[c]], count)
                        for j in range(6):
                            sp.dma_start(dst[DH * j:DH * j + DH, 6 * c:6 * c + 6, :], stack(scr, c, parts[j])).then_inc(s[rd[c]], 16)

        LOADED = loads[0] * 16

        @block.gpsimd
        def _(g):
            k = [0]

            def link(ins):
                k[0] += 1
                ins.then_inc(s["plink"], 1)
                g.wait_ge(s["plink"], k[0])

            made = [0]

            def const(ins):
                made[0] += 1
                ins.then_inc(s["consts"], 1)
                g.wait_ge(s["consts"], made[0])

            g.dma_start(tok_i[:], A["x"].rearrange("b (t p) -> p (b t)", p=P), allow_slow_non_contiguous=True).then_inc(s["tokens"], 16)
            link(g.memset(ident[:], 0.0))
            link(g.affine_select(out=ident[:], in_=ident[:], compare_op=ALU.not_equal, fill=1.0, base=0, pattern=[[-1, P]], channel_multiplier=1))
            const(g.tensor_copy(identb[:], ident[:]))
            link(g.memset(earlier[:], 1.0))
            const(g.affine_select(out=earlier[:], in_=earlier[:], compare_op=ALU.is_gt, fill=0.0, base=0, pattern=[[-1, P]], channel_multiplier=1))
            const(g.memset(ones[:], 1.0))
            const(g.memset(neghalf[:], -0.5))
            link(g.iota(slot_i[:], pattern=[[QC, 2], [1, QP]], base=0, channel_multiplier=0))
            const(g.tensor_copy(slot[:], slot_i[:]))
            link(g.iota(rowslot_i[:], pattern=[[QC, 2]], base=0, channel_multiplier=1))
            const(g.tensor_copy(rowslot[:], rowslot_i[:]))
            link(g.memset(vm[:], 0.0))
            const(g.memset(vm[:, :, DH:DH + 1], 1.0))
            const(g.memset(NTS[CH:CH + 1, :, :], 1.0))
            const(g.memset(CXT[CH:CH + 1, :, :], 1.0))
            const(g.memset(junk[CH:CH + 1, 0:2 * MS], 1.0))
            const(g.memset(srow[:], 0.0))
            link(g.memset(QS0[KP:KP + 4, :, :], 0.0))
            const(g.memset(cnt[:], 0.0))

            def rsqrt(dst, src, eps):
                link(g.tensor_scalar(tp[:], src, eps, None, ALU.add))
                return g.tensor_tensor(dst, tp[:], neghalf[:], ALU.pow)

            def inverse_deviation(b, n, second=None):
                g.wait_ge(s["stats"], b * 5 + n + 1)
                ins = rsqrt(rn[:], mv[:, :, 1], LN_EPS)
                if second is None:
                    ins.then_inc(s["rstd"], 1)
                    return
                link(ins)
                link(g.tensor_tensor(tp[:], mv[:, :, 1], rn[:], ALU.mult))
                link(g.tensor_tensor(rnn[:], tp[:], rn[:], ALU.mult))
                link(rsqrt(rnn[:], rnn[:], second))
                g.tensor_tensor(rnn[:], rnn[:], rn[:], ALU.mult).then_inc(s["rstd"], 1)

            for b in range(NB):
                if b == 0:
                    g.wait_ge(s["tokens"], 16)
                else:
                    g.wait_ge(s["h1"], b * 4)
                for t in range(T):
                    g.indirect_dma_start(G[:, t, :], None, A["L0_tok_embed_matrix"][:],
                                         bass.IndirectOffsetOnAxis(ap=tok_i[:, b * T + t:b * T + t + 1], axis=0)).then_inc(s["gathered"], 16)
                inverse_deviation(b, 0)
                inverse_deviation(b, 1, LN_EPS)
                for h in range(H):
                    g.wait_ge(s["ex0"], b * 36 + 3 * h + 3 + 4)
                    g.tensor_tensor(E0L[:, h % 2, :], E0[:, h % 2, :], E0H[:, h % 2, :], ALU.subtract).then_inc(s["low0"], 1)
                inverse_deviation(b, 2)
                inverse_deviation(b, 3)
                for i in range(NSTEP):
                    if i % STEPS < 3:
                        g.wait_ge(s["exps"], b * NSTEP + i + 3)
                        g.tensor_tensor(EL[:, i % RING, :], E[:, cut_of(i)[0] % 2, :], EH[:, i % RING, :], ALU.subtract).then_inc(s["plow"], 1)
                inverse_deviation(b, 4, RMS_EPS)
                g.wait_ge(s["hss"], b * 8 + 8)
                link(g.tensor_scalar(tp[:], ss[:], 1.0 / F, None, ALU.mult))
                rsqrt(rn[:], tp[:], RMS_EPS).then_inc(s["hrms"], 1)

        @block.tensor
        def _(pe):
            pe.wait_ge(s["consts"], 12)
            pe.wait_ge(s["filled"], 3)
            pe.wait_ge(s["loaded"], LOADED)
            for c in range(2):
                nc.tensor.transpose(S[0][0:CH, c * P:c * P + MS], memn[:, c * CH:(c + 1) * CH], ident[0:MS, 0:MS]).then_inc(s["pp"], 1)
            pe.wait_ge(s["pa"], 1)
            for m in range(2):
                for c in range(2):
                    r = CH + c
                    ins = nc.tensor.matmul(S[1][0:CH, m * P:m * P + MS], XT[0:r, c, m * CH:(m + 1) * CH], memt[0:r, c, :], start=c == 0, stop=c == 1)
            ins.then_inc(s["pp"], 1)
            for c in range(2):
                ins = nc.tensor.matmul(ST[0][0:MS, 0:D], memt[0:CH + c, c, :], XT[0:CH + c, c, D:2 * D], start=c == 0, stop=c == 1)
            ins.then_inc(s["pp"], 1)
            pe.wait_ge(s["pd"], 3)
            nc.tensor.matmul(PV[:, 0:1], ones[:], wsum[:, 0:1], start=True, stop=True)
            nc.tensor.matmul(PV[:, 1:2], ones[0:CH, :], wsum[0:CH, 1:2], start=True, stop=True).then_inc(s["pp"], 1)
            pe.wait_ge(s["pd"], 5)
            t1 = ST[1][:, 0:HALF].bitcast(BF16)
            t2 = ST[1][:, HALF:2 * HALF].bitcast(BF16)
            t3 = [ST[0][:, 0:HALF].bitcast(BF16), ST[0][:, HALF:2 * HALF].bitcast(BF16)]
            pe.wait_ge(s["pa"], 3)
            for f in range(FC):
                for c in range(2):
                    nc.tensor.transpose((t1, t2)[c][0:CH, f * P:(f + 1) * P], XQ[:, f, c * CH:(c + 1) * CH], identb[:])
            for f in range(FC):
                for c in range(2):
                    ins = nc.tensor.transpose(t3[f // 3][:, (f % 3) * D + c * CH:(f % 3) * D + (c + 1) * CH], HQT[0:CH, c, f * P:(f + 1) * P], identb[0:CH, 0:CH])
            ins.then_inc(s["pp"], 1)
            pe.wait_ge(s["pa"], 4)

            def turn(b, job, src, ready, counts):
                for i in range(4):
                    half, c = i // 2, i % 2
                    if c == 0:
                        pe.wait_ge(s[ready], b * counts[0] + counts[1 + half])
                    pe.wait_ge(s["evac"], b * 28 + 4 * job + i + 1)
                    for t in range(4):
                        ins = nc.tensor.transpose(S[i % 2][0:CH, t * P:(t + 1) * P], src[:, 4 * half + t, c * CH:(c + 1) * CH], ident[:])
                    ins.then_inc(s["turned"], 1)

            def rows(dst, lhs, w, cs, bias):
                n = len(cs)
                for i, (x, wt, c) in enumerate(cs):
                    r = CH + (1 if bias and c == 1 else 0)
                    ins = nc.tensor.matmul(dst, x[0:r], wt[0:r], start=i == 0, stop=i == n - 1)
                return ins

            def project(b, group, w, off, src, width, spans, chunks=(0, 1)):
                i = group
                for m in chunks:
                    for j in range(spans):
                        if i >= 4:
                            pe.wait_ge(s["resid"], b * 14 + i - 3)
                        for c in range(2):
                            r = CH + c
                            ins = nc.tensor.matmul(ring4[i % 4][0:CH, 0:width], w[0:r, c, off + m * CH:off + (m + 1) * CH],
                                                   src[0:r, c, j * width:(j + 1) * width], start=c == 0, stop=c == 1)
                        ins.then_inc(s["proj"], 1)
                        i += 1

            def values(b, use, w, off):
                for i in range(4):
                    n = 4 * use + i
                    if i >= 2:
                        pe.wait_ge(s["vres"], b * 8 + n - 1)
                    for t in (2 * i, 2 * i + 1):
                        for c in range(2):
                            r = CH + c
                            ins = nc.tensor.matmul(O[i % 2][:, (t % 2) * D:(t % 2 + 1) * D], XT[0:r, c, t * P:(t + 1) * P],
                                                   w[0:r, c, off:off + D], start=c == 0, stop=c == 1)
                    ins.then_inc(s["vproj"], 1)

            with pe.Fori(0, NB) as b:
                turn(b, 0, X, "xnorm", (8, 1, 2))
                pe.wait_ge(s["evac"], b * 28 + 4 + 2)
                for i in range(8):
                    m, half = i // 2, i % 2
                    if i >= 4:
                        pe.wait_ge(s["inproj_out"], b * 8 + i - 3)
                    for c in range(2):
                        ins = nc.tensor.matmul(ring4[i % 4][0:CH, :], win[:, c, m * CH:(m + 1) * CH], XT[0:CH, c, half * HALF:(half + 1) * HALF],
                                               start=c == 0, stop=c == 1)
                    ins.then_inc(s["inproj"], 1)
                pe.wait_ge(s["gated"], b * 2 + 2)
                for i in range(4):
                    if i >= 2:
                        pe.wait_ge(s["h1"], b * 4 + i - 1)
                    for t in (2 * i, 2 * i + 1):
                        for c in range(2):
                            ins = nc.tensor.matmul(O[i % 2][:, (t % 2) * D:(t % 2 + 1) * D], CUM[:, c, t * P:(t + 1) * P], wout[:, c, :],
                                                   start=c == 0, stop=c == 1)
                    ins.then_inc(s["outproj"], 1)
                turn(b, 1, X, "xnorm", (8, 3, 4))
                pe.wait_ge(s["evac"], b * 28 + 8 + 2)
                for t in range(T):
                    for c in range(2):
                        r = CH + c
                        ins = nc.tensor.matmul(PV[:, t:t + 1], XT[0:r, c, t * P:(t + 1) * P], wr[0:r, c, :], start=c == 0, stop=c == 1)
                ins.then_inc(s["logit"], 1)
                project(b, 0, wk, 0, XT, HALF, 2)
                pe.wait_ge(s["score"], b * 1 + 1)
                for t in range(T):
                    if t == 0:
                        pe.wait_ge(s["resid"], b * 14 + 4)
                    ins = nc.tensor.transpose(ST[0][:, t * P:(t + 1) * P], sc[:, t:t + 1].to_broadcast([P, P]), ident[:])
                ins.then_inc(s["srow_turned"], 1)
                for j in range(3):
                    for t in range(T):
                        lhs = X[:, t, j * CH:(j + 1) * CH] if j < 2 else ones[:, 0:CH]
                        ins = nc.tensor.matmul(ST[1][0:CH, j:j + 1], lhs, sc[:, t:t + 1], start=t == 0, stop=t == T - 1)
                ins.then_inc(s["pooled"], 1)
                pe.wait_ge(s["picks"], b * 2 + 1)
                pe.wait_ge(s["srow_copied"], b * 1 + 1)
                for t in range(T):
                    ins = nc.tensor.transpose(ST[0][:, t * P:(t + 1) * P], rank[:, t:t + 1].to_broadcast([P, P]), ident[:])
                ins.then_inc(s["rank_turned"], 1)
                pe.wait_ge(s["picks"], b * 2 + 2)
                for c in range(2):
                    for t in range(T):
                        ins = nc.tensor.matmul(S[0][0:CH, c * 2 * QP:(c + 1) * 2 * QP], X[:, t, c * CH:(c + 1) * CH], PSEL[:, t, :],
                                               start=t == 0, stop=t == T - 1)
                ins.then_inc(s["gathersel"], 1)
                pe.wait_ge(s["nts"], b * 2 + 2)
                pe.wait_ge(s["pt"], b * 1 + 1)
                project(b, 4, wq, 0, NTS, 2 * QP, 1)
                values(b, 0, wv, 0)

                def units0(h, us):
                    for u in us:
                        n = 4 * h + u
                        pe.wait_ge(s["reduced"], b * NUNITS + n + 1)
                        nc.tensor.matmul(S[n % 2][0:QP, :], QS0[0:KP, h, (u // 2) * QP:(u // 2 + 1) * QP],
                                         KS[0:KP, h, (u % 2) * HALF:(u % 2 + 1) * HALF], start=True, stop=True).then_inc(s["units"], 1)

                def maxrow0(h):
                    pe.wait_ge(s["rowmax"], b * 24 + h + 1)
                    pe.wait_ge(s["mcopied"], b * 24 + h + 1)
                    for q in range(2):
                        ins = nc.tensor.transpose(MT[KP:KP + 2, q * QP:(q + 1) * QP], nms[0:QP, h % 2, q, 0, :], identb[0:QP, 0:QP])
                    ins.then_inc(s["mturned"], 1)

                def exps0(h):
                    pe.wait_ge(s["mcopied"], b * 24 + h + 2)
                    for i in range(3):
                        n = 3 * h + i
                        pe.wait_ge(s["ex0"], b * 36 + n + 1)
                        for kt in range(3 * i, min(3 * i + 3, T)):
                            ins = nc.tensor.matmul(ring4[n % 4][:, (kt - 3 * i) * 2 * QP:(kt - 3 * i + 1) * 2 * QP], KS[0:KP + 2, h, kt * P:(kt + 1) * P],
                                                   QS0[0:KP + 2, h, :], start=True, stop=True)
                        ins.then_inc(s["st0"], 1)

                def pv0(h):
                    pe.wait_ge(s["low0"], b * H + h + 1)
                    if h == H // 2:
                        pe.wait_ge(s["acc0"], b * 2 + 1)
                    o = PV[h // 3 % 2 * VP:(h // 3 % 2 + 1) * VP, (h % 3) * 2 * QP:(h % 3 + 1) * 2 * QP]
                    for kt in range(T):
                        for part in (E0H, E0L):
                            ins = nc.tensor.matmul(o, V[:, kt, h, :], part[:, h % 2, kt * 2 * QP:(kt + 1) * 2 * QP],
                                                   start=kt == 0 and part is E0H, stop=kt == T - 1 and part is E0L)
                    ins.then_inc(s["pv0"], 1)

                pe.wait_ge(s["q0r"], b * 192 + 192)
                pe.wait_ge(s["kr0"], b * 192 + 96)
                pe.wait_ge(s["vcopied"], b * 8 + 4)
                pe.wait_ge(s["resid"], b * 14 + 6)
                units0(0, range(4))
                units0(1, range(2))
                maxrow0(0)
                units0(1, range(2, 4))
                for h in range(H):
                    exps0(h)
                    if h + 2 == 6:
                        pe.wait_ge(s["kr1"], b * 192 + 96)
                    if h + 2 < H:
                        units0(h + 2, range(2))
                    if h + 1 < H:
                        maxrow0(h + 1)
                    if h + 2 < H:
                        units0(h + 2, range(2, 4))
                    if h >= 1:
                        pv0(h - 1)
                pv0(H - 1)
                pe.wait_ge(s["acc0"], b * 2 + 2)
                for n in range(12):
                    g, j, q = n // 6, n // 2 % 3, n % 2
                    ins = nc.tensor.transpose(ST[n // 8][0:QP, n % 8 * P:(n % 8 + 1) * P], acc0[:, g, j * 2 * QP + q * QP:j * 2 * QP + (q + 1) * QP], ident[:])
                ins.then_inc(s["ctxr"], 1)
                pe.wait_ge(s["ctxn"], b * 1 + 1)
                for c in range(2):
                    for q in range(2):
                        ins = nc.tensor.transpose(ST[0][0:CH, (2 * c + q) * QP:(2 * c + q + 1) * QP], CX[:, q, c * CH:(c + 1) * CH], ident[0:QP, 0:QP])
                ins.then_inc(s["ctxt"], 1)
                pe.wait_ge(s["ctxtc"], b * 1 + 1)
                for q in range(2):
                    for c in range(2):
                        r = CH + c
                        ins = nc.tensor.matmul(ST[1][0:QP, q * D:(q + 1) * D], CXT[0:r, c, q * QP:(q + 1) * QP], wo[0:r, c, :], start=c == 0, stop=c == 1)
                ins.then_inc(s["att"], 1)
                pe.wait_ge(s["mixin"], b * 2 + 2)
                pe.wait_ge(s["atts"], b * 1 + 1)
                for t in range(T):
                    if t >= 2:
                        pe.wait_ge(s["merged"], b * 8 + t - 1)
                    o = O[t % 2]
                    for c in range(2):
                        r = CH + c
                        nc.tensor.matmul(o[:, 0:D], XT[0:r, c, t * P:(t + 1) * P], wm[0:r, c, :], start=c == 0, stop=c == 1)
                    for q in range(2):
                        ins = nc.tensor.matmul(o[:, D:2 * D], PT[0:QC, q, t * P:(t + 1) * P], ATS[0:QC, q, :], start=q == 0, stop=q == 1)
                    ins.then_inc(s["mixed"], 1)
                turn(b, 2, X, "xnorm", (8, 5, 6))
                pe.wait_ge(s["evac"], b * 28 + 12 + 2)
                for half in range(NH):
                    for f in range(FC):
                        i = half * FC + f
                        if i >= 4:
                            pe.wait_ge(s["gelu"], b * 12 + i - 3)
                        for c in range(2):
                            r = CH + c
                            ins = nc.tensor.matmul(ring4[i % 4], wf1[0:r, c, f * P:(f + 1) * P], XT[0:r, c, half * HALF:(half + 1) * HALF], start=c == 0, stop=c == 1)
                        ins.then_inc(s["hidden"], 1)
                for i in range(4):
                    pe.wait_ge(s["gelu"], b * 12 + (6 if i < 2 else 12))
                    if i >= 2:
                        pe.wait_ge(s["h2"], b * 4 + i - 1)
                    for t in (2 * i, 2 * i + 1):
                        o = O[i % 2][:, (t % 2) * D:(t % 2 + 1) * D]
                        for f in range(FC):
                            nc.tensor.matmul(o, hid[:, f, t * P:(t + 1) * P], wf2[:, f, :], start=f == 0, stop=False)
                        ins = nc.tensor.matmul(o, ones[0:1, :], bf2[:], start=False, stop=True)
                    ins.then_inc(s["ffn"], 1)
                turn(b, 3, X, "xnorm", (8, 7, 8))
                pe.wait_ge(s["evac"], b * 28 + 16 + 2)
                for c in range(2):
                    project(b, 6 + 4 * c, wat, D, XT, HALF, 2, (c,))
                    project(b, 8 + 4 * c, wat, 0, XT, HALF, 2, (c,))
                values(b, 1, wat, 2 * D)

                def unit(what):
                    n = UNIT_AT[what]
                    kind, h, u = what
                    if kind == "ctx":
                        pe.wait_ge(s["accout"], b * 2 * H + 2 * h + u + 1)
                    pe.wait_ge(s["reduced"], b * NUNITS + n + 1)
                    if kind == "ctx":
                        for t in range(4):
                            ins = nc.tensor.transpose(S[n % 2][:, t * P:(t + 1) * P], acc_out[:, u, t * P:(t + 1) * P], ident[:])
                    elif u < 16:
                        ins = nc.tensor.matmul(S[n % 2][:, :], QS[0:KP, h, (u // 2) * P:(u // 2 + 1) * P], KS[0:KP, h, (u % 2) * HALF:(u % 2 + 1) * HALF],
                                               start=True, stop=True)
                    else:
                        for t in range(4):
                            qt = 4 * (u - 16) + t
                            ins = nc.tensor.matmul(S[n % 2][:, t * MSP:t * MSP + MS], QS[0:KP, h, qt * P:(qt + 1) * P], ksm[0:KP, h, 0:MS], start=True, stop=True)
                    ins.then_inc(s["units"], 1)

                def maxrow(h):
                    pe.wait_ge(s["rowmax"], b * 24 + 12 + h + 1)
                    pe.wait_ge(s["mcopied"], b * 24 + 12 + h + 1)
                    for t in range(T):
                        ins = nc.tensor.transpose(MT[KP:KP + 4, t * P:(t + 1) * P], nms[:, h % 2, t, :, :].rearrange("p a c -> p (a c)"), identb[:])
                    ins.then_inc(s["mturned"], 1)

                def scores(i):
                    h, half, k = i // 10, i // 5 % 2, i % 5
                    pe.wait_ge(s["exps"], b * NSTEP + i + 1)
                    if i % 10 == 0:
                        pe.wait_ge(s["mcopied"], b * 24 + 12 + h + 2)
                    queries = QS[0:KP + 4, h, half * HALF:(half + 1) * HALF]
                    if k < 4:
                        for kt in (2 * k, 2 * k + 1):
                            ins = nc.tensor.matmul(ST[i % 2][:, (kt % 2) * HALF:(kt % 2 + 1) * HALF], KS[0:KP + 4, h, kt * P:(kt + 1) * P], queries, start=True, stop=True)
                    else:
                        ins = nc.tensor.matmul(ST[i % 2][0:MS, 0:HALF], ksm[0:KP + 4, h, 0:MS], queries, start=True, stop=True)
                    ins.then_inc(s["stile"], 1)

                def weigh(i):
                    h, k = i // 10, i % STEPS
                    if k < 4:
                        which, count = lows(i)
                        pe.wait_ge(s[which], b * LOWS[which] + count)
                    else:
                        pe.wait_ge(s["exps"], b * NSTEP + i + 3)
                    if k == 0 and i:
                        pe.wait_ge(s["accout"], b * 2 * H + i // STEPS)
                    if k < 4:
                        for kt in (2 * k, 2 * k + 1):
                            for part in (EH, EL):
                                ins = nc.tensor.matmul(PV[0:VP, :], V[:, kt, h, :], part[:, i % RING, (kt % 2) * HALF:(kt % 2 + 1) * HALF],
                                                       start=kt == 0 and part is EH, stop=kt == T - 1 and part is EL)
                    else:
                        ins = nc.tensor.matmul(PV[VP:VP + VW, :], vm[:, h, :], EH[0:MS, i % RING, :].bitcast(F32), start=True, stop=True)
                    ins.then_inc(s["pv"], 1)

                pe.wait_ge(s["kr0"], b * 192 + 192)
                pe.wait_ge(s["qr0"], b * 96 + 96)
                pe.wait_ge(s["vcopied"], b * 8 + 8)
                pe.wait_ge(s["mr"], 192)
                pe.wait_ge(s["resid"], b * 14 + 14)
                for what in FIRST_UNITS:
                    unit(what)
                maxrow(0)
                for i in range(NSTEP):
                    h, j = i // 10, i % 10
                    if h + 2 == 6 and j == 0:
                        pe.wait_ge(s["kr1"], b * 192 + 192)
                        pe.wait_ge(s["qr1"], b * 96 + 96)
                    units = STEP_UNITS[i]
                    first = [what for what in units[0:1] if what[0] == "max"]
                    for what in first:
                        unit(what)
                    scores(i)
                    second = [what for what in units[1:2] if what[0] == "max"]
                    for what in second:
                        unit(what)
                    if i >= LAG:
                        weigh(i - LAG)
                    for what in units[len(first + second):]:
                        unit(what)
                    if j == MAX_AT and h + 1 < H:
                        maxrow(h + 1)
                for i in range(NSTEP - LAG, NSTEP):
                    weigh(i)
                unit(LAST_UNITS[0])
                turn(b, 4, U, "reduced", (NUNITS, NUNITS + 2, NUNITS + 2))
                turn(b, 5, HP, "reduced", (NUNITS, NUNITS + 2, NUNITS + 2))
                pe.wait_ge(s["evac"], b * 28 + 24 + 2)
                for i in range(4):
                    if i >= 2:
                        pe.wait_ge(s["alphae"], b * 4 + i - 1)
                    for t in (2 * i, 2 * i + 1):
                        o = O[i % 2][:, (t % 2) * D:(t % 2 + 1) * D]
                        for c in range(4):
                            r = CH + (1 if c == 1 else 0)
                            x = XT[0:r, c, t * P:(t + 1) * P] if c < 2 else BT[:, c - 2, t * P:(t + 1) * P]
                            ins = nc.tensor.matmul(o, x, wal[0:r, c, :], start=c == 0, stop=c == 3)
                    ins.then_inc(s["alpha"], 1)
                turn(b, 6, X, "fusedx", (4, 2, 4))
                pe.wait_ge(s["evac"], b * 28 + 28 + 2)
                for i in range(4):
                    if i >= 2:
                        pe.wait_ge(s["h3"], b * 4 + i - 1)
                    for t in (2 * i, 2 * i + 1):
                        for c in range(2):
                            r = CH + c
                            ins = nc.tensor.matmul(O[i % 2][:, (t % 2) * D:(t % 2 + 1) * D], XT[0:r, c, t * P:(t + 1) * P], wpr[0:r, c, :], start=c == 0, stop=c == 1)
                    ins.then_inc(s["fproj"], 1)
                for i in range(4):
                    half, c = i // 2, i % 2
                    pe.wait_ge(s["quant"], b * 8 + 4 * half + 4)
                    if i >= 2:
                        pe.wait_ge(s["qcopied"], b * 4 + i - 1)
                    sb16 = S[i % 2][:, :].bitcast(BF16)
                    for t in range(4):
                        ins = nc.tensor.transpose(sb16[0:CH, t * P:(t + 1) * P], XQ[:, 4 * half + t, c * CH:(c + 1) * CH], identb[:])
                    ins.then_inc(s["qturned"], 1)
                pe.wait_ge(s["qcopied"], b * 4 + 4)
                for t in range(T):
                    if t >= 2:
                        pe.wait_ge(s["bgelu"], b * 8 + t - 1)
                    for n0, n1 in ((0, HALF), (HALF, F)):
                        for c in range(2):
                            ins = nc.tensor.matmul(ST[t % 2][:, n0:n1], XQT[:, c, t * P:(t + 1) * P], wb1[:, c, n0:n1], start=c == 0, stop=c == 1)
                    ins.then_inc(s["bhid"], 1)
                def down(t):
                    pe.wait_ge(s["hcopied"], b * 8 + t + 1)
                    if t >= 4:
                        pe.wait_ge(s["outs"], b * 4 + t // 2 - 1)
                    for f in range(FC):
                        ins = nc.tensor.matmul(O[(t // 2) % 2][:, (t % 2) * D:(t % 2 + 1) * D], HQT[:, t % 2, f * P:(f + 1) * P], wb2[:, f, :], start=f == 0, stop=f == FC - 1)
                    ins.then_inc(s["bout"], 1)

                for t in range(T):
                    pe.wait_ge(s["hquant"], b * 8 + t + 1)
                    if t >= 2:
                        pe.wait_ge(s["hcopied"], b * 8 + t - 1)
                    sb16 = S[t % 2][:, :].bitcast(BF16)
                    for f in range(FC):
                        ins = nc.tensor.transpose(sb16[:, f * P:(f + 1) * P], HQ[:, (t % 2) * F + f * P:(t % 2) * F + (f + 1) * P], identb[:])
                    ins.then_inc(s["hturned"], 1)
                    if t >= 1:
                        down(t - 1)
                down(T - 1)

        @block.scalar
        def _(act):
            A_ = nc.scalar.activation
            act.wait_ge(s["consts"], 12)
            act.wait_ge(s["filled"], 3)
            act.wait_ge(s["pp"], 2)
            A_(memt[0:CH, :, :], S[0][0:CH, 0:2 * P].rearrange("p (c n) -> p c n", c=2)[:, :, 0:MS], ACT.Copy).then_inc(s["pa"], 1)
            act.wait_ge(s["pp"], 3)
            A_(splm[:, 0, :, 0:MS], S[1][0:CH, 0:2 * P].rearrange("p (c n) -> p c n", c=2)[:, :, 0:MS], ACT.Copy).then_inc(s["hi"], 1)
            act.wait_ge(s["pp"], 4)
            A_(vm[:, :, 0:DH], ST[0][0:MS, 0:D].rearrange("p (h d) -> p h d", h=H), ACT.Copy).then_inc(s["pa"], 1)
            act.wait_ge(s["pd"], 1)
            A_(splm[:, 1, :, 0:MS], R1[:, 0, 0:2 * MSP].rearrange("p (c n) -> p c n", c=2)[:, :, 0:MS], ACT.Copy).then_inc(s["pa"], 1)
            act.wait_ge(s["pp"], 6)
            A_(wb1[:, 0, :], ST[1][0:CH, 0:HALF].bitcast(BF16)[:, 0:F], ACT.Copy)
            A_(wb1[:, 1, :], ST[1][0:CH, HALF:2 * HALF].bitcast(BF16)[:, 0:F], ACT.Copy)
            A_(wb2[:, 0:3, :], ST[0][:, 0:HALF].bitcast(BF16)[:, 0:3 * D].rearrange("p (f d) -> p f d", f=3), ACT.Copy)
            A_(wb2[:, 3:6, :], ST[0][:, HALF:2 * HALF].bitcast(BF16)[:, 0:3 * D].rearrange("p (f d) -> p f d", f=3), ACT.Copy).then_inc(s["evac"], 2)

            def evac(b, job, dst, scale=None, bias=None):
                for i in range(4):
                    half, c = i // 2, i % 2
                    act.wait_ge(s["turned"], b * 28 + 4 * job + i + 1)
                    o = dst[0:CH, c, half * HALF:(half + 1) * HALF]
                    if scale is None:
                        ins = A_(o, S[i % 2][0:CH, :], ACT.Copy)
                    else:
                        ins = A_(o, S[i % 2][0:CH, :], ACT.Identity, scale=cols[:, c, scale:scale + 1], bias=cols[:, c, bias:bias + 1])
                    ins.then_inc(s["evac"], 1)

            def cut(b, group, pieces, width):
                def mid(i):
                    dst, m, j = pieces[i - group]
                    act.wait_ge(s["resid"], b * 14 + i + 1)
                    A_(dst[:, 1, m, j * width:(j + 1) * width], R1[:, i % 2, 0:width], ACT.Copy).then_inc(s["mid"], 1)
                for i in range(group, group + len(pieces)):
                    dst, m, j = pieces[i - group]
                    act.wait_ge(s["proj"], b * 14 + i + 1)
                    A_(dst[:, 0, m, j * width:(j + 1) * width], ring4[i % 4][0:CH, 0:width], ACT.Copy).then_inc(s["hi"], 1)
                    if i > group:
                        mid(i - 1)
                mid(group + len(pieces) - 1)

            def vcut(b, use):
                def heads(x):
                    return x.rearrange("p (t h d) -> p t h d", t=2, h=H)

                def mid(i):
                    act.wait_ge(s["vres"], b * 8 + 4 * use + i + 1)
                    A_(V[:, 2 * i:2 * i + 2, :, DH:2 * DH], heads(RV[:, i % 2, :]), ACT.Copy).then_inc(s["vmid"], 1)
                for i in range(4):
                    act.wait_ge(s["vproj"], b * 8 + 4 * use + i + 1)
                    A_(V[:, 2 * i:2 * i + 2, :, 0:DH], heads(O[i % 2][:, 0:2 * D]), ACT.Copy).then_inc(s["vhi"], 1)
                    if i:
                        mid(i - 1)
                mid(3)

            act.wait_ge(s["mw"], 32)
            with act.Fori(0, NB) as b:
                evac(b, 0, XT)
                for i in range(8):
                    m, half = i // 2, i % 2
                    act.wait_ge(s["inproj"], b * 8 + i + 1)
                    if m < 2:
                        A_(XC[:, m, 2 + half * HALF:2 + (half + 1) * HALF], ring4[i % 4][0:CH, :], ACT.Copy).then_inc(s["inproj_out"], 1)
                    else:
                        A_(Z[:, m - 2, half * HALF:(half + 1) * HALF], ring4[i % 4][0:CH, :], ACT.Silu).then_inc(s["inproj_out"], 1)
                for c in range(2):
                    act.wait_ge(s["conv"], b * 2 + c + 1)
                    A_(XS[:, c, :], Y1[:, c, :], ACT.Silu).then_inc(s["silu"], 1)
                evac(b, 1, XT, 2, 3)
                act.wait_ge(s["logit"], b + 1)
                A_(sc1[:], PV[:, 0:T], ACT.Exp, scale=-1.0).then_inc(s["expz"], 1)
                cut(b, 0, PIECES_K0, HALF)
                act.wait_ge(s["srow_turned"], b + 1)
                A_(srow[:], ST[0][:, :], ACT.Copy).then_inc(s["srow_copied"], 1)
                act.wait_ge(s["gathersel"], b + 1)
                for c in range(2):
                    A_(NTS[0:CH, c, :], S[0][0:CH, c * 2 * QP:(c + 1) * 2 * QP], ACT.Identity, scale=cols[:, c, 2:3], bias=cols[:, c, 3:4]).then_inc(s["nts"], 1)
                cut(b, 4, PIECES_Q0, 2 * QP)
                vcut(b, 0)

                def mcopy0(h):
                    act.wait_ge(s["mturned"], b * 24 + h + 1)
                    A_(QS0[KP:KP + 2, h, :], MT[KP:KP + 2, 0:2 * QP], ACT.Copy).then_inc(s["mcopied"], 1)

                def sums0(g):
                    act.wait_ge(s["pv0"], b * H + (g + 1) * H // 2 + 2)
                    A_(acc0[:, g, :], PV[:, 0:3 * 2 * QP], ACT.Copy).then_inc(s["acc0"], 1)

                mcopy0(0)
                for h in range(H):
                    for i in range(3):
                        n = 3 * h + i
                        w = (3 if i < 2 else 2) * 2 * QP
                        act.wait_ge(s["st0"], b * 36 + n + 1)
                        act.wait_ge(s["pv0"], b * H + h + 1)
                        if h >= 2:
                            act.wait_ge(s["low0"], b * H + h - 1)
                        A_(E0H[:, h % 2, i * 6 * QP:i * 6 * QP + w], ring4[n % 4][:, 0:w], ACT.Exp, scale=float(DH) ** -0.5)
                        A_(E0[:, h % 2, i * 6 * QP:i * 6 * QP + w], ring4[n % 4][:, 0:w], ACT.Exp, scale=float(DH) ** -0.5).then_inc(s["ex0"], 1)
                    if h + 1 < H:
                        mcopy0(h + 1)
                    if h == H // 2:
                        sums0(0)
                sums0(1)
                act.wait_ge(s["ctxt"], b + 1)
                A_(CXT[0:CH, :, :], ST[0][0:CH, 0:4 * QP].rearrange("p (c n) -> p c n", c=2), ACT.Copy).then_inc(s["ctxtc"], 1)
                act.wait_ge(s["att"], b + 1)
                A_(ATS[:, :, :], ST[1][0:QP, 0:2 * D].rearrange("p (q d) -> p q d", q=2), ACT.Copy).then_inc(s["atts"], 1)
                evac(b, 2, XT, 4, 5)
                for i in range(12):
                    act.wait_ge(s["hidden"], b * 12 + i + 1)
                    A_(hid[:, i % FC, (i // FC) * HALF:(i // FC + 1) * HALF], ring4[i % 4], ACT.Gelu).then_inc(s["gelu"], 1)
                evac(b, 3, XT)
                act.wait_ge(s["kw0"], (b * 2 + 1) * 16)
                act.wait_ge(s["kw1"], (b * 2 + 1) * 16)
                cut(b, 6, PIECES_1, HALF)
                vcut(b, 1)

                def out_sums(j):
                    act.wait_ge(s["pv"], b * NSTEP + STEPS * (j + 1) + RING)
                    if j >= 2:
                        act.wait_ge(s["units"], b * NUNITS + UNIT_AT["ctx", (j - 2) // 2, j % 2] + 1)
                    A_(acc_out[:, j % 2, :], PV[:, :], ACT.Copy).then_inc(s["accout"], 1)

                act.wait_ge(s["qw0"], b * 16 + 16)
                act.wait_ge(s["qw1"], b * 16 + 16)
                for i in range(NSTEP):
                    h, k = i // 10, i % STEPS
                    act.wait_ge(s["stile"], b * NSTEP + i + 1)
                    act.wait_ge(s["pv"], b * NSTEP + i + 1)
                    if k < 4:
                        A_(EH[:, i % RING, :], ST[i % 2][:, :], ACT.Exp)
                        if k == SUMS_AT and i > STEPS:
                            out_sums(i // STEPS - 1)
                        cut = cut_of(i)[0]
                        if cut >= 2:
                            which, count = lows(step_of(cut - 2))
                            act.wait_ge(s[which], b * LOWS[which] + count)
                        A_(E[:, cut % 2, :], ST[i % 2][:, :], ACT.Exp).then_inc(s["exps"], 1)
                    else:
                        A_(EH[0:MS, i % RING, :].bitcast(F32), ST[i % 2][0:MS, 0:HALF], ACT.Exp).then_inc(s["exps"], 1)
                out_sums(2 * H - 1)
                evac(b, 4, XT)
                evac(b, 5, BT)
                for i in range(4):
                    act.wait_ge(s["alpha"], b * 4 + i + 1)
                    if i >= 2:
                        act.wait_ge(s["fusedx"], b * 4 + i - 1)
                    A_(e2[:, i % 2, :, :], O[i % 2][:, 0:2 * D].rearrange("p (t d) -> p t d", t=2), ACT.Exp, scale=-1.0).then_inc(s["alphae"], 1)
                evac(b, 6, XT)
                for i in range(4):
                    half, c = i // 2, i % 2
                    act.wait_ge(s["qturned"], b * 4 + i + 1)
                    A_(XQT[:, c, half * HALF:(half + 1) * HALF], S[i % 2][0:CH, :].bitcast(BF16)[:, 0:HALF], ACT.Copy).then_inc(s["qcopied"], 1)
                for t in range(T):
                    act.wait_ge(s["bhid"], b * 8 + t + 1)
                    A_(HG[:, t, :], ST[t % 2][:, 0:F], ACT.Gelu, scale=gsc[:, t:t + 1]).then_inc(s["bgelu"], 1)
                    act.wait_ge(s["bgelu"], b * 8 + t + 1)
                    if t >= 1:
                        act.wait_ge(s["hss"], b * 8 + t)
                    A_(junk[:, 0:F], HG[:, t, :], ACT.Square, accum_out=ss[:, t:t + 1]).then_inc(s["hss"], 1)
                for t in range(T):
                    act.wait_ge(s["hturned"], b * 8 + t + 1)
                    if t >= 2:
                        act.wait_ge(s["bout"], b * 8 + t - 1)
                    A_(HQT[:, t % 2, :], S[t % 2][:, :].bitcast(BF16)[:, 0:F], ACT.Copy).then_inc(s["hcopied"], 1)
                act.wait_ge(s["outs"], b * 4 + 4)
                act.dma_start(ovw[b], HS[:, :, :]).then_inc(s["stored"], 16)
            act.wait_ge(s["stored"], NB * 16 + 16)

        @block.vector
        def _(ve):
            v = nc.vector
            k = [0]
            at = {"b": None, "base": 0}

            def link(ins):
                k[0] += 1
                ins.then_inc(s["vlink"], 1)
                if at["b"] is None:
                    ve.wait_ge(s["vlink"], k[0])
                else:
                    ve.wait_ge(s["vlink"], at["b"] * VEC_LINKS + at["base"] + k[0])

            v.memset(nmp[:], 0.0).then_inc(s["reduced"], 2)
            v.memset(nms[:].rearrange("p a t c d -> p (a t c d)"), 0.0).then_inc(s["mcopied"], 1)
            v.memset(rec[:], 0.0).then_inc(s["ex0"], 4)
            v.memset(e2[:, 0, 0, 0:8], 0.0).then_inc(s["exps"], 2)
            v.memset(e2[:, 0, 0, 8:16], 0.0).then_inc(s["pv"], RING)
            v.memset(e2[:, 0, 0, 16:24], 0.0).then_inc(s["pv0"], 2)
            v.memset(CX[:, 0, 0:8], 0.0).then_inc(s["stored"], 16)
            link(v.memset(V[:], 0.0))
            v.memset(V[:, :, :, VONE:VONE + 1], 1.0).then_inc(s["filled"], 1)
            link(v.memset(KS[KP:KP + 4, :, :], 0.0))
            v.memset(KS[KP:KP + 2, :, :], 1.0).then_inc(s["filled"], 1)
            link(v.memset(ksm[KP:KP + 4, :, :], 1.0))
            v.memset(ksm[KP:KP + 2, :, :], 0.0).then_inc(s["filled"], 1)
            ve.wait_ge(s["filled"], 3)
            ve.wait_ge(s["consts"], 12)
            ve.wait_ge(s["loaded"], LOADED)
            link(v.memset(PV[:, :], 0.0))
            link(v.tensor_tensor(bmat[:], bmat[:], cmat[:], ALU.mult))
            link(v.tensor_reduce(cols[:, :, 6], bmat[:], AX.X, ALU.add))
            ve.wait_ge(s["hi"], 1)
            kmem = S[1][0:CH, 0:2 * P].rearrange("p (c n) -> p c n", c=2)[:, :, 0:MS]
            res = R1[:, 0, 0:2 * MSP].rearrange("p (c n) -> p c n", c=2)[:, :, 0:MS]
            v.tensor_tensor(res, kmem, splm[:, 0, :, 0:MS], ALU.subtract).then_inc(s["pd"], 1)
            ve.wait_ge(s["pa"], 3)
            v.tensor_tensor(splm[:, 2, :, 0:MS], res, splm[:, 1, :, 0:MS], ALU.subtract).then_inc(s["pd"], 1)
            w1, w2 = X[:, 0:FC, :], HG[0:CH, 0:2, :]
            v.tensor_reduce(wsum[:, 0:1], w1, AX.XY, ALU.add, apply_absolute_value=True)
            v.tensor_reduce(wsum[0:CH, 1:2], w2, AX.XY, ALU.add, apply_absolute_value=True).then_inc(s["pd"], 1)
            ve.wait_ge(s["pp"], 5)
            link(v.tensor_scalar(wsinv[:], PV[:, 0:2], 1.0 / (D * F), 1e-5, ALU.mult, ALU.max))
            link(v.reciprocal(wscale[:], wsinv[:]))
            for w, q, n, c in ((w1, XQ[:, 0:FC, :], P, 0), (w2, HQT[0:CH, :, :], CH, 1)):
                link(v.tensor_scalar(w, w, wscale[0:n, c:c + 1], MAGIC, ALU.mult, ALU.add))
                link(v.tensor_scalar(w, w, MAGIC, -1.0, ALU.subtract, ALU.max))
                v.tensor_scalar(q, w, 1.0, None, ALU.min).then_inc(s["pd"], 1)
            ve.wait_ge(s["pp"], 6)
            v.memset(XT[CH:CH + 1, 1, :], 1.0).then_inc(s["pa"], 1)
            at["base"] = k[0]
            k[0] = 0

            def stats(b, n, src):
                for t in range(T):
                    ins = v.bn_stats(st[:, t, :], src[:, t, :])
                link(ins)
                v.memset(rec[:, 0:1], 0.0)
                for t in range(T):
                    ins = v.bn_aggr(mv[:, t, :], st[:, t, :])
                ins.then_inc(s["stats"], 1)
                ve.wait_ge(s["rstd"], b * 5 + n + 1)

            def normalise(job, src, scale):
                for t in range(T):
                    ins = v.tensor_scalar(X[:, t, :], src[:, t, :], mv[:, t, 0:1], scale[:, t:t + 1], ALU.subtract, ALU.mult)
                    if t % 4 == 3:
                        ins.then_inc(s["xnorm"], 1)

            def cut(b, group, pieces, width):
                def low(i):
                    dst, m, j = pieces[i - group]
                    ve.wait_ge(s["mid"], b * 14 + i + 1)
                    v.tensor_tensor(dst[:, 2, m, j * width:(j + 1) * width], R1[:, i % 2, 0:width], dst[:, 1, m, j * width:(j + 1) * width],
                                    ALU.subtract).then_inc(s["lo"], 1)
                for i in range(group, group + len(pieces)):
                    dst, m, j = pieces[i - group]
                    ve.wait_ge(s["hi"], b * 14 + i + 2)
                    if i >= 2:
                        ve.wait_ge(s["lo"], b * 14 + i - 1)
                    v.tensor_tensor(R1[:, i % 2, 0:width], ring4[i % 4][0:CH, 0:width], dst[:, 0, m, j * width:(j + 1) * width],
                                    ALU.subtract).then_inc(s["resid"], 1)
                    if i > group:
                        low(i - 1)
                low(group + len(pieces) - 1)

            def vcut(b, use):
                def heads(x):
                    return x.rearrange("p (t h d) -> p t h d", t=2, h=H)

                def low(i):
                    ve.wait_ge(s["vmid"], b * 8 + 4 * use + i + 1)
                    v.tensor_tensor(V[:, 2 * i:2 * i + 2, :, 2 * DH:3 * DH], heads(RV[:, i % 2, :]), V[:, 2 * i:2 * i + 2, :, DH:2 * DH],
                                    ALU.subtract).then_inc(s["vcopied"], 1)
                for i in range(4):
                    ve.wait_ge(s["vhi"], b * 8 + 4 * use + i + 1)
                    if i >= 2:
                        ve.wait_ge(s["vcopied"], b * 8 + 4 * use + i - 1)
                    v.tensor_tensor(heads(RV[:, i % 2, :]), heads(O[i % 2][:, 0:2 * D]), V[:, 2 * i:2 * i + 2, :, 0:DH], ALU.subtract).then_inc(s["vres"], 1)
                    if i:
                        low(i - 1)
                low(3)

            with ve.Fori(0, NB) as b:
                at["b"] = b
                ve.wait_ge(s["gathered"], b * 128 + 128)
                stats(b, 0, G)
                normalise(0, G, rn)
                for c in range(2):
                    ve.wait_ge(s["inproj_out"], b * 8 + 2 * c + 2)
                    if c == 0:
                        link(v.memset(XC[:, :, 0:2], 0.0))
                    link(v.tensor_scalar(Y1[:, c, :], XC[:, c, 2:L + 2], convw[:, c, 2:3], cols[:, c, 0:1], ALU.mult, ALU.add))
                    link(v.scalar_tensor_tensor(out=Y1[:, c, :], in0=XC[:, c, 1:L + 1], scalar=convw[:, c, 1:2], in1=Y1[:, c, :], op0=ALU.mult, op1=ALU.add))
                    v.scalar_tensor_tensor(out=Y1[:, c, :], in0=XC[:, c, 0:L], scalar=convw[:, c, 0:1], in1=Y1[:, c, :], op0=ALU.mult, op1=ALU.add).then_inc(s["conv"], 1)
                for c in range(2):
                    ve.wait_ge(s["silu"], b * 2 + c + 1)
                    v.tensor_scalar(Y1[:, c, :], XS[:, c, :], cols[:, c, 1:2], None, ALU.mult)
                    link(v.tensor_tensor_scan(CUM[:, c, :], XS[:, c, :], XS[:, c, :], 0.0, ALU.add, ALU.bypass))
                    link(v.scalar_tensor_tensor(out=CUM[:, c, :], in0=CUM[:, c, :], scalar=cols[:, c, 6:7], in1=Y1[:, c, :], op0=ALU.mult, op1=ALU.add))
                    if c == 0:
                        ve.wait_ge(s["inproj_out"], b * 8 + 8)
                    v.tensor_tensor(CUM[:, c, :], CUM[:, c, :], Z[:, c, :], ALU.mult).then_inc(s["gated"], 1)
                ve.wait_ge(s["stored"], b * 16 + 16)
                for i in range(4):
                    ve.wait_ge(s["outproj"], b * 4 + i + 1)
                    v.tensor_tensor(HS[:, 2 * i:2 * i + 2, :], O[i % 2][:, 0:2 * D].rearrange("p (t d) -> p t d", t=2), G[:, 2 * i:2 * i + 2, :], ALU.add).then_inc(s["h1"], 1)
                ve.wait_ge(s["h1"], b * 4 + 4)
                stats(b, 1, HS)
                normalise(1, HS, rnn)
                for t in range(T):
                    v.tensor_scalar(U[:, t, :], HS[:, t, :], mv[:, t, 0:1], rn[:, t:t + 1], ALU.subtract, ALU.mult)
                ve.wait_ge(s["expz"], b + 1)
                link(v.tensor_scalar(sc1[:], sc1[:], 1.0, None, ALU.add))
                v.reciprocal(sc[:], sc1[:]).then_inc(s["score"], 1)
                ve.wait_ge(s["score"], b + 1)
                cut(b, 0, PIECES_K0, HALF)
                ve.wait_ge(s["srow_copied"], b + 1)
                for t in range(T):
                    v.tensor_scalar(junk[:, 0:L - t * P], srow[:, t * P:L], sc[:, t:t + 1], 0.0, ALU.is_lt, ALU.add, accum_out=cnt[:, 0, t:t + 1])
                    if t > 0:
                        v.tensor_scalar(junk[:, L - t * P:L], srow[:, 0:t * P], sc[:, t:t + 1], 0.0, ALU.is_le, ALU.add, accum_out=cnt[:, 1, t:t + 1])
                    link(v.scalar_tensor_tensor(out=junk2[:], in0=srow[:, t * P:(t + 1) * P], scalar=sc[:, t:t + 1], in1=earlier[:], op0=ALU.is_equal, op1=ALU.mult,
                                                accum_out=cnt[:, 2, t:t + 1]))
                link(v.tensor_tensor(rank[:], cnt[:, 0, :], cnt[:, 1, :], ALU.add))
                v.tensor_tensor(rank[:], rank[:], cnt[:, 2, :], ALU.add).then_inc(s["picks"], 1)
                ve.wait_ge(s["picks"], b * 2 + 1)
                v.tensor_scalar(notsel[:], rank[:], float(NSEL), None, ALU.is_ge)
                for t in range(T):
                    ins = v.tensor_scalar(PSEL[:, t, :], slot[:].rearrange("p a n -> p (a n)"), rank[:, t:t + 1], None, ALU.is_equal)
                ins.then_inc(s["picks"], 1)
                ve.wait_ge(s["rank_turned"], b + 1)
                for q in range(2):
                    ins = v.tensor_scalar(PT[0:QC, q, :], ST[0][0:QC, :], rowslot[0:QC, q:q + 1], None, ALU.is_equal)
                ins.then_inc(s["pt"], 1)
                ve.wait_ge(s["pooled"], b + 1)
                link(v.tensor_scalar(pool3[:, 0:1], ST[1][0:CH, 2:3], 1e-6, None, ALU.add))
                link(v.reciprocal(pool3[:, 1:2], pool3[:, 0:1]))
                link(v.tensor_scalar(pool3[:, 2:5], ST[1][0:CH, 0:3], pool3[:, 1:2], None, ALU.mult))
                link(v.tensor_tensor(pool3[:, 5:7], pool3[:, 2:4], cols[:, :, 2], ALU.mult))
                for c in range(2):
                    link(v.scalar_tensor_tensor(out=pool3[:, 5 + c:6 + c], in0=cols[:, c, 3:4], scalar=pool3[:, 4:5], in1=pool3[:, 5 + c:6 + c], op0=ALU.mult, op1=ALU.add))
                cut(b, 4, PIECES_Q0, 2 * QP)
                ve.wait_ge(s["lo"], b * 14 + 6)
                vcut(b, 0)
                for c in range(2):
                    v.scalar_tensor_tensor(out=XT[0:CH, c, :], in0=srow[0:CH, :], scalar=pool3[:, 5 + c:6 + c], in1=XT[0:CH, c, :], op0=ALU.mult, op1=ALU.add).then_inc(s["mixin"], 1)

                def chain(h, n, rows, tiles, kinds):
                    if n > 0:
                        ve.wait_ge(s["rowmax"], b * 24 + n)
                    link(v.tensor_reduce(nm[0:rows, 0:tiles, 0:1], nmp[0:rows, 0:tiles, :], AX.X, ALU.max, negate=True))
                    link(v.tensor_copy(nms[0:rows, h % 2, 0:tiles, 0:kinds, 0], nm[0:rows, 0:tiles, 0:kinds]))
                    v.tensor_tensor(nms[0:rows, h % 2, 0:tiles, 0:kinds, 1], nm[0:rows, 0:tiles, 0:kinds], nms[0:rows, h % 2, 0:tiles, 0:kinds, 0],
                                    ALU.subtract).then_inc(s["rowmax"], 1)

                for h in range(H):
                    for u in range(4):
                        n = 4 * h + u
                        ve.wait_ge(s["units"], b * NUNITS + n + 1)
                        v.tensor_reduce(nmp[0:QP, u // 2, u % 2:u % 2 + 1], S[n % 2][0:QP, :], AX.X, ALU.max).then_inc(s["reduced"], 1)
                    ve.wait_ge(s["reduced"], b * NUNITS + 4 * h + 6)
                    if h >= 2:
                        ve.wait_ge(s["mturned"], b * 24 + h - 1)
                    chain(h, h, QP, 2, 1)
                ve.wait_ge(s["ctxr"], b + 1)
                for n0, n1 in ((0, 8), (8, 12)):
                    src = ST[n0 // 8][0:QP, 0:(n1 - n0) * P].rearrange("p (n d) -> p n d", d=VP)
                    link(v.reciprocal(rec0[:, 2 * n0:2 * n1], src[:, :, VONE]))
                    link(v.tensor_reduce(sum0[:, 2 * n0:2 * n1, :], src[:, :, 0:3 * DH].rearrange("p n (a d) -> p n d a", a=3), AX.X, ALU.add))
                for n in range(12):
                    g, j, q = n // 6, n // 2 % 3, n % 2
                    dst = CX[:, q, :].rearrange("p (g a j d) -> p g a j d", g=2, a=2, j=3)[:, g, :, j, :]
                    ins = v.tensor_tensor(dst, sum0[:, 2 * n:2 * n + 2, :], rec0[:, 2 * n:2 * n + 2].unsqueeze(2).to_broadcast([QP, 2, DH]), ALU.mult)
                ins.then_inc(s["ctxn"], 1)
                for t in range(T):
                    ve.wait_ge(s["mixed"], b * 8 + t + 1)
                    o = O[t % 2]
                    link(v.scalar_tensor_tensor(out=HP[:, t, :], in0=o[:, 0:D], scalar=notsel[:, t:t + 1], in1=U[:, t, :], op0=ALU.mult, op1=ALU.add))
                    v.tensor_tensor(HP[:, t, :], HP[:, t, :], o[:, D:2 * D], ALU.add).then_inc(s["merged"], 1)
                ve.wait_ge(s["merged"], b * 8 + 8)
                stats(b, 2, HP)
                normalise(2, HP, rn)
                link(v.tensor_tensor(HS[:], HS[:], HP[:], ALU.add))
                for i in range(4):
                    ve.wait_ge(s["ffn"], b * 4 + i + 1)
                    v.tensor_tensor(HS[:, 2 * i:2 * i + 2, :], O[i % 2][:, 0:2 * D].rearrange("p (t d) -> p t d", t=2), HS[:, 2 * i:2 * i + 2, :], ALU.add).then_inc(s["h2"], 1)
                ve.wait_ge(s["h2"], b * 4 + 4)
                stats(b, 3, HS)
                normalise(3, HS, rn)
                cut(b, 6, PIECES_1, HALF)
                ve.wait_ge(s["lo"], b * 14 + 14)
                vcut(b, 1)

                def unit(what):
                    n = UNIT_AT[what]
                    kind, h, u = what
                    ve.wait_ge(s["units"], b * NUNITS + n + 1)
                    if kind == "ctx":
                        if h or u:
                            last = UNIT_AT["ctx", h - 1 + u, 1 - u]
                            ve.wait_ge(s["reduced"], b * NUNITS + last + 3)
                        src = S[n % 2][:, :].rearrange("p (t d) -> p t d", t=4)
                        inv = rec[:, 0:8].rearrange("p (t a) -> p t a", t=4)
                        link(v.reciprocal(inv, src[:, :, VONE:VP + DH + 1:VP + DH - VONE]))
                        link(v.tensor_reduce(vsum, src[:, :, 0:3 * DH].rearrange("p t (a d) -> p t d a", a=3), AX.X, ALU.add))
                        v.tensor_tensor(U[:, 4 * u:4 * u + 4, h * DH:(h + 1) * DH], vsum, inv[:, :, 0:1].to_broadcast([P, 4, DH]), ALU.mult)
                        v.tensor_tensor(HP[:, 4 * u:4 * u + 4, h * DH:(h + 1) * DH], src[:, :, VP:VP + DH], inv[:, :, 1:2].to_broadcast([P, 4, DH]), ALU.mult).then_inc(s["reduced"], 1)
                    elif u < 16:
                        v.tensor_reduce(nmp[:, u // 2, u % 2:u % 2 + 1], S[n % 2][:, :], AX.X, ALU.max).then_inc(s["reduced"], 1)
                    else:
                        j = 4 * (u - 16)
                        if j == 0:
                            ve.wait_ge(s["rowmax"], b * 24 + H + h)
                        v.tensor_reduce(nm[:, j:j + 4, 1], S[n % 2][:, 0:4 * MSP].rearrange("p (t n) -> p t n", t=4)[:, :, 0:MS], AX.X, ALU.max,
                                        negate=True).then_inc(s["reduced"], 1)
                    if kind == "max" and u == SCORE_UNITS - 1:
                        ve.wait_ge(s["reduced"], b * NUNITS + n + 3)
                        ve.wait_ge(s["mturned"], b * 24 + 12 + max(h - 1, 0))
                        chain(h, H + h, P, T, 2)

                def low(i):
                    ve.wait_ge(s["exps"], b * NSTEP + i + 3)
                    v.tensor_tensor(EL[:, i % RING, :], E[:, cut_of(i)[0] % 2, :], EH[:, i % RING, :], ALU.subtract).then_inc(s["vlow"], 1)

                def mcopy(h):
                    ve.wait_ge(s["mturned"], b * 24 + 12 + h + 1)
                    v.tensor_copy(QS[KP:KP + 4, h, :], MT[KP:KP + 4, :]).then_inc(s["mcopied"], 1)

                for what in FIRST_UNITS:
                    unit(what)
                mcopy(0)
                for i in range(NSTEP + 2):
                    if i < NSTEP:
                        for what in STEP_UNITS[i]:
                            unit(what)
                    if i % 10 == MAX_AT and i < NSTEP - 10:
                        mcopy(i // 10 + 1)
                    if i % STEPS == 0 and i:
                        low(i - 2)
                unit(LAST_UNITS[0])
                ve.wait_ge(s["reduced"], b * NUNITS + NUNITS + 2)
                for i in range(4):
                    ve.wait_ge(s["alphae"], b * 4 + i + 1)
                    e = e2[:, i % 2, :, :]
                    a, a1, x = U[:, 2 * i:2 * i + 2, :], HP[:, 2 * i:2 * i + 2, :], X[:, 2 * i:2 * i + 2, :]
                    v.tensor_scalar(e, e, 1.0, None, ALU.add)
                    link(v.tensor_tensor(a, a, a1, ALU.subtract))
                    link(v.reciprocal(e, e))
                    link(v.tensor_tensor(a, a, e, ALU.mult))
                    v.tensor_tensor(x, a, a1, ALU.add).then_inc(s["fusedx"], 1)
                for i in range(4):
                    ve.wait_ge(s["fproj"], b * 4 + i + 1)
                    v.tensor_tensor(HS[:, 2 * i:2 * i + 2, :], O[i % 2][:, 0:2 * D].rearrange("p (t d) -> p t d", t=2), HS[:, 2 * i:2 * i + 2, :], ALU.add).then_inc(s["h3"], 1)
                ve.wait_ge(s["h3"], b * 4 + 4)
                stats(b, 4, HS)
                for t in range(T):
                    ins = v.tensor_scalar(X[:, t, :], HS[:, t, :], mv[:, t, 0:1], rnn[:, t:t + 1], ALU.subtract, ALU.mult)
                link(ins)
                link(v.tensor_tensor(X[:], X[:], g1bc[:].unsqueeze(1).to_broadcast([P, T, D]), ALU.mult))
                link(v.tensor_reduce(amax[:], X[:], AX.X, ALU.max, apply_absolute_value=True))
                link(v.tensor_scalar(qinv[:], amax[:], 1e-5, 1.0 / 127.0, ALU.max, ALU.mult))
                v.tensor_scalar(gsc[:], qinv[:], wsinv[:, 0:1], None, ALU.mult)
                link(v.reciprocal(qsc[:], qinv[:]))
                for t in range(T):
                    link(v.tensor_scalar(X[:, t, :], X[:, t, :], qsc[:, t:t + 1], MAGIC, ALU.mult, ALU.add))
                    v.tensor_scalar(XQ[:, t, :], X[:, t, :], MAGIC, None, ALU.subtract).then_inc(s["quant"], 1)
                for t in range(T):
                    ve.wait_ge(s["hss"], b * 8 + t + 1)
                    link(v.tensor_tensor(HG[:, t, :], HG[:, t, :], g2bc[:], ALU.mult))
                    link(v.tensor_reduce(amax[:, t:t + 1], HG[:, t, :], AX.X, ALU.max, apply_absolute_value=True))
                ve.wait_ge(s["hrms"], b + 1)
                link(v.tensor_tensor(amax[:], amax[:], rn[:], ALU.mult))
                link(v.tensor_scalar(qinv[:], amax[:], 1e-5, 1.0 / 127.0, ALU.max, ALU.mult))
                link(v.reciprocal(qsc[:], qinv[:]))
                link(v.tensor_tensor(qsc[:], qsc[:], rn[:], ALU.mult))
                link(v.tensor_scalar(gsc[:], qinv[:], wsinv[:, 1:2], None, ALU.mult))

                def store(i):
                    ve.wait_ge(s["bout"], b * 8 + 2 * i + 2)
                    for t in (2 * i, 2 * i + 1):
                        ins = v.scalar_tensor_tensor(out=HS[:, t, :], in0=O[i % 2][:, (t % 2) * D:(t % 2 + 1) * D], scalar=gsc[:, t:t + 1], in1=HS[:, t, :],
                                                     op0=ALU.mult, op1=ALU.add)
                    ins.then_inc(s["outs"], 1)

                for t in range(T):
                    link(v.tensor_scalar(HG[:, t, :], HG[:, t, :], qsc[:, t:t + 1], MAGIC, ALU.mult, ALU.add))
                    if t >= 2:
                        ve.wait_ge(s["hturned"], b * 8 + t - 1)
                    v.tensor_scalar(HQ[:, (t % 2) * F:(t % 2 + 1) * F], HG[:, t, :], MAGIC, None, ALU.subtract).then_inc(s["hquant"], 1)
                    if t % 2 == 1 and t >= 3:
                        store(t // 2 - 1)
                store(3)
            assert k[0] == VEC_LINKS, k[0]


_INS = ['x', 'L0_tok_embed_matrix', 'L0_attn_W_in', 'L0_attn_conv_w', 'L0_attn_conv_b', 'L0_attn_B', 'L0_attn_C', 'L0_attn_D',
        'L0_attn_W_out', 'L0_ffn_g1', 'L0_ffn_b1', 'L0_ffn_g2', 'L0_ffn_b2', 'L0_ffn_Wr', 'L0_ffn_br', 'L0_ffn_Wq', 'L0_ffn_bq',
        'L0_ffn_Wk', 'L0_ffn_bk', 'L0_ffn_Wv', 'L0_ffn_bv', 'L0_ffn_Wo', 'L0_ffn_bo', 'L0_ffn_Wm', 'L0_ffn_bm', 'L0_ffn_W1',
        'L0_ffn_bf1', 'L0_ffn_W2', 'L0_ffn_bf2', 'L1_attn_w_attn', 'L1_attn_b_attn', 'L1_attn_w_proj', 'L1_attn_b_proj',
        'L1_attn_w_mem', 'L1_attn_b_mem', 'L1_attn_w_alpha', 'L1_attn_b_alpha', 'L1_attn_memory_features', 'L1_ffn_w1',
        'L1_ffn_g1', 'L1_ffn_w2', 'L1_ffn_g2']


def kernel(**inputs):
    import numpy as _np
    import concourse.bacc as _bacc
    from concourse import mybir as _mybir
    from concourse.bass_utils import run_bass_kernel_spmd as _run

    nc = _bacc.Bacc("TRN2", target_bir_lowering=False, num_devices=1)
    arrays, aps = {}, {}
    for name in _INS:
        a = _np.ascontiguousarray(inputs[name])
        arrays[f"in_{name}_dram"] = a
        aps[name] = nc.dram_tensor(f"in_{name}_dram", a.shape, _mybir.dt.from_np(a.dtype), kind="ExternalInput").ap()
    out = nc.dram_tensor("out_0_dram", (NB, L, D), _mybir.dt.float32, kind="ExternalOutput").ap()
    build(nc, aps, out)
    r = _run(nc, [arrays], core_ids=[0])
    return r.results[0]["out_0_dram"]
```
